# Optimizing a Trainium2 kernel written in Bass

```python
import numpy as np
import jax
import jax.numpy as jnp

def _softmax(x, axis=-1):
    return jax.nn.softmax(x, axis=axis)

def _gelu(x):
    return jax.nn.gelu(x, approximate=True)

def _silu(x):
    return jax.nn.silu(x)

def _sigmoid(x):
    return jax.nn.sigmoid(x)

def _layernorm(x, axis=-1, eps=1e-05):
    m = jnp.mean(x, axis=axis, keepdims=True)
    v = jnp.var(x, axis=axis, keepdims=True)
    return (x - m) / jnp.sqrt(v + eps)

def _scatter_add(tgt, idx, src, axis=0):
    return tgt.at[idx].add(src)

def _segment_sum(src, seg, n):
    return jax.ops.segment_sum(src, seg, n)
kernel_name = 'mk_gnn_ffn_d1_gnn_r8_021755'

def setup_inputs(seed: int=0):
    np.random.seed(seed)
    _w = jnp.asarray

    def _rec_inputs():
        import jax
        import jax.numpy as jnp
        _gk = jax.random.key(seed)
        x = -6.415e-05 + 1 * jax.random.normal(jax.random.fold_in(_gk, 1), (5000, 256), jnp.float32)
        _s = jax.random.randint(jax.random.fold_in(_gk, 2), (40000,), 0, 5000, jnp.int32)
        _d = jax.random.randint(jax.random.fold_in(_gk, 3), (40000,), 0, 5000, jnp.int32)
        _loop = jnp.arange(5000, dtype=jnp.int32)
        src = jnp.concatenate([_s, _d, _loop])
        dst = jnp.concatenate([_d, _s, _loop])
        _o = jnp.argsort(dst, stable=True)
        src = src[_o]
        dst = dst[_o]
        edge_type_9 = jax.random.randint(jax.random.fold_in(_gk, 12), (85000,), 0, 9, jnp.int32)
        return (x, src, dst, edge_type_9)
    x, src, dst, edge_type_9 = _rec_inputs()

    def _L0_gnn_setup():
        import jax, jax.numpy as jnp
        import numpy as np
        N, E, D, H, R = (5000, 40000, 256, 8, 9)
        B = 40

        def graph_norm(x, w, b, ms):
            xr = x.reshape(B, N // B, D)
            mean = xr.mean(axis=1, keepdims=True)
            sub = xr - mean * ms
            std = jnp.sqrt((sub ** 2).mean(axis=1, keepdims=True) + 1e-06)
            return (w * sub / std + b).reshape(N, D)

        def rel_graph_conv(h, src, dst, etype, bases, comb, bias):
            W = jnp.einsum('rb,bio->rio', comb, bases)
            hW = jnp.einsum('nd,rde->rne', h, W)
            msg = hW[etype, src]
            out = jax.ops.segment_sum(msg, dst, num_segments=N) + bias
            return jax.nn.relu(out)
        key = jax.random.key(seed)
        ks = jax.random.split(key, 16)
        s = 0.05
        inp = {'h': jax.random.normal(ks[0], (N, D), jnp.float32), 'src': jax.random.randint(ks[1], (E,), 0, N, jnp.int32), 'dst': jax.random.randint(ks[2], (E,), 0, N, jnp.int32), 'etype': jax.random.randint(ks[3], (E,), 0, R, jnp.int32), 'q_bases': jax.random.normal(ks[4], (R, D, D), jnp.float32) * s, 'q_comb': jax.random.normal(ks[5], (R, R), jnp.float32), 'q_bias': jnp.zeros((D,), jnp.float32), 'k_bases': jax.random.normal(ks[6], (R, D, D), jnp.float32) * s, 'k_comb': jax.random.normal(ks[7], (R, R), jnp.float32), 'k_bias': jnp.zeros((D,), jnp.float32), 'v_bases': jax.random.normal(ks[8], (R, D, D), jnp.float32) * s, 'v_comb': jax.random.normal(ks[9], (R, R), jnp.float32), 'v_bias': jnp.zeros((D,), jnp.float32), 'gn1_w': jnp.ones((D,), jnp.float32), 'gn1_b': jnp.zeros((D,), jnp.float32), 'gn1_ms': jnp.ones((D,), jnp.float32), 'gn2_w': jnp.ones((D,), jnp.float32), 'gn2_b': jnp.zeros((D,), jnp.float32), 'gn2_ms': jnp.ones((D,), jnp.float32), 'O_w': jax.random.normal(ks[10], (D, D), jnp.float32) * s, 'O_b': jnp.zeros((D,), jnp.float32), 'ffn1_w': jax.random.normal(ks[11], (D, 2 * D), jnp.float32) * s, 'ffn1_b': jnp.zeros((2 * D,), jnp.float32), 'ffn2_w': jax.random.normal(ks[12], (2 * D, D), jnp.float32) * s, 'ffn2_b': jnp.zeros((D,), jnp.float32)}
        return inp
    _L0_gnn_all = _L0_gnn_setup()
    _L0_gnn_in = {k: v for k, v in _L0_gnn_all.items() if k in ('q_bases', 'q_comb', 'q_bias', 'k_bases', 'k_comb', 'k_bias', 'v_bases', 'v_comb', 'v_bias', 'gn1_w', 'gn1_b', 'gn1_ms', 'gn2_w', 'gn2_b', 'gn2_ms', 'O_w', 'O_b', 'ffn1_w', 'ffn1_b', 'ffn2_w', 'ffn2_b')}
    del _L0_gnn_all

    def _L0_ffn_setup():
        import jax, jax.numpy as jnp
        import numpy as np
        BN_EPS = 0.001

        def _bn(h, g, b, m, v):
            return g * (h - m) * jax.lax.rsqrt(v + BN_EPS) + b
        key = jax.random.key(seed)
        ks = jax.random.split(key, 8)
        B, F, Df = (256, 64, 256)
        E, H, D = (8, 256, 256)
        s1 = 1.0 / np.sqrt(Df)
        s2 = 1.0 / np.sqrt(H)
        return {'x': jax.random.normal(ks[0], (B, F, Df), jnp.float32), 'Wr': jax.random.normal(ks[1], (Df, E), jnp.float32) * s1, 'br': jnp.zeros((E,), jnp.float32), 'W1': jax.random.normal(ks[2], (E, Df, H), jnp.float32) * s1, 'b1': jnp.zeros((E, H), jnp.float32), 'g1': jnp.ones((E, H), jnp.float32), 'be1': jnp.zeros((E, H), jnp.float32), 'm1': jnp.zeros((E, H), jnp.float32), 'v1': jnp.ones((E, H), jnp.float32), 'W2': jax.random.normal(ks[3], (E, H, H), jnp.float32) * s2, 'b2': jnp.zeros((E, H), jnp.float32), 'g2': jnp.ones((E, H), jnp.float32), 'be2': jnp.zeros((E, H), jnp.float32), 'm2': jnp.zeros((E, H), jnp.float32), 'v2': jnp.ones((E, H), jnp.float32), 'Wo': jax.random.normal(ks[4], (E, H, D), jnp.float32) * s2, 'bo': jnp.zeros((E, D), jnp.float32)}
    _L0_ffn_all = _L0_ffn_setup()
    _L0_ffn_in = {k: v for k, v in _L0_ffn_all.items() if k in ('Wr', 'br', 'W1', 'b1', 'g1', 'be1', 'm1', 'v1', 'W2', 'b2', 'g2', 'be2', 'm2', 'v2', 'Wo', 'bo')}
    del _L0_ffn_all
    return {'x': x, 'src': src, 'dst': dst, 'edge_type_9': edge_type_9, 'L0_gnn_q_bases': _L0_gnn_in['q_bases'], 'L0_gnn_q_comb': _L0_gnn_in['q_comb'], 'L0_gnn_q_bias': _L0_gnn_in['q_bias'], 'L0_gnn_k_bases': _L0_gnn_in['k_bases'], 'L0_gnn_k_comb': _L0_gnn_in['k_comb'], 'L0_gnn_k_bias': _L0_gnn_in['k_bias'], 'L0_gnn_v_bases': _L0_gnn_in['v_bases'], 'L0_gnn_v_comb': _L0_gnn_in['v_comb'], 'L0_gnn_v_bias': _L0_gnn_in['v_bias'], 'L0_gnn_gn1_w': _L0_gnn_in['gn1_w'], 'L0_gnn_gn1_b': _L0_gnn_in['gn1_b'], 'L0_gnn_gn1_ms': _L0_gnn_in['gn1_ms'], 'L0_gnn_gn2_w': _L0_gnn_in['gn2_w'], 'L0_gnn_gn2_b': _L0_gnn_in['gn2_b'], 'L0_gnn_gn2_ms': _L0_gnn_in['gn2_ms'], 'L0_gnn_O_w': _L0_gnn_in['O_w'], 'L0_gnn_O_b': _L0_gnn_in['O_b'], 'L0_gnn_ffn1_w': _L0_gnn_in['ffn1_w'], 'L0_gnn_ffn1_b': _L0_gnn_in['ffn1_b'], 'L0_gnn_ffn2_w': _L0_gnn_in['ffn2_w'], 'L0_gnn_ffn2_b': _L0_gnn_in['ffn2_b'], 'L0_ffn_Wr': _L0_ffn_in['Wr'], 'L0_ffn_br': _L0_ffn_in['br'], 'L0_ffn_W1': _L0_ffn_in['W1'], 'L0_ffn_b1': _L0_ffn_in['b1'], 'L0_ffn_g1': _L0_ffn_in['g1'], 'L0_ffn_be1': _L0_ffn_in['be1'], 'L0_ffn_m1': _L0_ffn_in['m1'], 'L0_ffn_v1': _L0_ffn_in['v1'], 'L0_ffn_W2': _L0_ffn_in['W2'], 'L0_ffn_b2': _L0_ffn_in['b2'], 'L0_ffn_g2': _L0_ffn_in['g2'], 'L0_ffn_be2': _L0_ffn_in['be2'], 'L0_ffn_m2': _L0_ffn_in['m2'], 'L0_ffn_v2': _L0_ffn_in['v2'], 'L0_ffn_Wo': _L0_ffn_in['Wo'], 'L0_ffn_bo': _L0_ffn_in['bo']}

def reference(x, src, dst, edge_type_9, L0_gnn_q_bases, L0_gnn_q_comb, L0_gnn_q_bias, L0_gnn_k_bases, L0_gnn_k_comb, L0_gnn_k_bias, L0_gnn_v_bases, L0_gnn_v_comb, L0_gnn_v_bias, L0_gnn_gn1_w, L0_gnn_gn1_b, L0_gnn_gn1_ms, L0_gnn_gn2_w, L0_gnn_gn2_b, L0_gnn_gn2_ms, L0_gnn_O_w, L0_gnn_O_b, L0_gnn_ffn1_w, L0_gnn_ffn1_b, L0_gnn_ffn2_w, L0_gnn_ffn2_b, L0_ffn_Wr, L0_ffn_br, L0_ffn_W1, L0_ffn_b1, L0_ffn_g1, L0_ffn_be1, L0_ffn_m1, L0_ffn_v1, L0_ffn_W2, L0_ffn_b2, L0_ffn_g2, L0_ffn_be2, L0_ffn_m2, L0_ffn_v2, L0_ffn_Wo, L0_ffn_bo):
    import jax
    import jax.numpy as jnp

    def _L0_gnn_ref(h, src, dst, etype, q_bases, q_comb, q_bias, k_bases, k_comb, k_bias, v_bases, v_comb, v_bias, gn1_w, gn1_b, gn1_ms, gn2_w, gn2_b, gn2_ms, O_w, O_b, ffn1_w, ffn1_b, ffn2_w, ffn2_b):
        import jax, jax.numpy as jnp
        import numpy as np
        N, E, D, H, R = (5000, 40000, 256, 8, 9)
        B = 40

        def graph_norm(x, w, b, ms):
            xr = x.reshape(B, N // B, D)
            mean = xr.mean(axis=1, keepdims=True)
            sub = xr - mean * ms
            std = jnp.sqrt((sub ** 2).mean(axis=1, keepdims=True) + 1e-06)
            return (w * sub / std + b).reshape(N, D)

        def rel_graph_conv(h, src, dst, etype, bases, comb, bias):
            W = jnp.einsum('rb,bio->rio', comb, bases)
            hW = jnp.einsum('nd,rde->rne', h, W)
            msg = hW[etype, src]
            out = jax.ops.segment_sum(msg, dst, num_segments=N) + bias
            return jax.nn.relu(out)
        dh = D // H
        hn = graph_norm(h, gn1_w, gn1_b, gn1_ms)
        Q = rel_graph_conv(hn, src, dst, etype, q_bases, q_comb, q_bias).reshape(N, H, dh)
        K = rel_graph_conv(hn, src, dst, etype, k_bases, k_comb, k_bias).reshape(N, H, dh)
        V = rel_graph_conv(hn, src, dst, etype, v_bases, v_comb, v_bias).reshape(N, H, dh)
        score = jnp.sum(K[src] * Q[dst], axis=-1, keepdims=True)
        score = jnp.exp(jnp.clip(score / np.sqrt(dh).astype(np.float32), -10.0, 10.0))
        wV = jax.ops.segment_sum(score * V[src], dst, num_segments=N)
        z = jax.ops.segment_sum(score, dst, num_segments=N)
        attn = (wV / (z + 1e-06)).reshape(N, D)
        h1 = attn @ O_w + O_b
        h2 = graph_norm(h1, gn2_w, gn2_b, gn2_ms)
        out = jax.nn.relu(h2 @ ffn1_w + ffn1_b) @ ffn2_w + ffn2_b
        return out

    def _L0_ffn_ref(x, Wr, br, W1, b1, g1, be1, m1, v1, W2, b2, g2, be2, m2, v2, Wo, bo):
        import jax, jax.numpy as jnp
        import numpy as np
        BN_EPS = 0.001

        def _bn(h, g, b, m, v):
            return g * (h - m) * jax.lax.rsqrt(v + BN_EPS) + b
        feat = jnp.mean(x, axis=0)
        w = jax.nn.softmax(feat @ Wr + br, axis=-1)
        h = jnp.einsum('bfd,edh->bfeh', x, W1) + b1
        h = jax.nn.relu(_bn(h, g1, be1, m1, v1))
        h = jnp.einsum('bfeh,ehk->bfek', h, W2) + b2
        h = jax.nn.relu(_bn(h, g2, be2, m2, v2))
        y = jnp.einsum('bfeh,ehd->bfed', h, Wo) + bo
        return jnp.einsum('bfed,fe->bfd', y, w)
    x = x + _L0_gnn_ref(_layernorm(x, axis=-1), src, dst, edge_type_9, L0_gnn_q_bases, L0_gnn_q_comb, L0_gnn_q_bias, L0_gnn_k_bases, L0_gnn_k_comb, L0_gnn_k_bias, L0_gnn_v_bases, L0_gnn_v_comb, L0_gnn_v_bias, L0_gnn_gn1_w, L0_gnn_gn1_b, L0_gnn_gn1_ms, L0_gnn_gn2_w, L0_gnn_gn2_b, L0_gnn_gn2_ms, L0_gnn_O_w, L0_gnn_O_b, L0_gnn_ffn1_w, L0_gnn_ffn1_b, L0_gnn_ffn2_w, L0_gnn_ffn2_b)
    x = x + _L0_ffn_ref(_layernorm(x, axis=-1)[None], L0_ffn_Wr, L0_ffn_br, L0_ffn_W1, L0_ffn_b1, L0_ffn_g1, L0_ffn_be1, L0_ffn_m1, L0_ffn_v1, L0_ffn_W2, L0_ffn_b2, L0_ffn_g2, L0_ffn_be2, L0_ffn_m2, L0_ffn_v2, L0_ffn_Wo, L0_ffn_bo)[0]
    return x

_drawn_inputs = setup_inputs


def setup_inputs(seed=0):
    import zlib

    import numpy as np

    out = dict(_drawn_inputs(seed))
    spreads = {'L0_gnn_q_bias': (0.0, 0.8),
     'L0_gnn_k_bias': (0.0, 0.8),
     'L0_gnn_v_bias': (0.0, 0.8),
     'L0_gnn_gn1_w': (1.0, 0.2),
     'L0_gnn_gn1_b': (0.0, 0.1),
     'L0_gnn_gn1_ms': (1.0, 0.6),
     'L0_gnn_gn2_w': (1.0, 0.2),
     'L0_gnn_gn2_b': (0.0, 0.1),
     'L0_gnn_gn2_ms': (1.0, 0.2),
     'L0_gnn_O_b': (0.0, 0.8),
     'L0_gnn_ffn1_b': (0.0, 0.1),
     'L0_gnn_ffn2_b': (0.0, 0.1),
     'L0_ffn_br': (0.0, 0.1),
     'L0_ffn_b1': (0.0, 0.378),
     'L0_ffn_g1': (1.0, 0.2),
     'L0_ffn_be1': (0.0, 0.38),
     'L0_ffn_m1': (0.0, 0.357),
     'L0_ffn_v1': (1.0, 0.6),
     'L0_ffn_b2': (0.0, 0.1),
     'L0_ffn_g2': (1.0, 0.2),
     'L0_ffn_be2': (0.0, 0.276),
     'L0_ffn_m2': (0.0, 0.273),
     'L0_ffn_v2': (1.0, 0.6),
     'L0_ffn_bo': (0.0, 0.1)}
    factors = {}
    for name, (base, spread) in spreads.items():
        noise = np.random.default_rng([zlib.crc32(name.encode()), seed]).standard_normal(out[name].shape)
        drawn = base * np.exp(spread * noise) if base else spread * noise
        out[name] = jnp.asarray(drawn.astype(out[name].dtype))
    for name, factor in factors.items():
        out[name] = (out[name] * factor).astype(out[name].dtype)
    return out
```

```python
from contextlib import ExitStack

import concourse.bass as bass
import concourse.mybir as mybir

F32, F16, I32 = mybir.dt.float32, mybir.dt.float16, mybir.dt.int32
ALU = mybir.AluOpType
ACT = mybir.ActivationFunctionType
X = mybir.AxisListType.X

N, D, R = 5000, 256, 9
ED = 85000
GN = 125
NG = N // GN
BN = 25
NB = N // BN
BPG = GN // BN
TPB = 4
WIN = TPB * 128
NT = NB * TPB
ETL = -(-ED // 128)
NCH = -(-ETL // TPB)
EP = 128 * 700
FAR = 1 << 20
NBIN = BN * R
GBIN = GN * R
H, DH = 8, 32
NX = 8
DST, SRC, TYP = 0, 1, 2
FF = 2 * D
TG = 4
TT = TG * GN
NS = N // TT
KC = D // 128

SA = 16.0
SW = 64.0
DESC = 1.0 / (SA * SW)
SQRT_DH = float(DH) ** 0.5


class Psum:

    def __init__(self, ctx, nc):
        self.all = ctx.enter_context(nc.psum_tensor("banks", [128, 8, 512], F32))
        self.b = [self.all[:, i, :] for i in range(8)]


def row(ap, p):
    return ap.rearrange("(a n) -> a n", a=1).broadcast_to([p, ap.shape[0]])


def build(nc, a, out):
    ctx = ExitStack()
    with ctx:
        psum = Psum(ctx, nc)
        ps = psum.b

        def keep(name, shape, dt):
            return ctx.enter_context(nc.sbuf_tensor(name, shape, dt))

        t = dict(
            psum=psum.all,
            tab=nc.dram_tensor("hn_table", [N, 2 * D], F16, kind="Internal").ap(),
            kv=nc.dram_tensor("kv_table", [N, 2 * D], F32, kind="Internal").ap(),
            win=nc.dram_tensor("edge_windows", [3, NT * 128], I32, kind="Internal").ap(),
            attn=nc.dram_tensor("attention_rows", [N, D], F32, kind="Internal").ap(),
            sdr=nc.dram_tensor("window_starts", [NB], I32, kind="Internal").ap(),
            wdr=nc.dram_tensor("relation_weights", [R, D, 3 * D], F32, kind="Internal").ap(),
            ident=keep("ident", [128, 128], F32),
            ident16=keep("ident16", [128, 128], F16),
            flag=keep("flag", [1, 1], I32),
            src=keep("src_cols", [128, NT + TG * BPG * TPB], I32),
            key=keep("key_cols", [128, NT + 2 * TPB], F32),
            loc=keep("loc_cols", [128, NT + 2 * TPB], F32),
            iota=keep("iota", [128, GBIN], F16),
            q=keep("q_rows", [GN, NG, 2, D], F16),
        )
        prepare_edges(nc, ps, a, t)
        relation_weights(nc, ps, a, t)
        normalise(nc, ps, a, t)
        with nc.If(nc.values_load(t["flag"][:], min_val=0, max_val=128) == 0):
            conv_fast(nc, ps, a, t)
            attend(nc, ps, a, t, out)
        with nc.Else():
            list_columns(nc, ps, a, t)
            conv_general(nc, ps, a, t)
            attend_edges_general(nc, ps, a, t)
            attend(nc, ps, a, t, out, general=True)


def prepare_edges(nc, ps, a, t):
    HB = NB // 2
    GRP = 8
    TPG = NT // GRP
    edges = a["edges"]
    with ExitStack() as c:
        sb = lambda n, s, d: c.enter_context(nc.sbuf_tensor(n, s, d))
        sem = lambda n: c.enter_context(nc.semaphore(n))
        first = sb("first", [1, ETL], I32)
        firstf = sb("firstf", [1, ETL], F32)
        firstb = sb("firstb", [128, ETL], F32)
        junk = sb("junk", [128, 4, ETL], F32)
        junk2 = sb("junk2", [128, 4, 128], F32)
        boundi = sb("boundi", [HB, 4], I32)
        bound = sb("bound", [HB, 4], F32)
        cnt = sb("cnt", [HB, 4], F32)
        rowi = sb("rowi", [HB, 4], I32)
        rowf = sb("rowf", [HB, 4], F32)
        rows = sb("rows", [HB, 4, 128], I32)
        rowsf = sb("rowsf", [HB, 4, 128], F32)
        cnt2 = sb("cnt2", [HB, 4], F32)
        start = sb("start", [HB, 4], F32)
        starti = sb("starti", [HB, 2], I32)
        over = sb("over", [128, 4], F32)
        bad = sb("bad", [128, 1], F32)
        bads = sb("bads", [1, 1], F32)
        ones = sb("ones_col", [128, 1], F32)
        srow = sb("srow", [1, NB], I32)
        dl = sb("dl", [GN, 2, ED // GN], I32)
        dlf = sb("dlf", [GN, 2, ED // GN], F32)
        tl = sb("tl", [TPG, GRP, 3, 128], I32)
        tf = sb("tf", [TPG, GRP, 3, 128], F32)
        far = sb("far", [TPG, GRP, 128], F32)
        blk = sb("blk", [TPG, 4], I32)
        blkf = sb("blkf", [TPG, 4], F32)
        off = sb("off", [TPG, 2], F32)
        ioti = sb("ioti", [128, GBIN], I32)
        loads, pool, dve, pe, act, rload, sload, wsem, tload = (sem(n) for n in (
            "list_loaded", "pool_done", "dve_done", "pe_done", "act_done", "rows_loaded",
            "starts_moved", "windows_moved", "tiles_loaded"))
        with nc.Block() as block:
            dst = edges[DST, :]

            @block.sync
            def _(sp):
                sp.dma_start(first[:], dst[0:ETL * 128].rearrange("(a t e) -> a t e", a=1, e=128)[:, :, 0],
                             allow_slow_non_contiguous=True).then_inc(loads, 16)
                for k in range(2):
                    sp.dma_start(dl[:, k, :], dst[k:k + ED].rearrange("(p e) -> p e", p=GN)).then_inc(loads, 16)
                sp.wait_ge(dve, 7)
                for k in range(2):
                    sp.dma_start(t["sdr"][k * HB:(k + 1) * HB].rearrange("(p o) -> p o", o=1),
                                 starti[:, k:k + 1]).then_inc(sload, 16)
                sp.wait_ge(sload, 32)
                sp.dma_start(srow[:], t["sdr"].rearrange("(o p) -> o p", o=1)).then_inc(sload, 16)
                sp.wait_ge(sload, 48)
                with sp.Fori(0, NB) as j:
                    s = sp.value_load(srow[0:1, bass.ds(j, 1)], min_val=0, max_val=ED)
                    sp.dma_start(t["win"][:, bass.ds(j * WIN, WIN)], edges[:, bass.ds(s, WIN)]).then_inc(wsem, 16)
                sp.wait_ge(wsem, 16 * NB)
                for g in range(GRP):
                    sp.dma_start(tl[:, g], t["win"][:, g * TPG * 128:(g + 1) * TPG * 128]
                                 .rearrange("a (p e) -> p a e", e=128)).then_inc(tload, 16)

            @block.gpsimd
            def _(p):
                p.memset(t["ident"][:], 0.0).then_inc(pool, 1)
                p.iota(ioti[:], [[1, GBIN]], base=0, channel_multiplier=0).then_inc(pool, 1)
                p.iota(boundi[:], [[BN, 2], [BN * HB, 2]], base=0, channel_multiplier=BN).then_inc(pool, 1)
                p.iota(blk[:, 0:1], [[1, 1]], base=0, channel_multiplier=1).then_inc(pool, 1)
                p.iota(blk[:, 1:2], [[1, 1]], base=0, channel_multiplier=205).then_inc(pool, 1)
                p.memset(t["key"][:, NT:], -1.0).then_inc(pool, 1)
                p.memset(t["loc"][:, NT:], -1.0).then_inc(pool, 1)
                p.memset(t["src"][:, NT:], 0)
                p.memset(ones[:], 1.0).then_inc(pool, 1)
                p.memset(bad[:], 0.0).then_inc(pool, 1)
                p.wait_ge(pool, 9)
                p.affine_select(out=t["ident"][:], in_=t["ident"][:], compare_op=ALU.not_equal, fill=1.0,
                                base=0, pattern=[[-1, 128]], channel_multiplier=1).then_inc(pool, 1)
                p.wait_ge(dve, 1)
                p.partition_broadcast(firstb[:], firstf[:]).then_inc(pool, 1)
                p.wait_ge(dve, 4)
                for k in range(4):
                    p.indirect_dma_start(out=rows[:, k, :], out_offset=None,
                                         in_=edges.rearrange("a (t e) -> (a t) e", e=128),
                                         in_offset=bass.IndirectOffsetOnAxis(ap=rowi[:, k:k + 1], axis=0)
                                         ).then_inc(rload, 16)

            @block.vector
            def _(v):
                v.wait_ge(loads, 48)
                v.tensor_copy(firstf[:], first[:]).then_inc(dve, 1)
                v.wait_ge(pool, 11)
                v.tensor_copy(t["iota"][:], ioti[:])
                v.tensor_copy(t["ident16"][:], t["ident"][:])
                v.tensor_copy(bound[:], boundi[:]).then_inc(dve, 1)
                v.wait_ge(dve, 2)
                for k in range(4):
                    i = v.tensor_scalar(junk[0:HB, k, :], firstb[0:HB, :], bound[:, k:k + 1], 0.0,
                                        ALU.is_lt, ALU.add, accum_out=cnt[:, k:k + 1])
                i.then_inc(dve, 1)
                v.wait_ge(dve, 3)
                v.tensor_scalar(rowf[:], cnt[:], -1.0, 0.0, ALU.add, ALU.max)
                v.tensor_scalar(rowi[:], cnt[:], -1.0, 0.0, ALU.add, ALU.max).then_inc(dve, 1)
                v.wait_ge(rload, 64)
                v.tensor_copy(rowsf[:], rows[:]).then_inc(dve, 1)
                v.wait_ge(dve, 5)
                for k in range(4):
                    i = v.tensor_scalar(junk2[0:HB, k, :], rowsf[:, k, :], bound[:, k:k + 1], 0.0,
                                        ALU.is_lt, ALU.add, accum_out=cnt2[:, k:k + 1])
                i.then_inc(dve, 1)
                v.wait_ge(dve, 6)
                v.scalar_tensor_tensor(start[:], rowf[:], 128.0, cnt2[:], ALU.mult, ALU.add)
                v.scalar_tensor_tensor(starti[:], rowf[:, 0:2], 128.0, cnt2[:, 0:2], ALU.mult, ALU.add).then_inc(dve, 1)
                v.wait_ge(dve, 7)
                v.scalar_tensor_tensor(over[0:HB, 0:2], start[:, 2:4], float(-WIN), start[:, 0:2], ALU.add, ALU.subtract)
                v.tensor_copy(dlf[:], dl[:]).then_inc(dve, 1)
                v.wait_ge(dve, 8)
                v.tensor_scalar(over[0:HB, 2:4], over[0:HB, 0:2], 0.0, 0.0, ALU.is_gt, ALU.max)
                v.tensor_tensor(dlf[:, 0, :], dlf[:, 0, :], dlf[:, 1, :], ALU.is_gt).then_inc(dve, 1)
                v.wait_ge(dve, 9)
                v.reduce_max(bad[0:GN, :], dlf[:, 0, :], X).then_inc(dve, 1)
                v.wait_ge(dve, 10)
                v.tensor_tensor(bad[0:HB, :], bad[0:HB, :], over[0:HB, 2:3], ALU.max).then_inc(dve, 1)
                v.wait_ge(dve, 11)
                v.tensor_tensor(bad[0:HB, :], bad[0:HB, :], over[0:HB, 3:4], ALU.max).then_inc(dve, 1)
                v.wait_ge(pe, 1)
                v.tensor_copy(t["flag"][:], ps[0][0:1, 0:1]).then_inc(dve, 1)
                v.tensor_single_scalar(blk[:, 2:3], blk[:, 0:1], 2, ALU.arith_shift_right)
                v.tensor_single_scalar(blk[:, 3:4], blk[:, 1:2], 12, ALU.arith_shift_right).then_inc(dve, 1)
                v.wait_ge(dve, 14)
                v.tensor_copy(blkf[:], blk[:]).then_inc(dve, 1)
                v.wait_ge(dve, 15)
                v.tensor_single_scalar(off[:, 0:1], blkf[:, 2:3], float(-BN), ALU.mult)
                v.tensor_single_scalar(off[:, 1:2], blkf[:, 3:4], float(-GN), ALU.mult).then_inc(dve, 1)
                v.wait_ge(dve, 16)
                v.scalar_tensor_tensor(off[:, 1:2], blkf[:, 2:3], float(BN), off[:, 1:2], ALU.mult, ALU.add).then_inc(dve, 1)
                v.wait_ge(tload, 16 * GRP)
                v.tensor_copy(tf[:], tl[:]).then_inc(dve, 1)
                v.wait_ge(dve, 18)
                for g in range(GRP):
                    i = v.tensor_scalar(tf[:, g, DST, :], tf[:, g, DST, :], off[:, 0:1], float(-BN * (TPG // TPB) * g), ALU.add, ALU.add)
                i.then_inc(dve, 1)
                v.wait_ge(dve, 19)
                v.scalar_tensor_tensor(tf[:, :, TYP, :], tf[:, :, DST, :], float(R), tf[:, :, TYP, :], ALU.mult, ALU.add)
                v.tensor_scalar(far[:], tf[:, :, DST, :], float(BN), float(FAR), ALU.is_ge, ALU.mult).then_inc(dve, 1)
                v.wait_ge(dve, 20)
                v.scalar_tensor_tensor(tf[:, :, DST, :], tf[:, :, DST, :], off[:, 1:2], far[:], ALU.add, ALU.add).then_inc(dve, 1)
                for g in range(GRP):
                    v.wait_ge(pe, 2 + g)
                    bank = ps[1 + g % 2]
                    cols = slice(g * TPG, (g + 1) * TPG)
                    v.tensor_copy(t["src"][:, cols], bank[:, 128:128 + TPG])
                    v.tensor_copy(t["loc"][:, cols], bank[:, 0:TPG])
                    v.tensor_copy(t["key"][:, cols], bank[:, 256:256 + TPG]).then_inc(dve, 1)

            @block.tensor
            def _(e):
                e.wait_ge(pool, 10)
                e.wait_ge(dve, 12)
                e.matmul(ps[0][0:1, 0:1], bad[:], ones[:], start=True, stop=True).then_inc(pe, 1)
                e.wait_ge(dve, 21)
                for g in range(GRP):
                    if g >= 2:
                        e.wait_ge(dve, 20 + g)
                    for k in range(3):
                        m = e.transpose(ps[1 + g % 2][:, 128 * k:128 * k + TPG], tf[:, g, k, :],
                                        t["ident"][0:TPG, 0:TPG])
                    m.then_inc(pe, 1)


def relation_weights(nc, ps, a, t):
    S = 8
    NCK = D // S
    KB = R * S
    with ExitStack() as c:
        sb = lambda n, s, d: c.enter_context(nc.sbuf_tensor(n, s, d))
        sem = lambda n: c.enter_context(nc.semaphore(n))
        bases = [sb(f"bases{e}", [KB, NCK, D], F32) for e in range(3)]
        comb = sb("comb", [KB, 3, R], F32)
        same = sb("same", [KB, R, S], F32)
        same8 = sb("same8", [KB, S], F32)
        kron = sb("kron", [KB, 3, R, S], F32)
        res = sb("res", [KB, 2, 4, 512], F32)
        lb = [sem(f"bases_loaded{e}") for e in range(3)]
        lc, pool, dve, pe, done, st0, st1 = (sem(n) for n in (
            "comb_loaded", "pool_done", "kron_ready", "product_ready", "copied", "stored_even", "stored_odd"))
        st = [st0, st1]
        names = ("q", "k", "v")
        with nc.Block() as block:
            @block.sync
            def _(sp):
                for e, n in enumerate(names):
                    for b in range(R):
                        sp.dma_start(bases[e][b * S:(b + 1) * S],
                                     a[f"{n}_bases"][b].rearrange("(c i) o -> i c o", i=S)).then_inc(lb[e], 16)
                for k in range(12):
                    e, cc = k // 4, k % 4
                    sp.wait_ge(done, 4 * (k + 1))
                    for r in range(R):
                        sp.dma_start(t["wdr"][r, cc * 64:(cc + 1) * 64, e * D:(e + 1) * D].rearrange("(c i) o -> i c o", i=S),
                                     res[r * S:(r + 1) * S, k % 2].rearrange("p a (c o) -> p (a c) o", c=2)
                                     ).then_inc(st[k % 2], 16)
                sp.wait_ge(st0, 16 * R * 6)
                sp.wait_ge(st1, 16 * R * 6)

            @block.gpsimd
            def _(p):
                p.memset(same[:], 0.0).then_inc(pool, 1)
                p.wait_ge(pool, 1)
                p.affine_select(out=same[:], in_=same[:], compare_op=ALU.not_equal, fill=1.0, base=0,
                                pattern=[[-S, R], [-1, S]], channel_multiplier=1).then_inc(pool, 1)

            @block.scalar
            def _(s):
                for e, n in enumerate(names):
                    for b in range(R):
                        s.dma_start(comb[b * S:(b + 1) * S, e, :],
                                    a[f"{n}_comb"].rearrange("r b -> b r")[b:b + 1, :].broadcast_to([S, R]),
                                    allow_slow_non_contiguous=True).then_inc(lc, 16)
                for m in range(48):
                    s.wait_ge(pe, m + 1)
                    if m % 4 == 0 and m >= 8:
                        s.wait_ge(st[(m // 4) % 2], 16 * R * ((m // 4) // 2))
                    s.activation(res[:, (m // 4) % 2, m % 4, :], ps[m % 8][0:KB, :], ACT.Copy).then_inc(done, 1)

            @block.vector
            def _(v):
                v.wait_ge(pool, 2)
                v.reduce_sum(same8[:], same[:].rearrange("p b i -> p i b"), X).then_inc(dve, 1)
                v.wait_ge(dve, 1)
                v.wait_ge(lc, 16 * 3 * R)
                for e in range(3):
                    v.tensor_tensor(kron[:, e], comb[:, e, :].unsqueeze(2).broadcast_to([KB, R, S]),
                                    same8[:].unsqueeze(1).broadcast_to([KB, R, S]), ALU.mult).then_inc(dve, 1)

            @block.tensor
            def _(q):
                q.wait_ge(dve, 4)
                for m in range(48):
                    e, cc = m // 16, m % 16
                    if cc == 0:
                        q.wait_ge(lb[e], 16 * R)
                    if m >= 8:
                        q.wait_ge(done, m - 7)
                    q.matmul(ps[m % 8][0:KB, :], kron[:, e].rearrange("p r i -> p (r i)"),
                             bases[e][:, 2 * cc:2 * cc + 2, :].rearrange("p c o -> p (c o)"),
                             start=True, stop=True).then_inc(pe, 1)


def normalise(nc, ps, a, t):
    PG = 8
    NBT = NG // PG
    with ExitStack() as c:
        sb = lambda n, s, d: c.enter_context(nc.sbuf_tensor(n, s, d))
        sem = lambda n: c.enter_context(nc.semaphore(n))
        x = sb("x_in", [GN, 2, PG, D], F32)
        mv = sb("mv", [GN, PG, 2], F32)
        st6 = sb("st6", [GN, PG, 6], F32)
        rstd = sb("rstd", [GN, PG, 1], F32)
        rinv = sb("rinv", [GN, PG, 1], F32)
        y = sb("y", [GN, PG, D], F32)
        u = sb("u", [GN, PG, D], F32)
        sub = sb("sub", [GN, PG, D], F32)
        sq = sb("sq", [GN, PG, D], F32)
        std = sb("std", [GN, PG, D], F32)
        hl = sb("hl", [GN, 2, PG, 2, D], F16)
        par = sb("gn1_par", [GN, 3, D], F32)
        mean1 = sb("mean_mat", [GN, GN], F32)
        eps = sb("eps", [GN, 2], F32)
        lx0, lx1, lp, pool, dve, act, pe, st0, st1 = (sem(n) for n in (
            "x_even", "x_odd", "params", "pool_done", "dve_done", "act_done", "pe_done", "stored_e", "stored_o"))
        lx, st = [lx0, lx1], [st0, st1]
        NDV, NAC, NPE = 11, 4, 2
        xg = a["x"].rearrange("(b g p) d -> b p g d", p=GN, g=PG)
        tg = t["tab"].rearrange("(b g p) d -> b p g d", p=GN, g=PG)
        bc = lambda k: par[:, k:k + 1, :].broadcast_to([GN, PG, D])
        with nc.Block() as block:
            @block.sync
            def _(sp):
                for k, n in enumerate(("gn1_ms", "gn1_w", "gn1_b")):
                    sp.dma_start(par[:, k, :], row(a[n], GN)).then_inc(lp, 16)
                sp.dma_start(x[:, 0], xg[0]).then_inc(lx0, 16)
                for b in range(NBT):
                    if b + 1 < NBT:
                        if b >= 1:
                            sp.wait_ge(dve, NDV * (b - 1) + 4)
                        sp.dma_start(x[:, (b + 1) % 2], xg[b + 1]).then_inc(lx[(b + 1) % 2], 16)
                    sp.wait_ge(dve, NDV * (b + 1))
                    sp.dma_start(tg[b], hl[:, b % 2].rearrange("p g l d -> p g (l d)")).then_inc(st[b % 2], 16)
                sp.wait_ge(st0, 16 * 3)
                sp.wait_ge(st1, 16 * 2)

            @block.gpsimd
            def _(p):
                p.memset(mean1[:], 1.0 / GN).then_inc(pool, 1)
                p.memset(eps[:, 0:1], 1e-5).then_inc(pool, 1)
                p.memset(eps[:, 1:2], 1e-6).then_inc(pool, 1)

            @block.vector
            def _(v):
                v.wait_ge(lp, 48)
                for b in range(NBT):
                    o = NDV * b
                    v.wait_ge(lx[b % 2], 16 * (b // 2 + 1))
                    for g in range(PG):
                        i = v.bn_stats(st6[:, g, :], x[:, b % 2, g, :])
                    i.then_inc(dve, 1)
                    v.wait_ge(dve, o + 1)
                    for g in range(PG):
                        i = v.bn_aggr(mv[:, g, :], st6[:, g, :])
                    i.then_inc(dve, 1)
                    v.wait_ge(act, NAC * b + 1)
                    v.reciprocal(rinv[:], rstd[:]).then_inc(dve, 1)
                    v.wait_ge(dve, o + 3)
                    for g in range(PG):
                        i = v.tensor_scalar(y[:, g, :], x[:, b % 2, g, :], mv[:, g, 0:1], rinv[:, g, :],
                                            ALU.subtract, ALU.mult)
                    i.then_inc(dve, 1)
                    for k in range(4):
                        v.wait_ge(pe, NPE * 4 * b + k + 1)
                        i = v.tensor_tensor(u[:, 2 * k:2 * k + 2, :],
                                            ps[k][0:GN, :].rearrange("p (g d) -> p g d", g=2),
                                            par[:, 0:1, :].broadcast_to([GN, 2, D]), ALU.mult)
                    i.then_inc(dve, 1)
                    v.wait_ge(dve, o + 5)
                    v.tensor_tensor(sub[:], y[:], u[:], ALU.subtract).then_inc(dve, 1)
                    v.wait_ge(act, NAC * b + 3)
                    v.reciprocal(u[:], std[:]).then_inc(dve, 1)
                    v.wait_ge(dve, o + 7)
                    v.tensor_tensor(u[:], u[:], bc(1), ALU.mult).then_inc(dve, 1)
                    v.wait_ge(dve, o + 8)
                    v.tensor_tensor(u[:], u[:], sub[:], ALU.mult).then_inc(dve, 1)
                    v.wait_ge(dve, o + 9)
                    v.tensor_tensor(u[:], u[:], bc(2), ALU.add).then_inc(dve, 1)
                    v.wait_ge(act, NAC * b + 4)
                    v.scalar_tensor_tensor(hl[:, b % 2, :, 1, :], u[:], SA, hl[:, b % 2, :, 0, :],
                                           ALU.mult, ALU.subtract).then_inc(dve, 1)

            @block.scalar
            def _(s):
                s.wait_ge(pool, 3)
                for b in range(NBT):
                    o = NDV * b
                    s.wait_ge(dve, o + 2)
                    s.activation(rstd[:], mv[:, :, 1:2], ACT.Sqrt, bias=eps[:, 0:1]).then_inc(act, 1)
                    s.wait_ge(dve, o + 6)
                    s.activation(sq[:], sub[:], ACT.Square).then_inc(act, 1)
                    for k in range(4):
                        s.wait_ge(pe, NPE * 4 * b + 4 + k + 1)
                        i = s.activation(std[:, 2 * k:2 * k + 2, :], ps[4 + k][0:GN, :].rearrange("p (g d) -> p g d", g=2),
                                         ACT.Sqrt, bias=eps[:, 1:2])
                    i.then_inc(act, 1)
                    s.wait_ge(dve, o + 10)
                    if b >= 2:
                        s.wait_ge(st[b % 2], 16 * (b // 2))
                    s.activation(hl[:, b % 2, :, 0, :], u[:], ACT.Copy, scale=SA).then_inc(act, 1)

            @block.tensor
            def _(e):
                e.wait_ge(pool, 3)
                for b in range(NBT):
                    e.wait_ge(dve, NDV * b + 4)
                    for k in range(4):
                        e.matmul(ps[k][0:GN, :], mean1[:], y[:, 2 * k:2 * k + 2, :].rearrange("p g d -> p (g d)"),
                                 start=True, stop=True).then_inc(pe, 1)
                    e.wait_ge(act, NAC * b + 2)
                    for k in range(4):
                        e.matmul(ps[4 + k][0:GN, :], mean1[:], sq[:, 2 * k:2 * k + 2, :].rearrange("p g d -> p (g d)"),
                                 start=True, stop=True).then_inc(pe, 1)


def conv_fast(nc, ps, a, t):
    STEP = 2
    BB = STEP * BPG
    W3 = 3 * D
    HC = W3 // 2
    with ExitStack() as c:
        sb = lambda n, s, d: c.enter_context(nc.sbuf_tensor(n, s, d))
        sem = lambda n: c.enter_context(nc.semaphore(n))
        w = sb("w_parts", [128, R, KC, 2, W3], F16)
        wst = sb("w_stage", [128, 2, KC, W3], F32)
        bias = sb("qkv_bias", [GN, W3], F32)
        rows = [sb(f"rows{k}", [128, TPB, 2 * D], F16) for k in range(BPG)]
        stage = [sb(f"src_stage{k}", [128, BPG * TPB], I32) for k in range(2)]
        hot = [sb(f"hot{k}", [128, TPB, NBIN], F16) for k in range(2)]
        agg = [sb(f"agg{k}", [128, 2, KC, R, GN], F16) for k in range(2)]
        qkv = [sb(f"qkv{k}", [GN, W3], F32) for k in range(2)]
        kvo = [sb(f"kvo{k}", [GN, 2 * D], F32) for k in range(2)]

        lw = [sem(f"w_loaded{k}") for k in range(2)]
        lb, whi, wlo = (sem(n) for n in ("bias_loaded", "w_high", "w_low"))
        gathered = [sem(f"gathered{k}") for k in range(BPG)]
        stored, kvo_free = sem("kv_stored"), sem("kv_rows_free")
        staged, hot_ready, sum_ready, hi_done, lo_done, conv_ready, biased, q_high, kv_ready = (sem(n) for n in (
            "staged", "hot_ready", "sum_ready", "sums_high", "sums_low", "conv_ready", "biased", "q_high", "kv_ready"))
        C_SUM, C_RING = BPG, 2
        ticks = sem("ticks")
        sums = [ps[0], ps[1]]
        cps = [(ps[2], ps[3]), (ps[4], ps[5])]

        with nc.Block() as block:
            @block.sync
            def _(sp):
                sp.sem_inc(kvo_free, C_RING)
                for k, n in enumerate(("q", "k", "v")):
                    sp.dma_start(bias[:, k * D:(k + 1) * D], row(a[f"{n}_bias"], GN)).then_inc(lb, 16)
                for r in range(R):
                    if r >= 2:
                        sp.wait_ge(wlo, r - 1)
                    sp.dma_start(wst[:, r % 2], t["wdr"][r].rearrange("(k p) o -> p k o", p=128)).then_inc(lw[r % 2], 16)
                with sp.Fori(0, NG // STEP) as i:
                    for g in range(STEP):
                        sp.wait_ge(kv_ready, STEP * i + g + 1 + C_RING)
                        sp.dma_start(t["kv"][bass.ds((STEP * i + g) * GN, GN), :], kvo[g][:]).then_inc(stored, 16)
                        sp.wait_ge(stored, 16 * (STEP * i + g + 1))
                        sp.sem_inc(kvo_free)

            @block.gpsimd
            def _(p):
                def gather(i, b):
                    q = b // BPG
                    if b % BPG == 0:
                        p.wait_ge(staged, STEP * i + q + 1)
                    p.wait_ge(sum_ready, BB * i + b + 1)
                    p.sem_inc(ticks)
                    for k in range(TPB):
                        p.indirect_dma_start(
                            out=rows[b % BPG][:, k, :], out_offset=None, in_=t["tab"],
                            in_offset=bass.IndirectOffsetOnAxis(
                                ap=stage[q % 2][:, (b % BPG) * TPB + k:(b % BPG) * TPB + k + 1], axis=0)
                        ).then_inc(gathered[b % BPG], 16)

                gather(0, 0)
                with p.Fori(0, NG // STEP) as i:
                    for b in range(1, BB + 1):
                        gather(i, b)

            @block.scalar
            def _(s):
                def put_stage(i, h):
                    s.activation(stage[h][:], t["src"][:, bass.ds((STEP * i + h) * BPG * TPB, BPG * TPB)],
                                 ACT.Copy).then_inc(staged, 1)

                def high(i, b):
                    q = b // BPG
                    s.wait_ge(sum_ready, BB * i + b + 1 + C_SUM)
                    if b % BPG == 0:
                        s.wait_ge(conv_ready, STEP * i + q + 1)
                    s.activation(block_of(agg[q % 2], 0, b % BPG), block_sums(sums[b % 2]), ACT.Copy).then_inc(hi_done, 1)

                s.sem_inc(kv_ready, C_RING)
                for h in range(STEP):
                    put_stage(0, h)
                for r in range(R):
                    s.wait_ge(lw[r % 2], 16 * (r // 2 + 1))
                    s.activation(w[:, r, :, 0, :], wst[:, r % 2], ACT.Copy, scale=SW).then_inc(whi, 1)
                high(0, 0)
                with s.Fori(0, NG // STEP) as i:
                    for g in range(STEP):
                        for b in range(g * BPG + 1, (g + 1) * BPG + 1):
                            high(i, b)
                            if b % BPG == BPG - 1:
                                put_stage(i + 1, g)
                        s.wait_ge(biased, STEP * i + g + 1 + C_RING)
                        s.activation(q_part(t, STEP * i + g, 0), qkv[g][:, 0:D], ACT.Relu).then_inc(q_high, 1)
                        s.wait_ge(kvo_free, STEP * i + g + 1)
                        s.activation(kvo[g][:], qkv[g][:, D:W3], ACT.Relu).then_inc(kv_ready, 1)

            @block.vector
            def _(v):
                def make_hot(i, b):
                    v.wait_ge(sum_ready, BB * i + b - 1 + C_SUM)
                    for k in range(TPB):
                        m = v.tensor_scalar(hot[b % 2][:, k, :], t["iota"][:, 0:NBIN],
                                            t["key"][:, bass.ds((BB * i + b) * TPB + k, 1)], None, ALU.is_equal)
                    m.then_inc(hot_ready, 1)

                def low(i, b):
                    q = b // BPG
                    v.wait_ge(hi_done, BB * i + b + 1)
                    v.tensor_tensor(block_of(agg[q % 2], 1, b % BPG), block_sums(sums[b % 2]),
                                    block_of(agg[q % 2], 0, b % BPG), ALU.subtract).then_inc(lo_done, 1)

                v.sem_inc(lo_done, C_RING)
                v.sem_inc(biased, C_RING)
                for r in range(R):
                    v.wait_ge(whi, r + 1)
                    v.scalar_tensor_tensor(w[:, r, :, 1, :], wst[:, r % 2], SW, w[:, r, :, 0, :],
                                           ALU.mult, ALU.subtract).then_inc(wlo, 1)
                v.wait_ge(lb, 48)
                make_hot(0, 0)
                make_hot(0, 1)
                low(0, 0)
                with v.Fori(0, NG // STEP) as i:
                    for g in range(STEP):
                        for b in range(g * BPG + 1, (g + 1) * BPG + 1):
                            make_hot(i, b + 1)
                            low(i, b)
                        v.wait_ge(conv_ready, STEP * i + g + 1 + C_RING)
                        v.wait_ge(kv_ready, STEP * i + g + 1)
                        for h in range(2):
                            m = v.scalar_tensor_tensor(qkv[g][:, h * HC:(h + 1) * HC], cps[g][h][0:GN, 0:HC], DESC,
                                                       bias[:, h * HC:(h + 1) * HC], ALU.mult, ALU.add)
                        m.then_inc(biased, 1)
                        v.wait_ge(q_high, STEP * i + g + 1)
                        v.wait_ge(biased, STEP * i + g + 1 + C_RING)
                        m = v.scalar_tensor_tensor(q_part(t, STEP * i + g, 1), qkv[g][:, 0:D], 0.0,
                                                   q_part(t, STEP * i + g, 0), ALU.max, ALU.subtract)

            @block.tensor
            def _(e):
                def sum_block(i, b):
                    q = b // BPG
                    e.wait_ge(gathered[b % BPG], 16 * TPB * (STEP * i + q + 1))
                    e.wait_ge(hot_ready, BB * i + b + 1)
                    e.wait_ge(lo_done, BB * i + b + 1)
                    for kc in range(KC):
                        for k in range(TPB):
                            for part in range(2):
                                m = e.matmul(sums[b % 2][:, kc * NBIN:(kc + 1) * NBIN],
                                             rows[b % BPG][:, k, part * D + kc * 128:part * D + (kc + 1) * 128],
                                             hot[b % 2][:, k, :], start=(k == 0 and part == 0),
                                             stop=(k == TPB - 1 and part == 1))
                    m.then_inc(sum_ready, 1)

                e.sem_inc(sum_ready, C_SUM)
                e.sem_inc(conv_ready, C_RING)
                e.wait_ge(wlo, R)
                sum_block(0, 0)
                with e.Fori(0, NG // STEP) as i:
                    for g in range(STEP):
                        for b in range(g * BPG + 1, (g + 1) * BPG + 1):
                            sum_block(i, b)
                        e.wait_ge(lo_done, BB * i + (g + 1) * BPG + C_RING)
                        e.wait_ge(biased, STEP * i + g + 1)
                        conv_product(e, agg[g], w, cps[g], HC).then_inc(conv_ready, 1)


def q_part(t, graph, part):
    return t["q"][:, bass.ds(graph, 1), part, :].rearrange("p o d -> p (o d)")


def block_sums(bank):
    return bank[:, 0:KC * NBIN].rearrange("p (c n r) -> p c r n", c=KC, r=R)


def block_of(agg, part, b):
    return agg[:, part, :, :, b * BN:(b + 1) * BN]


def conv_product(e, agg, w, banks, hc):
    for h in range(2):
        n = 0
        for r in range(R):
            for kc in range(KC):
                for pa, pw in ((0, 0), (0, 1), (1, 0)):
                    m = e.matmul(banks[h][0:GN, 0:hc], agg[:, pa, kc, r, :], w[:, r, kc, pw, h * hc:(h + 1) * hc],
                                 start=(n == 0), stop=(n == R * KC * 3 - 1))
                    n += 1
    return m

def list_columns(nc, ps, a, t):
    TPG, GRP = 100, 7
    with ExitStack() as c:
        sb = lambda n, s, d: c.enter_context(nc.sbuf_tensor(n, s, d))
        sem = lambda n: c.enter_context(nc.semaphore(n))
        tl = sb("list_tiles", [TPG, GRP, 3, 128], I32)
        tf = sb("list_tiles_f", [TPG, GRP, 3, 128], F32)
        load, dve, pe = (sem(n) for n in ("list_tiles_loaded", "columns_done", "list_turned"))
        with nc.Block() as block:
            @block.sync
            def _(sp):
                for g in range(GRP):
                    sp.dma_start(tl[:, g], a["edges"][:, g * TPG * 128:(g + 1) * TPG * 128]
                                 .rearrange("a (p e) -> p a e", e=128)).then_inc(load, 16)

            @block.vector
            def _(v):
                v.wait_ge(load, 16 * GRP)
                v.tensor_copy(tf[:], tl[:]).then_inc(dve, 1)
                v.wait_ge(dve, 1)
                v.scalar_tensor_tensor(tf[:, :, TYP, :], tf[:, :, DST, :], float(R), tf[:, :, TYP, :],
                                       ALU.mult, ALU.add).then_inc(dve, 1)
                for g in range(GRP):
                    v.wait_ge(pe, 1 + g)
                    cols = slice(g * TPG, (g + 1) * TPG)
                    v.tensor_copy(t["loc"][:, cols], ps[g % 2][:, 0:TPG])
                    v.tensor_copy(t["src"][:, cols], ps[g % 2][:, 128:128 + TPG])
                    v.tensor_copy(t["key"][:, cols], ps[g % 2][:, 256:256 + TPG]).then_inc(dve, 1)

            @block.tensor
            def _(e):
                for g in range(GRP):
                    e.wait_ge(dve, max(2, g + 1))
                    for k in range(3):
                        m = e.transpose(ps[g % 2][:, 128 * k:128 * k + TPG], tf[:, g, k, :], t["ident"][0:TPG, 0:TPG])
                    m.then_inc(pe, 1)


def conv_general(nc, ps, a, t):
    W3 = 3 * D
    HC = W3 // 2
    C = NCH
    with ExitStack() as c:
        sb = lambda n, s, d: c.enter_context(nc.sbuf_tensor(n, s, d))
        sem = lambda n: c.enter_context(nc.semaphore(n))
        w = sb("g_w_parts", [128, R, KC, 2, W3], F16)
        wst = sb("g_w_stage", [128, 2, KC, W3], F32)
        bias = sb("g_qkv_bias", [GN, W3], F32)
        rows = sb("g_rows", [128, TPB, 2 * D], F16)
        stage = sb("g_stage", [128, TPB], I32)
        hot = sb("g_hot", [128, TPB, GBIN], F16)
        zero = sb("g_zero", [128, 512], F16)
        agg = sb("g_agg", [128, 2, KC, R, GN], F16)
        qkv = sb("g_qkv", [GN, W3], F32)
        kvo = sb("g_kvo", [GN, 2 * D], F32)
        lw = [sem(f"g_w_loaded{k}") for k in range(2)]
        ticks = sem("g_ticks")
        lb, whi, wlo, zeroed, gathered, hot_ready, summed, opened, hi_done, lo_done, conv_ready, biased, act_ready, shifted, stored = (
            sem("g_" + n) for n in ("bias_loaded", "w_high", "w_low", "zeroed", "gathered", "hot_ready", "summed", "opened",
                                    "hi_done", "lo_done", "conv_ready", "biased", "act_ready", "shifted", "stored"))
        kvo_free = sem("g_kvo_free")
        with nc.Block() as block:
            @block.sync
            def _(sp):
                sp.sem_inc(kvo_free)
                for k, n in enumerate(("q", "k", "v")):
                    sp.dma_start(bias[:, k * D:(k + 1) * D], row(a[f"{n}_bias"], GN)).then_inc(lb, 16)
                for r in range(R):
                    if r >= 2:
                        sp.wait_ge(wlo, r - 1)
                    sp.dma_start(wst[:, r % 2], t["wdr"][r].rearrange("(k p) o -> p k o", p=128)).then_inc(lw[r % 2], 16)
                with sp.Fori(0, NG) as g:
                    sp.wait_ge(act_ready, g + 1)
                    sp.dma_start(t["kv"][bass.ds(g * GN, GN), :], kvo[:]).then_inc(stored, 16)
                    sp.wait_ge(stored, 16 * (g + 1))
                    sp.sem_inc(kvo_free)

            @block.gpsimd
            def _(p):
                p.memset(zero[:], 0.0).then_inc(zeroed, 1)
                with p.Fori(0, NG) as g:
                    with p.Fori(0, C) as i:
                        p.wait_ge(hot_ready, g * C + i + 1)
                        p.sem_inc(ticks)
                        for k in range(TPB):
                            p.indirect_dma_start(out=rows[:, k, :], out_offset=None, in_=t["tab"],
                                                 in_offset=bass.IndirectOffsetOnAxis(ap=stage[:, k:k + 1], axis=0)
                                                 ).then_inc(gathered, 16)

            @block.vector
            def _(v):
                v.sem_inc(lo_done)
                v.sem_inc(biased)
                for r in range(R):
                    v.wait_ge(whi, r + 1)
                    v.scalar_tensor_tensor(w[:, r, :, 1, :], wst[:, r % 2], SW, w[:, r, :, 0, :],
                                           ALU.mult, ALU.subtract).then_inc(wlo, 1)
                v.wait_ge(lb, 48)
                with v.Fori(0, NG) as g:
                    with v.Fori(0, C) as i:
                        v.wait_ge(summed, g * C + i + 1)
                        v.tensor_copy(stage[:], t["src"][:, bass.ds(i * TPB, TPB)])
                        for k in range(TPB):
                            m = v.tensor_scalar(hot[:, k, :], t["iota"][:], t["key"][:, bass.ds(i * TPB + k, 1)],
                                                None, ALU.is_equal)
                        m.then_inc(hot_ready, 1)
                    v.wait_ge(hot_ready, g * C + C)
                    v.tensor_scalar(t["key"][:, 0:NCH * TPB], t["key"][:, 0:NCH * TPB], float(-GBIN), None, ALU.add).then_inc(shifted, 1)
                    v.wait_ge(shifted, g + 1)
                    for b in range(BPG):
                        v.wait_ge(hi_done, BPG * g + b + 1)
                        v.tensor_tensor(block_of(agg, 1, b), block_sums(ps[b]), block_of(agg, 0, b), ALU.subtract).then_inc(lo_done, 1)
                    v.wait_ge(conv_ready, g + 2)
                    for h in range(2):
                        m = v.scalar_tensor_tensor(qkv[:, h * HC:(h + 1) * HC], ps[5 + h][0:GN, 0:HC], DESC,
                                                   bias[:, h * HC:(h + 1) * HC], ALU.mult, ALU.add)
                    m.then_inc(biased, 1)
                    v.wait_ge(act_ready, g + 1)
                    v.wait_ge(biased, 2 * g + 2)
                    v.scalar_tensor_tensor(q_part(t, g, 1), qkv[:, 0:D], 0.0, q_part(t, g, 0), ALU.max, ALU.subtract).then_inc(biased, 1)

            @block.scalar
            def _(s):
                for r in range(R):
                    s.wait_ge(lw[r % 2], 16 * (r // 2 + 1))
                    s.activation(w[:, r, :, 0, :], wst[:, r % 2], ACT.Copy, scale=SW).then_inc(whi, 1)
                with s.Fori(0, NG) as g:
                    s.wait_ge(summed, g * C + C + 1)
                    s.wait_ge(conv_ready, g + 1)
                    for b in range(BPG):
                        s.activation(block_of(agg, 0, b), block_sums(ps[b]), ACT.Copy).then_inc(hi_done, 1)
                    s.wait_ge(biased, 2 * g + 2)
                    s.wait_ge(kvo_free, g + 1)
                    s.activation(q_part(t, g, 0), qkv[:, 0:D], ACT.Relu)
                    s.activation(kvo[:], qkv[:, D:W3], ACT.Relu).then_inc(act_ready, 1)

            @block.tensor
            def _(e):
                e.sem_inc(summed)
                e.sem_inc(conv_ready)
                e.wait_ge(wlo, R)
                e.wait_ge(zeroed, 1)
                with e.Fori(0, NG) as g:
                    e.wait_ge(lo_done, BPG * g + 1)
                    for b in range(BPG):
                        e.matmul(ps[b][:, 0:KC * NBIN], zero[:, 0:128], zero[:, 0:KC * NBIN], start=True, stop=False,
                                 skip_group_check=True)
                    with e.Fori(0, C) as i:
                        e.wait_ge(gathered, (g * C + i + 1) * 16 * TPB)
                        e.wait_ge(hot_ready, g * C + i + 1)
                        for b in range(BPG):
                            for kc in range(KC):
                                for k in range(TPB):
                                    for part in range(2):
                                        m = e.matmul(ps[b][:, kc * NBIN:(kc + 1) * NBIN],
                                                     rows[:, k, part * D + kc * 128:part * D + (kc + 1) * 128],
                                                     hot[:, k, b * NBIN:(b + 1) * NBIN], start=False,
                                                     stop=(part == 1 and k == TPB - 1), skip_group_check=True)
                        m.then_inc(summed, 1)
                    e.wait_ge(lo_done, BPG * g + BPG + 1)
                    e.wait_ge(biased, 2 * g + 1)
                    conv_product(e, agg, w, (ps[5], ps[6]), HC).then_inc(conv_ready, 1)


def attend_edges_general(nc, ps, a, t):
    C = NCH
    with ExitStack() as c:
        sb = lambda n, s, d: c.enter_context(nc.sbuf_tensor(n, s, d))
        sem = lambda n: c.enter_context(nc.semaphore(n))
        kv = sb("ge_kv", [128, TPB, 2 * D], F32)
        stage = sb("ge_stage", [128, TPB], I32)
        hot = sb("ge_hot", [128, TPB, GN], F32)
        hotT = sb("ge_hotT", [GN, TPB, 128], F16)
        prod = sb("ge_prod", [128, TPB, D], F32)
        raw = sb("ge_raw", [128, TPB, H], F32)
        clip = sb("ge_clip", [128, TPB, H], F32)
        sv = sb("ge_sv", [128, TPB, D + H], F32)
        zero = sb("ge_zero", [128, D + H], F32)
        zinv = sb("ge_zinv", [GN, 2, H], F32)
        rows = sb("ge_rows", [GN, D], F32)
        ticks = sem("ge_ticks")
        gathered, hot_ready, turned, ht_ready, q_ready, dve, exp_ready, sv_ready, summed, norm, stored, zeroed = (
            sem("ge_" + n) for n in ("gathered", "hot_ready", "turned", "hotT_ready", "q_ready", "scores", "exp_ready",
                                     "weighted", "summed", "normalised", "stored", "zeroed"))
        rows_free = sem("ge_rows_free")
        with nc.Block() as block:
            @block.sync
            def _(sp):
                sp.sem_inc(rows_free)
                with sp.Fori(0, NG) as g:
                    sp.wait_ge(norm, 4 * g + 5)
                    sp.dma_start(t["attn"][bass.ds(g * GN, GN), :], rows[:]).then_inc(stored, 16)
                    sp.wait_ge(stored, 16 * (g + 1))
                    sp.sem_inc(rows_free)

            @block.gpsimd
            def _(p):
                p.memset(zero[:], 0.0).then_inc(zeroed, 1)
                with p.Fori(0, NG) as g:
                    with p.Fori(0, C) as i:
                        p.wait_ge(hot_ready, g * C + i + 1)
                        p.sem_inc(ticks)
                        for k in range(TPB):
                            p.indirect_dma_start(out=kv[:, k, :], out_offset=None, in_=t["kv"],
                                                 in_offset=bass.IndirectOffsetOnAxis(ap=stage[:, k:k + 1], axis=0)
                                                 ).then_inc(gathered, 16)

            @block.vector
            def _(v):
                v.sem_inc(norm)
                with v.Fori(0, NG) as g:
                    with v.Fori(0, C) as i:
                        n = g * C + i
                        v.wait_ge(summed, n + 1)
                        v.tensor_copy(stage[:], t["src"][:, bass.ds(i * TPB, TPB)])
                        for k in range(TPB):
                            m = v.tensor_scalar(hot[:, k, :], t["iota"][:, 0:GN], t["loc"][:, bass.ds(i * TPB + k, 1)],
                                                None, ALU.is_equal)
                        m.then_inc(hot_ready, 1)
                        v.wait_ge(q_ready, n + 1)
                        v.wait_ge(gathered, (n + 1) * 16 * TPB)
                        for k in range(2):
                            m = v.tensor_tensor(prod[:, 2 * k:2 * k + 2, :], ps[1 + k].rearrange("p (k d) -> p k d", k=2),
                                                kv[:, 2 * k:2 * k + 2, 0:D], ALU.mult)
                        m.then_inc(dve, 1)
                        v.wait_ge(dve, 3 * n + 1)
                        v.reduce_sum(raw[:].rearrange("p k h -> p (k h)"),
                                     prod[:].rearrange("p k (h d) -> p (k h) d", h=H), X).then_inc(dve, 1)
                        v.wait_ge(dve, 3 * n + 2)
                        v.tensor_scalar(clip[:], raw[:], -10.0 * SQRT_DH, 10.0 * SQRT_DH, ALU.max, ALU.min).then_inc(dve, 1)
                        v.wait_ge(exp_ready, n + 1)
                        v.tensor_tensor(sv[:, :, 0:D].rearrange("p k (h d) -> p k h d", h=H),
                                        kv[:, :, D:].rearrange("p k (h d) -> p k h d", h=H),
                                        sv[:, :, D:].unsqueeze(3).broadcast_to([128, TPB, H, DH]), ALU.mult).then_inc(sv_ready, 1)
                    v.wait_ge(hot_ready, g * C + C)
                    v.tensor_scalar(t["loc"][:, 0:NCH * TPB], t["loc"][:, 0:NCH * TPB], float(-GN), None, ALU.add).then_inc(norm, 1)
                    v.wait_ge(summed, g * C + C + 1)
                    v.tensor_scalar(zinv[:, 0, :], ps[3][0:GN, D:D + H], 1e-6, None, ALU.add).then_inc(norm, 1)
                    v.wait_ge(norm, 4 * g + 3)
                    v.reciprocal(zinv[:, 1, :], zinv[:, 0, :])
                    v.wait_ge(rows_free, g + 1)
                    v.tensor_copy(rows[:], ps[3][0:GN, 0:D]).then_inc(norm, 1)
                    v.wait_ge(norm, 4 * g + 4)
                    v.tensor_tensor(rows[:].rearrange("p (h d) -> p h d", h=H), rows[:].rearrange("p (h d) -> p h d", h=H),
                                    zinv[:, 1, :].unsqueeze(2).broadcast_to([GN, H, DH]), ALU.mult).then_inc(norm, 1)

            @block.scalar
            def _(s):
                with s.Fori(0, NG) as g:
                    with s.Fori(0, C) as i:
                        n = g * C + i
                        s.wait_ge(turned, n + 1)
                        s.activation(hotT[:], ps[0][0:GN, :].rearrange("p (k e) -> p k e", k=TPB), ACT.Copy).then_inc(ht_ready, 1)
                        s.wait_ge(dve, 3 * n + 3)
                        s.activation(sv[:, :, D:], clip[:], ACT.Exp, scale=1.0 / SQRT_DH).then_inc(exp_ready, 1)

            @block.tensor
            def _(e):
                e.sem_inc(summed)
                e.wait_ge(zeroed, 1)
                with e.Fori(0, NG) as g:
                    e.wait_ge(norm, 4 * g + 1)
                    e.matmul(ps[3][0:GN, 0:D + H], zero[:, 0:GN], zero[:], start=True, stop=False, skip_group_check=True)
                    with e.Fori(0, C) as i:
                        n = g * C + i
                        e.wait_ge(hot_ready, n + 1)
                        for k in range(TPB):
                            m = e.transpose(ps[0][0:GN, k * 128:(k + 1) * 128], hot[:, k, :], t["ident"][:])
                        m.then_inc(turned, 1)
                        e.wait_ge(ht_ready, n + 1)
                        for k in range(TPB):
                            for part in range(2):
                                m = e.matmul(ps[1 + k // 2][:, (k % 2) * D:(k % 2 + 1) * D], hotT[:, k, :],
                                             q_part(t, g, part), start=(part == 0), stop=(part == 1))
                        m.then_inc(q_ready, 1)
                        e.wait_ge(sv_ready, n + 1)
                        for k in range(TPB):
                            m = e.matmul(ps[3][0:GN, 0:D + H], hot[:, k, :], sv[:, k, :], start=False, stop=(k == TPB - 1),
                                         skip_group_check=True)
                        m.then_inc(summed, 1)


class Steps:

    def __init__(self, sem, names):
        self.sem, self.names = sem, names

    def at(self, s, name):
        return s * len(self.names) + self.names.index(name) + 2

    def before(self, s):
        return s * len(self.names) + 1


BS = TG * BPG
RK = 4
WHEN = {"attnT": 3, "o": 4, "up_0": 6, "up_1": 7, "down": 9, "rowsT": 11, "route": 13, "l1_0": 13,
        "l2_0": 15, "l1_1": 16, "l3_0": 17, "l2_1": 18, "l1_2": 19, "l3_1": 20, "mixT": 20, "l2_2": 21,
        "bo": 22, "l1_3": 23, "l3_2": 24, "l2_3": 25, "l1_4": 26, "l3_3": 27, "l2_4": 28, "l1_5": 29,
        "l3_4": 30, "l2_5": 31, "l1_6": 32, "l3_5": 33, "l2_6": 34, "l1_7": 35, "l3_6": 36, "l2_7": 37,
        "l3_7": 38}
PRODUCTS = list(WHEN)
EXPERTS = [x for x in PRODUCTS if x[0] == "l"]
ACT_OF = {"attnT": ["attnT_hi"], "o": ["o_out", "gn_std", "gn_hi"], "up_0": ["up_0", "up_0_hi"],
          "up_1": ["up_1", "up_1_hi"], "down": ["ln_std"], "rowsT": ["rowsT_hi"], "route": ["mix_exp"],
          "mixT": [], "bo": []}
DVE_OF = {"attnT": ["attnT_lo"], "o": ["gn_st", "gn_mv", "gn_a", "gn_b", "gn_c", "gn_d", "gn_e", "gn_f", "gn_g", "gn_h", "gn_out", "gn_lo"],
          "up_0": ["up_0_lo"], "up_1": ["up_1_lo"], "down": ["x_bias", "x1", "ln_st", "ln_mv", "ln_rstd", "ln_out"],
          "rowsT": ["rowsT_lo"], "route": ["logit", "lmax", "lsub", "lsum", "lrec", "mix", "mix_d"],
          "mixT": ["mixT_out"], "bo": ["bo_add"]}
for _x in EXPERTS:
    ACT_OF[_x] = [_x, _x + "_hi"] if _x[:2] != "l3" else []
    DVE_OF[_x] = [_x + "_lo"] if _x[:2] != "l3" else [_x + "_add"]


def prepare_ffn(nc, ps, a, t, k, pre):
    BNS = ("v1", "g1", "be1", "b1", "m1", "v2", "g2", "be2", "b2", "m2")
    SHORT = (("O_b", KC), ("gn2_w", KC), ("gn2_b", KC), ("gn2_ms", KC), ("ffn1_b", FF // 128))
    EK = NX * KC
    with ExitStack() as c:
        sb = lambda n, s, d: c.enter_context(nc.sbuf_tensor(pre + n, s, d))
        sem = lambda n: c.enter_context(nc.semaphore(pre + n))
        stg = sb("weight_stage", [128, 2, 3 * KC * D], F32)
        lines = sb("par_rows", [EK, 15, 128], F32)
        bsd = sb("bn_std", [128, 2, EK], F32)
        btm = sb("bn_tmp", [128, 2, EK], F32)
        pieces = []
        for e in range(NX):
            pieces.append(([a[n][e].rearrange("(k p) o -> p k o", p=128) for n in ("W1", "W2", "Wo")], KC * D,
                           lambda part, e=e: k["we"][:, e, :, :, part, :].rearrange("p l k o -> p (l k) o"), 3 * KC, D))
        for n, w, m, o in (("O_w", "wo", KC, D), ("ffn1_w", "w1", KC, FF), ("ffn2_w", "w2", FF // 128, D), ("Wr", "wr", KC, NX)):
            pieces.append(([a[n].rearrange("(k p) o -> p k o", p=128)], m * o, lambda part, w=w: k[w][:, :, part, :], m, o))
        lw = [sem(f"piece_loaded{i}") for i in range(2)]
        ll, lo_, pool, hi, low, pe, dve, act = (sem(n) for n in (
            "rows_loaded", "others_loaded", "pool_done", "high_done", "low_done", "turned", "dve_done", "act_done"))
        stage = lambda n, m, o: stg[:, n % 2, 0:m * o].rearrange("p (k o) -> p k o", o=o)
        with nc.Block() as block:
            @block.sync
            def _(sp):
                total = [0, 0]
                for n, (srcs, width, _, m, o) in enumerate(pieces):
                    if n >= 2:
                        sp.wait_ge(low, n - 1)
                    for j, src in enumerate(srcs):
                        sp.dma_start(stg[:, n % 2, j * width:(j + 1) * width].rearrange("p (k o) -> p k o", o=o), src
                                     ).then_inc(lw[n % 2], 16)

            @block.gpsimd
            def _(p):
                p.memset(lines[:], 0.0).then_inc(pool, 1)
                p.memset(k["epsc"][:, 0:1], 1e-5).then_inc(pool, 1)
                p.memset(k["epsc"][:, 1:2], 1e-6).then_inc(pool, 1)
                p.memset(k["epsc"][:, 2:3], 1e-3).then_inc(pool, 1)

            @block.scalar
            def _(s):
                s.wait_ge(pool, 4)
                for j, n in enumerate(BNS):
                    s.dma_start(lines[:, j, :], a[n].rearrange("e (k p) -> (e k) p", p=128)).then_inc(ll, 16)
                for j, (n, r) in enumerate(SHORT):
                    s.dma_start(lines[0:r, len(BNS) + j, :], a[n].rearrange("(k p) -> k p", p=128)).then_inc(ll, 16)
                s.dma_start(k["rb"][:, 0:D], row(a["ffn2_b"], GN)).then_inc(lo_, 16)
                s.dma_start(k["rb"][:, D:], row(a["br"], GN)).then_inc(lo_, 16)
                s.dma_start(k["bo"][:], a["bo"]).then_inc(lo_, 16)
                s.wait_ge(dve, 1)
                for l in range(2):
                    i = s.activation(bsd[:, l, :], k["par"][:, 5 * l, :], ACT.Sqrt, bias=k["epsc"][:, 2:3])
                i.then_inc(act, 1)
                loads = [0, 0]
                for n, (srcs, width, place, m, o) in enumerate(pieces):
                    loads[n % 2] += 16 * len(srcs)
                    s.wait_ge(lw[n % 2], loads[n % 2])
                    s.activation(place(0), stage(n, m, o), ACT.Copy, scale=SW).then_inc(hi, 1)
                s.wait_ge(lo_, 48)

            @block.vector
            def _(v):
                v.wait_ge(pe, 1)
                v.tensor_copy(k["par"][:].rearrange("p j r -> p (j r)"), ps[0][:, 0:15 * EK]).then_inc(dve, 1)
                v.wait_ge(act, 1)
                v.reciprocal(btm[:], bsd[:]).then_inc(dve, 1)
                v.wait_ge(dve, 2)
                for l in range(2):
                    v.tensor_tensor(btm[:, l, :], btm[:, l, :], k["par"][:, 5 * l + 1, :], ALU.mult)
                    i = v.tensor_tensor(bsd[:, l, :], k["par"][:, 5 * l + 3, :], k["par"][:, 5 * l + 4, :], ALU.subtract)
                i.then_inc(dve, 1)
                v.wait_ge(dve, 3)
                v.tensor_tensor(bsd[:], bsd[:], btm[:], ALU.mult).then_inc(dve, 1)
                v.wait_ge(dve, 4)
                for l in range(2):
                    i = v.tensor_tensor(bsd[:, l, :], bsd[:, l, :], k["par"][:, 5 * l + 2, :], ALU.add)
                i.then_inc(dve, 1)
                v.wait_ge(dve, 5)
                v.tensor_scalar(k["bsc"][:], btm[:], 1.0 / SW, None, ALU.mult)
                v.tensor_scalar(k["bbi"][:], bsd[:], SA, None, ALU.mult)
                v.tensor_scalar(k["upb"][:], k["par"][:, 14, 0:FF // 128], SA, None, ALU.mult)
                for j, col in enumerate((13, 11, 12)):
                    for g in range(TG):
                        v.tensor_copy(k["gnp"][:, j, :, g], k["par"][:, col, 0:KC])
                for n, (srcs, width, place, m, o) in enumerate(pieces):
                    v.wait_ge(hi, n + 1)
                    v.scalar_tensor_tensor(place(1), stage(n, m, o), SW, place(0), ALU.mult, ALU.subtract).then_inc(low, 1)
                v.wait_ge(low, len(pieces))

            @block.tensor
            def _(e):
                e.wait_ge(ll, 16 * 15)
                for j in range(15):
                    m = e.transpose(ps[0][:, j * EK:(j + 1) * EK], lines[:, j, :], t["ident"][0:EK, 0:EK])
                m.then_inc(pe, 1)


def attend(nc, ps, a, t, out, general=False):
    pre = "general_" if general else ""
    with ExitStack() as c:
        sb = lambda n, s, d: c.enter_context(nc.sbuf_tensor(pre + n, s, d))
        sem = lambda n: c.enter_context(nc.semaphore(pre + n))
        we = sb("expert_w", [128, NX, 3, KC, 2, D], F16)
        wo = sb("o_w", [128, KC, 2, D], F16)
        w1 = sb("up_w", [128, KC, 2, FF], F16)
        w2 = sb("down_w", [128, FF // 128, 2, D], F16)
        wr = sb("router_w", [128, KC, 2, NX], F16)
        bo = sb("bo", [NX, D], F32)
        rb = sb("row_bias", [GN, D + NX], F32)
        par = sb("feature_par", [128, 15, 16], F32)
        bsc = sb("bn_scale", [128, 2, NX * KC], F32)
        bbi = sb("bn_bias", [128, 2, NX * KC], F32)
        gnp = sb("gn2_par", [128, 3, KC, TG], F32)
        upb = sb("up_bias", [128, FF // 128], F32)
        epsc = sb("eps2", [128, 3], F32)
        prepare_ffn(nc, ps, a, t, dict(we=we, wo=wo, w1=w1, w2=w2, wr=wr, bo=bo, rb=rb, par=par, bsc=bsc, bbi=bbi,
                                       gnp=gnp, upb=upb, epsc=epsc), pre)
        kv = [sb(f"kv_rows{k}", [128, TPB, 2 * D], F32) for k in range(RK)]
        stage = [sb(f"kv_stage{k}", [128, BS // 2 * TPB], I32) for k in range(2)]
        hot = [sb(f"hot_node{k}", [128, TPB, GN], F16) for k in range(RK)]
        hot32 = [sb(f"hot_node_wide{k}", [128, TPB, GN], F32) for k in range(2)]
        hotT = [sb(f"hot_nodeT{k}", [GN, TPB, 128], F16) for k in range(2)]
        prod = sb("prod", [128, TPB, D], F32)
        raw = sb("score_raw", [128, TPB, H], F32)
        clip = sb("score_clip", [128, TPB, H], F32)
        sv = [sb(f"weighted{k}", [128, TPB, D + H], F32) for k in range(2)]
        zinv = sb("zinv", [GN, 2, H], F32)
        attn = sb("attn", [GN, TG, D], F32)
        xt = sb("x_tile", [GN, TG, D], F32)
        rows = sb("ln_rows", [GN, TG, D], F32)
        actT = sb("actT", [128, 2, KC, TT], F16)
        gnT = sb("gnT", [128, 2, KC, TT], F16)
        wide = sb("wide", [128, 4, TT], F32)
        parts = sb("parts", [128, 2, 2, KC, TT], F16)
        st = sb("st", [128, 2 * TG, 6], F32)
        mv = sb("mv2", [128, 2 * TG, 2], F32)
        gs = sb("gs", [128, 8, 2 * TG], F32)
        lst = sb("lst", [GN, TG, 6], F32)
        lmv = sb("lmv", [GN, TG, 2], F32)
        lsd = sb("lsd", [GN, 2, TG], F32)
        lg = sb("lg", [GN, 4, TG, NX], F32)
        lred = sb("lred", [GN, 3, TG], F32)
        mixd = sb("mixd", [GN, TG, NX], F32)
        mixT = sb("mixT", [NX, TT], F32)

        gathered = [sem(f"kv_gathered{k}") for k in range(RK)]
        names = ("staged", "hot_ready", "hotT_sum", "hotT_ready", "q_ready", "prod_ready", "raw_ready", "clip_ready",
                 "exp_ready", "hot_wide_ready", "weighted_ready", "summed", "z_ready", "attn_ready")
        (staged, hot_ready, t_ready, ht_ready, q_ready, prod_ready, raw_ready, clip_ready, exp_ready, wide_ready, sv_ready,
         summed, z_ready, attn_ready) = (sem(n) for n in names)
        x_loaded, stored, ticks = sem("x_loaded"), sem("out_stored"), sem("ticks2")
        PE = Steps(sem("tensor_steps"), PRODUCTS)
        AC = Steps(sem("scalar_steps"), [x for p in PRODUCTS for x in ACT_OF[p]])
        DV = Steps(sem("vector_steps"), [x for p in PRODUCTS for x in DVE_OF[p]])
        pT, pQ, pW = ps[0], (ps[1], ps[2]), ps[3]
        bankT = pT[0:GN, :].rearrange("p (k e) -> p k e", k=TPB)
        pair = [t["psum"][:, 4:6, :], t["psum"][:, 6:8, :]]
        PAIR = {"attnT": 0, "o": 1, "up_0": 0, "up_1": 1, "down": 0, "rowsT": 1, "route": 1, "mixT": 0, "bo": 1}
        for x in EXPERTS:
            PAIR[x] = int(x[3:]) % 2
        TAKEN = {"attnT": (DV, "attnT_lo"), "o": (AC, "o_out"), "up_0": (AC, "up_0"), "up_1": (AC, "up_1"),
                 "down": (DV, "x1"), "rowsT": (DV, "rowsT_lo"), "route": (DV, "logit"), "mixT": (DV, "mixT_out"),
                 "bo": (DV, "bo_add")}
        for x in EXPERTS:
            TAKEN[x] = (DV, x + "_add") if x[:2] == "l3" else (AC, x)
        CW, CQ, CV, CE = RK, 2, RK, RK

        def schedule(eng, s, edges_step, product, late):
            for b in range(BS):
                for half in range(2):
                    if edges_step:
                        edges_step(b, half)
                    if product:
                        for p in PRODUCTS:
                            if WHEN[p] + late == 2 * b + half:
                                product(s, p)

        def stream(eng, edges_step, product, late):
            if general:
                with eng.Fori(0, NS) as i:
                    schedule(eng, i, None, product, late)
                return
            schedule(eng, None, lambda b, h: edges_step(0, b, h), None, late)
            with eng.Fori(0, NS - 1) as i:
                schedule(eng, i, lambda b, h: edges_step(i + 1, b, h), product, late)
            for b, half in ((0, 0), (0, 1), (1, 0)):
                edges_step(NS, b, half)
            schedule(eng, NS - 1, None, product, late)

        def ends(s, b):
            return isinstance(s, int) and s == 0 and b == 0, isinstance(s, int) and s == NS

        with nc.Block() as block:
            @block.sync
            def _(sp):
                with sp.Fori(0, NS) as s:
                    if general:
                        sp.wait_ge(PE.sem, PE.before(s))
                        sp.dma_start(attn[:], t["attn"][bass.ds(s * TT, TT), :].rearrange("(g p) d -> p g d", p=GN)
                                     ).then_inc(attn_ready, 16)
                    sp.dma_start(xt[:], a["x"][bass.ds(s * TT, TT), :].rearrange("(g p) d -> p g d", p=GN)).then_inc(x_loaded, 16)
                    sp.wait_ge(DV.sem, DV.at(s, f"l3_{NX - 1}_add"))
                    sp.dma_start(out[bass.ds(s * TT, TT), :].rearrange("(g p) d -> p g d", p=GN), xt[:]).then_inc(stored, 16)
                    sp.wait_ge(stored, 16 * (s + 1))
                    sp.sem_inc(ticks)

            @block.gpsimd
            def _(p):
                if general:
                    return
                with p.Fori(0, NS) as s:
                    for b in range(BS):
                        h = b // (BS // 2)
                        if b % (BS // 2) == 0:
                            p.wait_ge(staged, 2 * s + h + 1)
                        p.wait_ge(sv_ready, BS * s + b + 1)
                        p.sem_inc(ticks)
                        for k in range(TPB):
                            col = (b - h * BS // 2) * TPB + k
                            p.indirect_dma_start(
                                out=kv[b % RK][:, k, :], out_offset=None, in_=t["kv"],
                                in_offset=bass.IndirectOffsetOnAxis(ap=stage[h][:, col:col + 1], axis=0)
                            ).then_inc(gathered[b % RK], 16)

            @block.scalar
            def _(v):
                def put_stage(s, h):
                    n = BS // 2 * TPB
                    v.activation(stage[h][:], t["src"][:, bass.ds((2 * s + h) * n, n)], ACT.Copy).then_inc(staged, 1)

                def transposed(s, b):
                    v.wait_ge(t_ready, BS * s + b + 1)
                    v.wait_ge(q_ready, BS * s + b + 1)
                    v.activation(hotT[b % 2][:], bankT, ACT.Copy).then_inc(ht_ready, 1)

                def edges_step(s, b, half):
                    first, last = ends(s, b)
                    if last:
                        return
                    if half == 0:
                        if first:
                            transposed(s, 0)
                        transposed(s, b + 1)
                    else:
                        v.wait_ge(clip_ready, BS * s + b + 1)
                        v.wait_ge(summed, BS * s + b - 1 + CW)
                        v.activation(hot32[b % 2][:], hot[b % RK][:], ACT.Copy).then_inc(wide_ready, 1)
                        v.activation(sv[b % 2][:, :, D:], clip[:], ACT.Exp, scale=1.0 / SQRT_DH).then_inc(exp_ready, 1)
                        if b in (BS // 2 - 1, BS - 1):
                            h = b // (BS // 2)
                            put_stage(s + 1, h)

                def product(s, p):
                    bk = pair[PAIR[p]]
                    if p in ("attnT", "rowsT"):
                        v.wait_ge(PE.sem, PE.at(s, p))
                        v.activation(actT[:, 0], bk[:, :, 0:TT], ACT.Copy, scale=SA).then_inc(AC.sem, 1)
                    elif p == "o":
                        v.wait_ge(PE.sem, PE.at(s, p))
                        for m in range(KC):
                            i = v.activation(wide[:, m, :], bk[:, m, 0:TT], ACT.Identity, bias=par[:, 10, m:m + 1], scale=DESC)
                        i.then_inc(AC.sem, 1)
                        v.wait_ge(DV.sem, DV.at(s, "gn_d"))
                        v.activation(gs[:, 3, :], gs[:, 2, :], ACT.Sqrt, bias=epsc[:, 1:2]).then_inc(AC.sem, 1)
                        v.wait_ge(DV.sem, DV.at(s, "gn_out"))
                        v.activation(gnT[:, 0], wide[:, 2:4, :], ACT.Copy).then_inc(AC.sem, 1)
                    elif p[:2] == "up":
                        h = int(p[3])
                        v.wait_ge(PE.sem, PE.at(s, p))
                        if h == 1:
                            v.wait_ge(DV.sem, DV.at(s, "gn_lo"))
                        for m in range(KC):
                            i = v.activation(wide[:, 2 * h + m, :], bk[:, m, 0:TT], ACT.Relu, scale=DESC * SA,
                                             bias=upb[:, 2 * h + m:2 * h + m + 1])
                        i.then_inc(AC.sem, 1)
                        v.wait_ge(AC.sem, AC.at(s, p))
                        v.activation(parts[:, h, 0], wide[:, 2 * h:2 * h + 2, :], ACT.Copy).then_inc(AC.sem, 1)
                    elif p == "down":
                        v.wait_ge(DV.sem, DV.at(s, "ln_mv"))
                        v.activation(lsd[:, 0, :], lmv[:, :, 1], ACT.Sqrt, bias=epsc[0:GN, 0:1]).then_inc(AC.sem, 1)
                    elif p == "route":
                        v.wait_ge(DV.sem, DV.at(s, "lsub"))
                        v.activation(lg[:, 2], lg[:, 1], ACT.Exp).then_inc(AC.sem, 1)
                    elif p[:2] in ("l1", "l2"):
                        e, l = int(p[3:]), int(p[1]) - 1
                        v.wait_ge(PE.sem, PE.at(s, p))
                        for m in range(KC):
                            k = e * KC + m
                            i = v.activation(wide[:, 2 * (e % 2) + m, :], bk[:, m, 0:TT], ACT.Relu,
                                             scale=bsc[:, l, k:k + 1], bias=bbi[:, l, k:k + 1])
                        i.then_inc(AC.sem, 1)
                        v.wait_ge(AC.sem, AC.at(s, p))
                        v.activation(parts[:, e % 2, 0], wide[:, 2 * (e % 2):2 * (e % 2) + 2, :], ACT.Copy).then_inc(AC.sem, 1)

                v.sem_inc(AC.sem, 1)
                v.sem_inc(exp_ready, CE)
                if not general:
                    for h in range(2):
                        put_stage(0, h)
                stream(v, edges_step, product, 1)

            @block.vector
            def _(v):
                def make_hot(s, b):
                    v.wait_ge(exp_ready, BS * s + b + 1)
                    for k in range(TPB):
                        m = v.tensor_scalar(hot[b % RK][:, k, :], t["iota"][:, 0:GN],
                                            t["loc"][:, bass.ds((BS * s + b) * TPB + k, 1)], None, ALU.is_equal)
                    m.then_inc(hot_ready, 1)

                def weigh(s, b):
                    v.wait_ge(exp_ready, BS * s + b + 1 + CE)
                    x = sv[b % 2]
                    v.tensor_tensor(x[:, :, 0:D].rearrange("p k (h d) -> p k h d", h=H),
                                    kv[b % RK][:, :, D:].rearrange("p k (h d) -> p k h d", h=H),
                                    x[:, :, D:].unsqueeze(3).broadcast_to([128, TPB, H, DH]), ALU.mult).then_inc(sv_ready, 1)

                def graph_out(g_abs, g):
                    v.wait_ge(summed, (g_abs + 1) * BPG + CW)
                    v.tensor_scalar(zinv[:, 0, :], pW[0:GN, D:D + H], 1e-6, None, ALU.add).then_inc(z_ready, 1)
                    v.wait_ge(z_ready, 2 * g_abs + 1)
                    v.reciprocal(zinv[:, 1, :], zinv[:, 0, :]).then_inc(z_ready, 1)
                    v.wait_ge(z_ready, 2 * g_abs + 2)
                    v.tensor_tensor(attn[:, g, :].rearrange("p (h d) -> p h d", h=H),
                                    pW[0:GN, 0:D].rearrange("p (h d) -> p h d", h=H),
                                    zinv[:, 1, :].unsqueeze(2).broadcast_to([GN, H, DH]), ALU.mult).then_inc(attn_ready, 1)

                def edges_step(s, b, half):
                    first, last = ends(s, b)
                    n = BS * s + b
                    if half == 0:
                        if first:
                            make_hot(s, 0)
                            make_hot(s, 1)
                        if not first and not (last and b):
                            weigh(s if b else s - 1, b - 1 if b else BS - 1)
                        if not last:
                            v.wait_ge(q_ready, n + 1 + CQ)
                            v.wait_ge(gathered[b % RK], 16 * TPB * ((BS // RK) * s + b // RK + 1))
                            if not first:
                                v.wait_ge(raw_ready, n)
                            for k in range(2):
                                m = v.tensor_tensor(prod[:, 2 * k:2 * k + 2, :], pQ[k].rearrange("p (k d) -> p k d", k=2),
                                                    kv[b % RK][:, 2 * k:2 * k + 2, 0:D], ALU.mult)
                            m.then_inc(prod_ready, 1)
                        if b % BPG == 1 and (b > 1 or not isinstance(s, int) or s > 0):
                            g = TG * s + b // BPG - 1
                            if b == BPG + 1 and not isinstance(s, int):
                                v.wait_ge(PE.sem, PE.at(s - 1, "attnT"))
                            graph_out(g, (b // BPG - 1) % TG)
                    elif not last:
                        v.wait_ge(prod_ready, n + 1)
                        v.reduce_sum(raw[:].rearrange("p k h -> p (k h)"),
                                     prod[:].rearrange("p k (h d) -> p (k h) d", h=H), X).then_inc(raw_ready, 1)
                        v.wait_ge(raw_ready, n + 1)
                        v.wait_ge(exp_ready, n + CE)
                        v.tensor_scalar(clip[:], raw[:], -10.0 * SQRT_DH, 10.0 * SQRT_DH, ALU.max, ALU.min).then_inc(clip_ready, 1)
                        make_hot(s, b + 2)

                def product(s, p):
                    bk = pair[PAIR[p]]
                    wait = lambda e, n: v.wait_ge(e.sem, e.at(s, n))
                    inc = lambda i: i.then_inc(DV.sem, 1)
                    if p in ("attnT", "rowsT"):
                        wait(AC, p + "_hi")
                        inc(v.scalar_tensor_tensor(actT[:, 1], bk[:, :, 0:TT], SA, actT[:, 0], ALU.mult, ALU.subtract))
                    elif p == "o":
                        wait(AC, "o_out")
                        for m in range(KC):
                            for g in range(TG):
                                i = v.bn_stats(st[:, TG * m + g, :], wide[:, m, g * GN:(g + 1) * GN])
                        inc(i)
                        wait(DV, "gn_st")
                        v.sem_inc(ticks)
                        for k in range(2 * TG):
                            i = v.bn_aggr(mv[:, k, :], st[:, k, :])
                        inc(i)
                        wait(DV, "gn_mv")
                        ms, gw, gb = (gnp[:, k].rearrange("p m g -> p (m g)") for k in range(3))
                        inc(v.tensor_tensor(gs[:, 0, :], mv[:, :, 0], ms, ALU.mult))
                        wait(DV, "gn_a")
                        inc(v.tensor_tensor(gs[:, 1, :], mv[:, :, 0], gs[:, 0, :], ALU.subtract))
                        wait(DV, "gn_b")
                        inc(v.tensor_tensor(gs[:, 4, :], gs[:, 1, :], gs[:, 1, :], ALU.mult))
                        wait(DV, "gn_c")
                        inc(v.tensor_tensor(gs[:, 2, :], gs[:, 4, :], mv[:, :, 1], ALU.add))
                        wait(AC, "gn_std")
                        inc(v.reciprocal(gs[:, 5, :], gs[:, 3, :]))
                        wait(DV, "gn_e")
                        inc(v.scalar_tensor_tensor(gs[:, 6, :], gs[:, 5, :], SA, gw, ALU.mult, ALU.mult))
                        wait(DV, "gn_f")
                        inc(v.tensor_tensor(gs[:, 7, :], gs[:, 0, :], gs[:, 6, :], ALU.mult))
                        wait(DV, "gn_g")
                        inc(v.scalar_tensor_tensor(gs[:, 5, :], gb, SA, gs[:, 7, :], ALU.mult, ALU.subtract))
                        wait(DV, "gn_h")
                        for m in range(KC):
                            for g in range(TG):
                                k = TG * m + g
                                i = v.tensor_scalar(wide[:, 2 + m, g * GN:(g + 1) * GN], wide[:, m, g * GN:(g + 1) * GN],
                                                    gs[:, 6, k:k + 1], gs[:, 5, k:k + 1], ALU.mult, ALU.add)
                        inc(i)
                        wait(AC, "gn_hi")
                        inc(v.tensor_tensor(gnT[:, 1], wide[:, 2:4, :], gnT[:, 0], ALU.subtract))
                    elif p[:2] == "up":
                        h = int(p[3])
                        wait(AC, p + "_hi")
                        inc(v.tensor_tensor(parts[:, h, 1], wide[:, 2 * h:2 * h + 2, :], parts[:, h, 0], ALU.subtract))
                    elif p == "down":
                        v.wait_ge(x_loaded, 16 * (s + 1))
                        inc(v.tensor_tensor(xt[:], xt[:], rb[:, 0:D].unsqueeze(1).broadcast_to([GN, TG, D]), ALU.add))
                        wait(PE, "down")
                        wait(DV, "x_bias")
                        inc(v.scalar_tensor_tensor(xt[:].rearrange("p (b g) d -> p b (g d)", b=2), bk[0:GN], DESC,
                                                   xt[:].rearrange("p (b g) d -> p b (g d)", b=2), ALU.mult, ALU.add))
                        wait(DV, "x1")
                        for g in range(TG):
                            i = v.bn_stats(lst[:, g, :], xt[:, g, :])
                        inc(i)
                        wait(DV, "ln_st")
                        v.sem_inc(ticks)
                        for g in range(TG):
                            i = v.bn_aggr(lmv[:, g, :], lst[:, g, :])
                        inc(i)
                        wait(AC, "ln_std")
                        inc(v.reciprocal(lsd[:, 1, :], lsd[:, 0, :]))
                        wait(DV, "ln_rstd")
                        for g in range(TG):
                            i = v.tensor_scalar(rows[:, g, :], xt[:, g, :], lmv[:, g, 0:1], lsd[:, 1, g:g + 1],
                                                ALU.subtract, ALU.mult)
                        inc(i)
                    elif p == "route":
                        wait(PE, "route")
                        inc(v.scalar_tensor_tensor(lg[:, 0], bk[0:GN, 0, 0:TG * NX].rearrange("p (g e) -> p g e", g=TG), DESC,
                                                   rb[:, D:].unsqueeze(1).broadcast_to([GN, TG, NX]), ALU.mult, ALU.add))
                        wait(DV, "logit")
                        inc(v.reduce_max(lred[:, 0, :], lg[:, 0], X))
                        wait(DV, "lmax")
                        inc(v.tensor_tensor(lg[:, 1], lg[:, 0], lred[:, 0, :].unsqueeze(2).broadcast_to([GN, TG, NX]), ALU.subtract))
                        wait(AC, "mix_exp")
                        inc(v.reduce_sum(lred[:, 1, :], lg[:, 2], X))
                        wait(DV, "lsum")
                        inc(v.reciprocal(lred[:, 2, :], lred[:, 1, :]))
                        wait(DV, "lrec")
                        inc(v.tensor_tensor(lg[:, 3], lg[:, 2], lred[:, 2, :].unsqueeze(2).broadcast_to([GN, TG, NX]), ALU.mult))
                        wait(DV, "mix")
                        inc(v.tensor_scalar(mixd[:], lg[:, 3], DESC, None, ALU.mult))
                    elif p == "mixT":
                        wait(PE, "mixT")
                        inc(v.tensor_copy(mixT[:], bk[0:NX, 0, 0:TT]))
                    elif p == "bo":
                        wait(PE, "bo")
                        wait(DV, "l3_1_add")
                        inc(v.tensor_tensor(xt[:].rearrange("p (b g) d -> p b (g d)", b=2), bk[0:GN],
                                            xt[:].rearrange("p (b g) d -> p b (g d)", b=2), ALU.add))
                    elif p[:2] in ("l1", "l2"):
                        e = int(p[3:]) % 2
                        wait(AC, p + "_hi")
                        inc(v.tensor_tensor(parts[:, e, 1], wide[:, 2 * e:2 * e + 2, :], parts[:, e, 0], ALU.subtract))
                    else:
                        e = int(p[3:])
                        wait(PE, p)
                        wait(DV, "ln_out" if e == 0 else "bo_add" if e == 2 else f"l3_{e - 1}_add")
                        for g in range(TG):
                            i = v.scalar_tensor_tensor(xt[:, g, :], bk[0:GN, g // 2, (g % 2) * D:(g % 2 + 1) * D],
                                                       mixd[:, g, e:e + 1], xt[:, g, :], ALU.mult, ALU.add)
                        inc(i)

                v.sem_inc(sv_ready, CV)
                v.sem_inc(DV.sem, 1)
                stream(v, edges_step, product, 1)

            @block.tensor
            def _(e):
                def turn(s, b):
                    e.wait_ge(hot_ready, BS * s + b + 1)
                    if not (isinstance(s, int) and s == 0 and b == 0):
                        e.wait_ge(ht_ready, BS * s + b)
                    for k in range(TPB):
                        m = e.matmul(bankT[:, k, :], hot[b % RK][:, k, :], t["ident16"][:], start=True, stop=True)
                    m.then_inc(t_ready, 1)

                def look_up(s, b):
                    n = BS * s + b
                    e.wait_ge(ht_ready, n + 1)
                    if not (isinstance(s, int) and s == 0 and b == 0):
                        e.wait_ge(prod_ready, n)
                    for k in range(TPB):
                        for part in range(2):
                            m = e.matmul(pQ[k // 2][:, (k % 2) * D:(k % 2 + 1) * D], hotT[b % 2][:, k, :],
                                         t["q"][:, bass.ds(s * TG + b // BPG, 1), part, :].rearrange("p o d -> p (o d)"),
                                         start=(part == 0), stop=(part == 1))
                    m.then_inc(q_ready, 1)

                def add_up(s, b):
                    n = BS * s + b
                    e.wait_ge(sv_ready, n + 1 + CV)
                    if b % BPG == 0 and not (isinstance(s, int) and s == 0 and b == 0):
                        e.wait_ge(attn_ready, TG * s + b // BPG)
                    for k in range(TPB):
                        m = e.matmul(pW[0:GN, 0:D + H], hot32[b % 2][:, k, :], sv[b % 2][:, k, :],
                                     start=(b % BPG == 0 and k == 0), stop=(b % BPG == BPG - 1 and k == TPB - 1))
                    m.then_inc(summed, 1)

                def edges_step(s, b, half):
                    first, last = ends(s, b)
                    if half == 0:
                        if first:
                            turn(s, 0)
                        if b == 0 and not last:
                            look_up(s, 0)
                        if not last:
                            turn(s, b + 1)
                    else:
                        if b + 1 < BS and not last:
                            look_up(s, b + 1)
                        if not first:
                            add_up(s if b else s - 1, b - 1 if b else BS - 1)

                def parts3(dst, left, right, start, stop):
                    for n, (pl, pr) in enumerate(((0, 0), (0, 1), (1, 0))):
                        m = e.matmul(dst, left(pl), right(pr), start=(start and n == 0), stop=(stop and n == 2))
                    return m

                def product(s, p):
                    q = PAIR[p]
                    bk = pair[q]
                    before = [x for x in PRODUCTS[:PRODUCTS.index(p)] if PAIR[x] == q]
                    if before:
                        eng, name = TAKEN[before[-1]]
                        e.wait_ge(eng.sem, eng.at(s, name))
                    else:
                        e.wait_ge(DV.sem, DV.before(s))
                    wait = lambda eng, n: e.wait_ge(eng.sem, eng.at(s, n))
                    if p == "attnT" or p == "rowsT":
                        src = attn if p == "attnT" else rows
                        if p == "attnT":
                            e.wait_ge(attn_ready, (16 if general else TG) * (s + 1))
                        else:
                            wait(DV, "ln_out")
                        for kc in range(KC):
                            for g in range(TG):
                                m = e.transpose(bk[:, kc, g * GN:(g + 1) * GN], src[:, g, kc * 128:(kc + 1) * 128],
                                                t["ident"][0:GN, 0:GN])
                    elif p in ("o", "up_0", "up_1") or p[:2] in ("l1", "l2"):
                        if p == "o":
                            wait(DV, "attnT_lo")
                            x, m0 = lambda k, pa: actT[:, pa, k, :], 0
                            w = lambda k, pw, m: wo[:, k, pw, m * 128:(m + 1) * 128]
                        elif p[:2] == "up":
                            wait(DV, "gn_lo")
                            x, m0 = lambda k, pa: gnT[:, pa, k, :], 2 * int(p[3])
                            w = lambda k, pw, m: w1[:, k, pw, m * 128:(m + 1) * 128]
                        else:
                            ex, l, m0 = int(p[3:]), int(p[1]) - 1, 0
                            w = lambda k, pw, m: we[:, ex, l, k, pw, m * 128:(m + 1) * 128]
                            if l == 0:
                                wait(DV, "rowsT_lo")
                                x = lambda k, pa: actT[:, pa, k, :]
                            else:
                                wait(DV, f"l1_{ex}_lo")
                                x = lambda k, pa: parts[:, ex % 2, pa, k, :]
                        for mm in range(KC):
                            for k in range(KC):
                                m = parts3(bk[:, mm, 0:TT], lambda pw: w(k, pw, m0 + mm), lambda pa: x(k, pa),
                                           k == 0, k == KC - 1)
                    elif p == "down":
                        wait(DV, "up_1_lo")
                        for g in range(TG):
                            for k in range(FF // 128):
                                m = parts3(bk[0:GN, g // 2, (g % 2) * D:(g % 2 + 1) * D],
                                           lambda pa: parts[:, k // 2, pa, k % 2, g * GN:(g + 1) * GN],
                                           lambda pw: w2[:, k, pw, :], k == 0, k == FF // 128 - 1)
                    elif p == "route":
                        wait(DV, "rowsT_lo")
                        for g in range(TG):
                            for k in range(KC):
                                m = parts3(bk[0:GN, 0, g * NX:(g + 1) * NX], lambda pa: actT[:, pa, k, g * GN:(g + 1) * GN],
                                           lambda pw: wr[:, k, pw, :], k == 0, k == KC - 1)
                    elif p == "mixT":
                        wait(DV, "mix")
                        for g in range(TG):
                            m = e.transpose(bk[0:NX, 0, g * GN:(g + 1) * GN], lg[:, 3, g, :], t["ident"][0:GN, 0:GN])
                    elif p == "bo":
                        for g in range(TG):
                            m = e.matmul(bk[0:GN, g // 2, (g % 2) * D:(g % 2 + 1) * D], mixT[:, g * GN:(g + 1) * GN], bo[:],
                                         start=True, stop=True)
                    else:
                        ex = int(p[3:])
                        wait(DV, f"l2_{ex}_lo")
                        for g in range(TG):
                            for k in range(KC):
                                m = parts3(bk[0:GN, g // 2, (g % 2) * D:(g % 2 + 1) * D],
                                           lambda pa: parts[:, ex % 2, pa, k, g * GN:(g + 1) * GN],
                                           lambda pw: we[:, ex, 2, k, pw, :], k == 0, k == KC - 1)
                    m.then_inc(PE.sem, 1)

                e.sem_inc(summed, CW)
                e.sem_inc(q_ready, CQ)
                e.sem_inc(PE.sem, 1)
                stream(e, edges_step, product, 0)


_GNN = [f"{n}_{m}" for n in ("q", "k", "v") for m in ("bases", "comb", "bias")] + [
    "gn1_w", "gn1_b", "gn1_ms", "gn2_w", "gn2_b", "gn2_ms", "O_w", "O_b", "ffn1_w", "ffn1_b", "ffn2_w", "ffn2_b"]
_FFN = ["Wr", "br", "W1", "b1", "g1", "be1", "m1", "v1", "W2", "b2", "g2", "be2", "m2", "v2", "Wo", "bo"]


def arrays(inputs):
    import numpy as np
    edges = np.zeros((3, EP), np.int32)
    edges[DST] = FAR
    for r, n in ((DST, "dst"), (SRC, "src"), (TYP, "edge_type_9")):
        edges[r, :ED] = np.asarray(inputs[n])
    arr = {"x": np.asarray(inputs["x"]), "edges": edges}
    arr.update({n: np.asarray(inputs[f"L0_gnn_{n}"]) for n in _GNN})
    arr.update({n: np.asarray(inputs[f"L0_ffn_{n}"]) for n in _FFN})
    return arr


def kernel(**inputs):
    import concourse.bacc as bacc
    from concourse.bass_utils import run_bass_kernel_spmd

    nc = bacc.Bacc("TRN2", target_bir_lowering=False, num_devices=1)
    arr = arrays(inputs)
    a = {n: nc.dram_tensor(f"in_{n}", list(v.shape), mybir.dt.from_np(v.dtype), kind="ExternalInput").ap()
         for n, v in arr.items()}
    out = nc.dram_tensor("out", [N, D], F32, kind="ExternalOutput").ap()
    build(nc, a, out)
    r = run_bass_kernel_spmd(nc, [{f"in_{n}": v for n, v in arr.items()}], core_ids=[0])
    return r.results[0]["out"]
```

```python
from contextlib import ExitStack

import concourse.bass as bass
import concourse.mybir as mybir

F32, F16, I32 = mybir.dt.float32, mybir.dt.float16, mybir.dt.int32
ALU = mybir.AluOpType
ACT = mybir.ActivationFunctionType
X = mybir.AxisListType.X

N, D, R = 5000, 256, 9
ED = 85000
GN = 125
NG = N // GN
BN = 25
NB = N // BN
BPG = GN // BN
TPB = 4
WIN = TPB * 128
NT = NB * TPB
ETL = -(-ED // 128)
NCH = -(-ETL // TPB)
EP = 128 * 700
FAR = 1 << 20
NBIN = BN * R
GBIN = GN * R
H, DH = 8, 32
NX = 8
DST, SRC, TYP = 0, 1, 2
FF = 2 * D
TG = 4
TT = TG * GN
NS = N // TT
KC = D // 128

SA = 16.0
SW = 64.0
WS = 1.0 / 64
DESC = 1.0 / (SA * SW)
SQRT_DH = float(DH) ** 0.5


class Psum:

    def __init__(self, ctx, nc):
        self.all = ctx.enter_context(nc.psum_tensor("banks", [128, 8, 512], F32))
        self.b = [self.all[:, i, :] for i in range(8)]


def row(ap, p):
    return ap.rearrange("(a n) -> a n", a=1).broadcast_to([p, ap.shape[0]])


def build(nc, a, out):
    ctx = ExitStack()
    with ctx:
        psum = Psum(ctx, nc)
        ps = psum.b

        def keep(name, shape, dt):
            return ctx.enter_context(nc.sbuf_tensor(name, shape, dt))

        t = dict(
            psum=psum.all,
            tab=nc.dram_tensor("hn_table", [N, 2 * D], F16, kind="Internal").ap(),
            kv=nc.dram_tensor("kv_table", [N, 2 * D], F32, kind="Internal").ap(),
            win=nc.dram_tensor("edge_windows", [3, NT * 128], I32, kind="Internal").ap(),
            attn=nc.dram_tensor("attention_rows", [N, D], F32, kind="Internal").ap(),
            sdr=nc.dram_tensor("window_starts", [NB], I32, kind="Internal").ap(),
            wdr=nc.dram_tensor("relation_weights", [R, D, 3 * D], F32, kind="Internal").ap(),
            ident=keep("ident", [128, 128], F32),
            ident16=keep("ident16", [128, 128], F16),
            flag=keep("flag", [1, 1], I32),
            src=keep("src_cols", [128, NT + TG * BPG * TPB], I32),
            key=keep("key_cols", [128, NT + 2 * TPB], F32),
            loc=keep("loc_cols", [128, NT + 2 * TPB], F32),
            iota=keep("iota", [128, GBIN], F16),
            w=keep("w_parts", [128, R, KC, 2, 3 * D], F16),
        )
        prologue(nc, ps, a, t)
        made = {}

        def shared_sem(name):
            if name not in made:
                made[name] = ctx.enter_context(nc.semaphore(name))
            return made[name]

        t["shared_sem"] = shared_sem
        t["q"] = keep("q_rows", [GN, NG, 2, D], F16)
        with nc.If(nc.values_load(t["flag"][:], min_val=0, max_val=128) == 0):
            conv_fast(nc, ps, a, t)
            attend(nc, ps, a, t, out)
        with nc.Else():
            list_columns(nc, ps, a, t)
            conv_general(nc, ps, a, t)
            attend_edges_general(nc, ps, a, t)
            attend(nc, ps, a, t, out, general=True)


def prologue(nc, ps, a, t):
    HB = NB // 2
    GRP = 8
    TPG = NT // GRP
    S = 8
    NCK = D // S
    KB = R * S
    NH = NCK // 2
    W3 = 3 * D
    PG = 2
    NBT = NG // PG
    XR = 4
    WPB = NB // 2 // NBT
    NWS = 6
    AHEAD = 11
    edges = a["edges"]
    with ExitStack() as c:
        sb = lambda n, s, d: c.enter_context(nc.sbuf_tensor(n, s, d))
        sem = lambda n: c.enter_context(nc.semaphore(n))
        ints = sb("ints", [128, GRP * 3 * 128], I32)
        first = ints[0:1, 0:ETL]
        rows = ints[0:HB, ETL:ETL + 512].rearrange("p (k e) -> p k e", k=4)
        dl = ints[0:GN, ETL + 512:ETL + 512 + 2 * (ED // GN)].rearrange("p (k e) -> p k e", k=2)
        tl = ints[0:TPG].rearrange("p (g a e) -> p g a e", g=GRP, a=3)
        nb = sb("node_buffers", [GN, 5, 2, PG * D], F32)
        nbuf = lambda k, b: nb[:, k, b % 2, :].rearrange("p (g d) -> p g d", g=PG)
        flat = nb[:].rearrange("p a b c -> p (a b c)")
        junk = flat[0:HB, 0:4 * ETL].rearrange("p (k e) -> p k e", k=4)
        junk2 = flat[0:HB, 4 * ETL:4 * ETL + 512].rearrange("p (k e) -> p k e", k=4)
        far = flat[0:TPG, 0:GRP * 128].rearrange("p (g e) -> p g e", g=GRP)
        y, u, sub, sq, std = (lambda b, k=k: nbuf(k, b) for k in range(5))
        firstf = sb("firstf", [1, ETL], F32)
        firstb = sb("firstb", [128, ETL], F32)
        boundi = sb("boundi", [HB, 4], I32)
        bound = sb("bound", [HB, 4], F32)
        cnt = sb("cnt", [HB, 4], F32)
        rowi = sb("rowi", [HB, 4], I32)
        rowf = sb("rowf", [HB, 4], F32)
        rowsf = sb("rowsf", [HB, 4, 128], F32)
        cnt2 = sb("cnt2", [HB, 4], F32)
        start = sb("start", [HB, 4], F32)
        starti = sb("starti", [HB, 2], I32)
        over = sb("over", [128, 4], F32)
        bad = sb("bad", [128, 1], F32)
        ones = sb("ones_col", [128, 1], F32)
        srow = sb("srow", [1, NB], I32)
        down = sb("steps_down", [GN, ED // GN], F32)
        blk = sb("blk", [TPG, 4], I32)
        blkf = sb("blkf", [TPG, 4], F32)
        off = sb("off", [TPG, 2], F32)
        ioti = sb("ioti", [128, GBIN], I32)

        bases = sb("bases", [128, 3, NH, D], F32)
        wst = lambda r: bases[:, (r % NWS) // 2, 8 * (r % 2):8 * (r % 2) + 6, :].rearrange("p (k b) o -> p k (b o)", k=KC)
        comb = sb("comb", [R, 3, R], F32)
        rep = sb("repeat", [R, R, S], F32)
        same = sb("same", [KB, R, S], F32)
        same8 = sb("same8", [KB, S], F32)
        kron = sb("kron", [KB, 3, R, S], F32)
        resb = sb("res", [128, 2, 4, 512], F32)
        res = resb[0:KB]
        tf = resb[0:TPG].rearrange("p a b c -> p (a b c)")[:, 0:GRP * 3 * 128].rearrange("p (g a e) -> p g a e", g=GRP, a=3)

        x = sb("x_in", [GN, XR, PG, D], F32)
        mv = sb("mv", [GN, 2, PG, 2], F32)
        st6 = sb("st6", [GN, 2, PG, 6], F32)
        rstd = sb("rstd", [GN, 2, PG, 1], F32)
        rinv = sb("rinv", [GN, 2, PG, 1], F32)
        nrm = sb("normed", [GN, 2, PG, D], F32)
        hl = sb("hl", [GN, XR, PG, 2, D], F16)
        par = sb("gn1_par", [GN, 3, D], F32)
        mean1 = sb("mean_mat", [GN, GN], F32)
        eps = sb("eps", [GN, 2], F32)

        loads, pool, dve, cnt_ready, turned, marked, rload, sload, wsp, wpool, tload, cols_out = (sem(n) for n in (
            "list_loaded", "pool_done", "edges_dve", "tiles_below", "tiles_turned", "marks_counted", "rows_loaded",
            "starts_moved", "windows_by_sync", "windows_by_pool", "tiles_loaded", "columns_out"))
        lb = [sem(f"bases_loaded{k}") for k in range(3)]
        lc, repeated, same_ready, kdve, product, copied = (sem(n) for n in (
            "comb_loaded", "comb_repeated", "same_ready", "kron_ready", "product_ready", "product_copied"))
        stw = [sem(f"weights_stored{k}") for k in range(2)]
        lw = [sem(f"weights_back{k}") for k in range(NWS)]
        whi, wlo = sem("w_high"), sem("w_low")
        lx = [sem(f"x_loaded{k}") for k in range(XR)]
        st = [sem(f"table_stored{k}") for k in range(XR)]
        lp, const, nticks = sem("params_loaded"), sem("constants_ready"), sem("node_ticks")
        (stats, moments, rinv_ready, y_ready, mean_scaled, centred, weighted, inverted, divided, normed, low) = (sem(n) for n in (
            "row_stats", "row_moments", "rinv_ready", "y_ready", "mean_scaled", "centred", "weighted", "inverted", "divided",
            "normed_ready", "low_ready"))
        rdev, squared, gdev, high = (sem(n) for n in ("row_dev", "squared", "graph_dev", "high_ready"))
        mean_ready, var_ready = sem("graph_mean"), sem("graph_var")
        xg = a["x"].rearrange("(b g p) d -> p b g d", p=GN, g=PG)
        tg = t["tab"].rearrange("(b g p) d -> p b g d", p=GN, g=PG)
        gp = lambda k: par[:, k:k + 1, :].broadcast_to([GN, PG, D])
        w = t["w"]
        dst = edges[DST, :]
        names = ("q", "k", "v")

        def batches(eng, step):
            for i in range(XR):
                step(i, i, 0)
            with eng.Fori(0, 3) as j:
                for k in range(XR):
                    step(XR * j + XR + k, k, j + 1)
            for i in range(4 * XR, NBT + XR):
                step(i, i % XR, i // XR)

        def between(i):
            return range(0, AHEAD) if i < 0 else range(min(48, AHEAD + 3 * i), min(48, AHEAD + 3 * i + 3))

        def has(b):
            return not isinstance(b, int) or 0 <= b < NBT

        def window(eng, j, k, done):
            starts = [eng.value_load(srow[0:1, bass.ds(j + n, 1)], min_val=0, max_val=ED) for n in range(k)]
            for n in range(k):
                eng.dma_start(t["win"][:, bass.ds((j + n) * WIN, WIN)], edges[:, bass.ds(starts[n], WIN)]).then_inc(done, 16)

        def one(ap, b):
            return ap[:, bass.ds(b, 1)].rearrange("p o g d -> p (o g) d")

        with nc.Block() as block:
            @block.sync
            def _(sp):
                for k in range(XR):
                    sp.sem_inc(st[k], 16)
                sp.dma_start(first, dst[0:ETL * 128].rearrange("(a t e) -> a t e", a=1, e=128)[:, :, 0],
                             allow_slow_non_contiguous=True).then_inc(loads, 16)
                for k in range(2):
                    sp.dma_start(dl[:, k, :], dst[k:k + ED].rearrange("(p e) -> p e", p=GN)).then_inc(loads, 16)
                for k, n in enumerate(("gn1_ms", "gn1_w", "gn1_b")):
                    sp.dma_start(par[:, k, :], row(a[n], GN)).then_inc(lp, 16)
                for b in range(2):
                    sp.dma_start(x[:, b], one(xg, b)).then_inc(lx[b], 16)
                sp.wait_ge(dve, 6)
                for k in range(2):
                    sp.dma_start(t["sdr"][k * HB:(k + 1) * HB].rearrange("(p o) -> p o", o=1),
                                 starti[:, k:k + 1]).then_inc(sload, 16)
                sp.wait_ge(sload, 32)
                sp.dma_start(srow[:], t["sdr"].rearrange("(o p) -> o p", o=1)).then_inc(sload, 16)
                sp.wait_ge(sload, 48)

                def step(i, k, lap):
                    if has(i + 2) and (not isinstance(i, int) or i + 2 < NBT):
                        if not isinstance(i, int) or i >= 2:
                            sp.wait_ge(y_ready, i - 1)
                        sp.dma_start(x[:, (k + 2) % XR], one(xg, i + 2)).then_inc(lx[(k + 2) % XR], 16)
                    if has(i):
                        window(sp, WPB * i, WPB, wsp)
                    if has(i - 4):
                        sp.wait_ge(low, i - 2)
                        sp.dma_start(one(tg, i - 4), hl[:, k]).then_inc(st[k], 16)

                batches(sp, step)
                sp.wait_ge(wsp, 16 * HB)
                sp.wait_ge(wpool, 16 * HB)
                sp.wait_ge(dve, 9)
                for g in range(GRP):
                    sp.dma_start(tl[:, g], t["win"][:, g * TPG * 128:(g + 1) * TPG * 128]
                                 .rearrange("a (p e) -> p a e", e=128)).then_inc(tload, 16)
                for k in range(XR):
                    sp.wait_ge(st[k], 16 * (NBT // XR + 1))

            @block.gpsimd
            def _(p):
                p.memset(same[:], 0.0).then_inc(same_ready, 1)
                p.memset(rep[:], 0.0).then_inc(same_ready, 1)
                p.wait_ge(same_ready, 2)
                p.affine_select(out=rep[:], in_=rep[:], compare_op=ALU.not_equal, fill=1.0, base=0,
                                pattern=[[1, R], [0, S]], channel_multiplier=-1).then_inc(same_ready, 1)
                p.affine_select(out=same[:], in_=same[:], compare_op=ALU.not_equal, fill=1.0, base=0,
                                pattern=[[-S, R], [-1, S]], channel_multiplier=1).then_inc(same_ready, 1)
                p.memset(t["ident"][:], 0.0).then_inc(pool, 1)
                p.iota(boundi[:], [[BN, 2], [BN * HB, 2]], base=0, channel_multiplier=BN).then_inc(pool, 1)
                p.memset(ones[:], 1.0).then_inc(pool, 1)
                p.memset(bad[:], 0.0).then_inc(pool, 1)
                p.wait_ge(dve, 1)
                p.partition_broadcast(firstb[:], firstf[:]).then_inc(pool, 1)
                p.memset(mean1[:], 1.0 / GN).then_inc(const, 1)
                p.memset(eps[:, 0:1], 1e-5).then_inc(const, 1)
                p.memset(eps[:, 1:2], 1e-6).then_inc(const, 1)
                p.iota(ioti[:], [[1, GBIN]], base=0, channel_multiplier=0).then_inc(pool, 1)
                p.iota(blk[:, 0:1], [[1, 1]], base=0, channel_multiplier=1).then_inc(pool, 1)
                p.iota(blk[:, 1:2], [[1, 1]], base=0, channel_multiplier=205).then_inc(pool, 1)
                p.memset(t["key"][:, NT:], -1.0).then_inc(pool, 1)
                p.memset(t["loc"][:, NT:], -1.0).then_inc(pool, 1)
                p.memset(t["src"][:, NT:], 0)
                p.wait_ge(pool, 10)
                p.affine_select(out=t["ident"][:], in_=t["ident"][:], compare_op=ALU.not_equal, fill=1.0,
                                base=0, pattern=[[-1, 128]], channel_multiplier=1).then_inc(pool, 1)
                p.wait_ge(dve, 3)
                for k in range(4):
                    p.indirect_dma_start(out=rows[:, k, :], out_offset=None,
                                         in_=edges.rearrange("a (t e) -> (a t) e", e=128),
                                         in_offset=bass.IndirectOffsetOnAxis(ap=rowi[:, k:k + 1], axis=0)
                                         ).then_inc(rload, 16)
                p.wait_ge(sload, 48)
                with p.Fori(0, NBT) as i:
                    window(p, HB + WPB * i, WPB, wpool)

            @block.scalar
            def _(s):
                def load_bases(h):
                    s.dma_start(bases[0:KB, h % 3],
                                a[f"{names[h // 2]}_bases"].rearrange("b (i c) o -> (b i) c o", i=S)
                                [:, (h % 2) * NH:(h % 2 + 1) * NH]).then_inc(lb[h % 3], 16)

                def load_back(r):
                    s.dma_start(wst(r), t["wdr"][r].rearrange("(k p) o -> p k o", p=128)).then_inc(lw[r % NWS], 16)

                for e, n in enumerate(names):
                    s.dma_start(comb[:, e, :], a[f"{n}_comb"].rearrange("r b -> b r"),
                                allow_slow_non_contiguous=True).then_inc(lc, 16)
                for h in range(3):
                    load_bases(h)

                def weights(m):
                    s.wait_ge(product, m + 1)
                    if m % 8 == 0 and m // 8 in (1, 2, 3):
                        load_bases(m // 8 + 2)
                    if m % 4 == 0 and m >= 8:
                        s.wait_ge(stw[(m // 4) % 2], 16 * ((m // 4) // 2))
                    s.activation(res[:, (m // 4) % 2, m % 4, :], ps[1 + m % 3][0:KB, :], ACT.Copy).then_inc(copied, 1)
                    if m % 4 == 3:
                        k = m // 4
                        e, cc = k // 4, k % 4
                        s.wait_ge(copied, m + 1)
                        s.dma_start(t["wdr"].rearrange("r (i c) o -> (r i) c o", i=S)[:, cc * 8:(cc + 1) * 8, e * D:(e + 1) * D],
                                    res[:, k % 2].rearrange("p a (c o) -> p (a c) o", c=2)).then_inc(stw[k % 2], 16)

                for m in between(-1):
                    weights(m)
                s.wait_ge(const, 3)

                def step(i, k, lap):
                    if has(i):
                        s.wait_ge(moments, i + 1)
                        s.activation(rstd[:, k % 2], mv[:, k % 2, :, 1:2], ACT.Sqrt, bias=eps[:, 0:1]).then_inc(rdev, 1)
                    if has(i - 2):
                        s.wait_ge(centred, i - 1)
                        s.activation(sq(k), sub(k), ACT.Square).then_inc(squared, 1)
                        s.wait_ge(var_ready, i - 1)
                        s.activation(std(k), ps[6 + k % 2][0:GN, :].rearrange("p (g d) -> p g d", g=PG),
                                     ACT.Sqrt, bias=eps[:, 1:2]).then_inc(gdev, 1)
                    if has(i - 3):
                        s.wait_ge(normed, i - 2)
                        s.wait_ge(st[(k + 1) % XR], 16 * (lap + k // 3))
                        s.activation(hl[:, (k + 1) % XR, :, 0, :], nrm[:, (k + 1) % 2], ACT.Copy, scale=SA).then_inc(high, 1)

                for i in range(NBT + XR):
                    step(i, i % XR, i // XR)
                    for m in between(i):
                        weights(m)
                    if i == 15:
                        for k in range(2):
                            s.wait_ge(stw[k], 16 * 6)
                        for r in range(NWS):
                            load_back(r)
                for r in range(R):
                    s.wait_ge(lw[r % NWS], 16 * (r // NWS + 1))
                    if r >= NWS // 2 and r - NWS // 2 + NWS < R:
                        s.wait_ge(wlo, r - NWS // 2 + 1)
                        load_back(r - NWS // 2 + NWS)
                    s.activation(w[:, r, :, 0, :], wst(r), ACT.Copy, scale=SW).then_inc(whi, 1)

            @block.vector
            def _(v):
                v.wait_ge(loads, 48)
                v.tensor_copy(firstf[:], first).then_inc(dve, 1)
                v.wait_ge(same_ready, 4)
                v.reduce_sum(same8[:], same[:].rearrange("p b i -> p i b"), X).then_inc(kdve, 1)
                v.wait_ge(pool, 5)
                v.tensor_copy(bound[:], boundi[:]).then_inc(dve, 1)
                v.wait_ge(dve, 2)
                for k in range(4):
                    i = v.tensor_scalar(junk[:, k, :], firstb[0:HB, :], bound[:, k:k + 1], 0.0,
                                        ALU.is_lt, ALU.add, accum_out=cnt[:, k:k + 1])
                i.then_inc(cnt_ready, 1)
                v.wait_ge(cnt_ready, 1)
                v.tensor_scalar(rowf[:], cnt[:], -1.0, 0.0, ALU.add, ALU.max)
                v.tensor_scalar(rowi[:], cnt[:], -1.0, 0.0, ALU.add, ALU.max).then_inc(dve, 1)
                v.wait_ge(kdve, 1)
                v.wait_ge(repeated, 1)
                for e in range(3):
                    v.tensor_tensor(kron[:, e], ps[1][0:KB, e * R:(e + 1) * R].unsqueeze(2).broadcast_to([KB, R, S]),
                                    same8[:].unsqueeze(1).broadcast_to([KB, R, S]), ALU.mult).then_inc(kdve, 1)
                v.wait_ge(rload, 64)
                v.tensor_copy(rowsf[:], rows).then_inc(dve, 1)
                v.wait_ge(dve, 4)
                for k in range(4):
                    i = v.tensor_scalar(junk2[:, k, :], rowsf[:, k, :], bound[:, k:k + 1], 0.0,
                                        ALU.is_lt, ALU.add, accum_out=cnt2[:, k:k + 1])
                i.then_inc(dve, 1)
                v.wait_ge(dve, 5)
                v.scalar_tensor_tensor(start[:], rowf[:], 128.0, cnt2[:], ALU.mult, ALU.add)
                v.scalar_tensor_tensor(starti[:], rowf[:, 0:2], 128.0, cnt2[:, 0:2], ALU.mult, ALU.add).then_inc(dve, 1)
                v.wait_ge(dve, 6)
                v.scalar_tensor_tensor(over[0:HB, 0:2], start[:, 2:4], float(-WIN), start[:, 0:2], ALU.add, ALU.subtract).then_inc(dve, 1)
                v.wait_ge(dve, 7)
                v.tensor_scalar(over[0:HB, 2:4], over[0:HB, 0:2], 0.0, 0.0, ALU.is_gt, ALU.max).then_inc(dve, 1)
                v.tensor_tensor(down[:], dl[:, 0, :], dl[:, 1, :], ALU.is_gt).then_inc(dve, 1)
                v.wait_ge(pool, 11)
                v.wait_ge(dve, 9)
                v.reduce_max(bad[0:GN, :], down[:], X).then_inc(dve, 1)
                v.wait_ge(dve, 10)
                v.tensor_tensor(bad[0:HB, :], bad[0:HB, :], over[0:HB, 2:3], ALU.max).then_inc(dve, 1)
                v.wait_ge(dve, 11)
                v.tensor_tensor(bad[0:HB, :], bad[0:HB, :], over[0:HB, 3:4], ALU.max).then_inc(dve, 1)
                v.tensor_copy(t["iota"][:], ioti[:])
                v.tensor_copy(t["ident16"][:], t["ident"][:])
                v.tensor_single_scalar(blk[:, 2:3], blk[:, 0:1], 2, ALU.arith_shift_right)
                v.tensor_single_scalar(blk[:, 3:4], blk[:, 1:2], 12, ALU.arith_shift_right).then_inc(dve, 1)
                v.wait_ge(dve, 13)
                v.tensor_copy(blkf[:], blk[:]).then_inc(dve, 1)
                v.wait_ge(dve, 14)
                v.tensor_single_scalar(off[:, 0:1], blkf[:, 2:3], float(-BN), ALU.mult)
                v.tensor_single_scalar(off[:, 1:2], blkf[:, 3:4], float(-GN), ALU.mult).then_inc(dve, 1)
                v.wait_ge(dve, 15)
                v.scalar_tensor_tensor(off[:, 1:2], blkf[:, 2:3], float(BN), off[:, 1:2], ALU.mult, ALU.add).then_inc(dve, 1)
                v.wait_ge(lp, 48)
                v.sem_inc(low)

                def step(i, k, lap):
                    o = (k + 1) % 2
                    if has(i):
                        v.wait_ge(lx[k], 16 * (lap + 1))
                        for g in range(PG):
                            m = v.bn_stats(st6[:, k % 2, g, :], x[:, k, g, :])
                        m.then_inc(stats, 1)
                        v.wait_ge(stats, i + 1)
                        v.sem_inc(nticks)
                        for g in range(PG):
                            m = v.bn_aggr(mv[:, k % 2, g, :], st6[:, k % 2, g, :])
                        m.then_inc(moments, 1)
                    if has(i - 1):
                        v.wait_ge(rdev, i)
                        v.reciprocal(rinv[:, o], rstd[:, o]).then_inc(rinv_ready, 1)
                        v.wait_ge(rinv_ready, i)
                        for g in range(PG):
                            m = v.tensor_scalar(y(k + 1)[:, g, :], x[:, (k + 3) % XR, g, :], mv[:, o, g, 0:1], rinv[:, o, g, :],
                                                ALU.subtract, ALU.mult)
                        m.then_inc(y_ready, 1)
                    if has(i - 2):
                        v.wait_ge(mean_ready, i - 1)
                        v.tensor_tensor(u(k), ps[4 + k % 2][0:GN, :].rearrange("p (g d) -> p g d", g=PG), gp(0), ALU.mult
                                        ).then_inc(mean_scaled, 1)
                        v.wait_ge(mean_scaled, i - 1)
                        v.tensor_tensor(sub(k), y(k), u(k), ALU.subtract).then_inc(centred, 1)
                    if has(i - 3):
                        n = nrm[:, o]
                        if not isinstance(i, int) or i > 3:
                            v.wait_ge(low, i - 3)
                        v.tensor_tensor(n, sub(k + 1), gp(1), ALU.mult).then_inc(weighted, 1)
                        v.wait_ge(gdev, i - 2)
                        v.reciprocal(std(k + 1), std(k + 1)).then_inc(inverted, 1)
                        v.wait_ge(weighted, i - 2)
                        v.wait_ge(inverted, i - 2)
                        v.tensor_tensor(n, n, std(k + 1), ALU.mult).then_inc(divided, 1)
                        v.wait_ge(divided, i - 2)
                        v.tensor_tensor(n, n, gp(2), ALU.add).then_inc(normed, 1)
                    if has(i - 4):
                        v.wait_ge(high, i - 3)
                        v.scalar_tensor_tensor(hl[:, k, :, 1, :], nrm[:, k % 2], SA, hl[:, k, :, 0, :],
                                               ALU.mult, ALU.subtract).then_inc(low, 1)

                batches(v, step)
                v.wait_ge(marked, 1)
                v.tensor_copy(t["flag"][:], ps[0][0:1, 0:1]).then_inc(dve, 1)
                for r in range(R):
                    v.wait_ge(whi, r + 1)
                    v.scalar_tensor_tensor(w[:, r, :, 1, :], wst(r), SW, w[:, r, :, 0, :],
                                           ALU.mult, ALU.subtract).then_inc(wlo, 1)
                v.wait_ge(tload, 16 * GRP)
                v.tensor_copy(tf, tl).then_inc(dve, 1)
                v.wait_ge(dve, 18)
                for g in range(GRP):
                    i = v.tensor_scalar(tf[:, g, DST, :], tf[:, g, DST, :], off[:, 0:1], float(-BN * (TPG // TPB) * g), ALU.add, ALU.add)
                i.then_inc(dve, 1)
                v.wait_ge(dve, 19)
                v.scalar_tensor_tensor(tf[:, :, TYP, :], tf[:, :, DST, :], float(R), tf[:, :, TYP, :], ALU.mult, ALU.add)
                v.tensor_scalar(far, tf[:, :, DST, :], float(BN), float(FAR), ALU.is_ge, ALU.mult).then_inc(dve, 1)
                v.wait_ge(dve, 20)
                v.scalar_tensor_tensor(tf[:, :, DST, :], tf[:, :, DST, :], off[:, 1:2], far, ALU.add, ALU.add).then_inc(dve, 1)
                for g in range(GRP):
                    v.wait_ge(turned, 1 + g)
                    bank = ps[g % 2]
                    cols = slice(g * TPG, (g + 1) * TPG)
                    v.tensor_copy(t["src"][:, cols], bank[:, 128:128 + TPG])
                    v.tensor_copy(t["loc"][:, cols], bank[:, 0:TPG])
                    v.tensor_copy(t["key"][:, cols], bank[:, 256:256 + TPG]).then_inc(cols_out, 1)

            @block.tensor
            def _(e):
                e.wait_ge(lc, 16 * 3)
                e.wait_ge(same_ready, 4)
                e.matmul(ps[1][0:KB, 0:3 * R], rep[:].rearrange("p b i -> p (b i)"),
                         comb[:].rearrange("p e r -> p (e r)"), start=True, stop=True).then_inc(repeated, 1)
                e.wait_ge(kdve, 4)

                def weights(m):
                    h, cc = m // 8, m % 8
                    if cc == 0:
                        e.wait_ge(lb[h % 3], 16 * (h // 3 + 1))
                    if m >= 3:
                        e.wait_ge(copied, m - 2)
                    e.matmul(ps[1 + m % 3][0:KB, :], kron[:, m // 16].rearrange("p r i -> p (r i)"),
                             bases[0:KB, h % 3, 2 * cc:2 * cc + 2, :].rearrange("p c o -> p (c o)"),
                             start=True, stop=True).then_inc(product, 1)

                for m in between(-1):
                    weights(m)
                e.wait_ge(dve, 12)
                e.matmul(ps[0][0:1, 0:1], bad[:], ones[:], start=True, stop=True).then_inc(marked, 1)
                e.wait_ge(const, 3)

                def step(i, k, lap):
                    if has(i - 1):
                        e.wait_ge(y_ready, i)
                        e.matmul(ps[4 + (k + 1) % 2][0:GN, :], mean1[:], y(k + 1).rearrange("p g d -> p (g d)"),
                                 start=True, stop=True).then_inc(mean_ready, 1)
                    if has(i - 2):
                        e.wait_ge(squared, i - 1)
                        e.matmul(ps[6 + k % 2][0:GN, :], mean1[:], sq(k).rearrange("p g d -> p (g d)"),
                                 start=True, stop=True).then_inc(var_ready, 1)

                for i in range(NBT + XR):
                    step(i, i % XR, i // XR)
                    for m in between(i):
                        weights(m)
                e.wait_ge(pool, 11)
                e.wait_ge(dve, 21)
                for g in range(GRP):
                    if g >= 2:
                        e.wait_ge(cols_out, g - 1)
                    for k in range(3):
                        m = e.transpose(ps[g % 2][:, 128 * k:128 * k + TPG], tf[:, g, k, :],
                                        t["ident"][0:TPG, 0:TPG])
                    m.then_inc(turned, 1)


def conv_fast(nc, ps, a, t):
    STEP = 2
    BB = STEP * BPG
    W3 = 3 * D
    HC = W3 // 2
    with ExitStack() as c:
        sb = lambda n, s, d: c.enter_context(nc.sbuf_tensor(n, s, d))
        sem = lambda n: c.enter_context(nc.semaphore(n))
        w = t["w"]
        bias = sb("qkv_bias", [GN, W3], F32)
        rows = [sb(f"rows{k}", [128, TPB, 2 * D], F16) for k in range(BPG)]
        stage = [sb(f"src_stage{k}", [128, BPG * TPB], I32) for k in range(2)]
        hot = [sb(f"hot{k}", [128, TPB, NBIN], F16) for k in range(2)]
        agg = [sb(f"agg{k}", [128, 2, KC, R, GN], F16) for k in range(2)]
        qkv = [sb(f"qkv{k}", [GN, W3], F32) for k in range(2)]
        kvo = [sb(f"kvo{k}", [GN, 2 * D], F32) for k in range(2)]

        lb = sem("bias_loaded")
        gathered = [sem(f"gathered{k}") for k in range(BPG)]
        stored, kvo_free = sem("kv_stored"), sem("kv_rows_free")
        staged, hot_ready, sum_ready, hi_done, lo_done, conv_ready, biased, q_high, kv_ready = (sem(n) for n in (
            "staged", "hot_ready", "sum_ready", "sums_high", "sums_low", "conv_ready", "biased", "q_high", "kv_ready"))
        C_SUM, C_RING = BPG, 2
        ticks = sem("ticks")
        sums = [ps[0], ps[1]]
        cps = [(ps[2], ps[3]), (ps[4], ps[5])]

        with nc.Block() as block:
            @block.sync
            def _(sp):
                sp.sem_inc(kvo_free, C_RING)
                for k, n in enumerate(("q", "k", "v")):
                    sp.dma_start(bias[:, k * D:(k + 1) * D], row(a[f"{n}_bias"], GN)).then_inc(lb, 16)
                with sp.Fori(0, NG // STEP) as i:
                    for g in range(STEP):
                        sp.wait_ge(kv_ready, STEP * i + g + 1 + C_RING)
                        sp.dma_start(t["kv"][bass.ds((STEP * i + g) * GN, GN), :], kvo[g][:]).then_inc(stored, 16)
                        sp.wait_ge(stored, 16 * (STEP * i + g + 1))
                        sp.sem_inc(kvo_free)

            @block.gpsimd
            def _(p):
                def gather(i, b):
                    q = b // BPG
                    if b % BPG == 0:
                        p.wait_ge(staged, STEP * i + q + 1)
                    p.wait_ge(sum_ready, BB * i + b + 1)
                    p.sem_inc(ticks)
                    for k in range(TPB):
                        p.indirect_dma_start(
                            out=rows[b % BPG][:, k, :], out_offset=None, in_=t["tab"],
                            in_offset=bass.IndirectOffsetOnAxis(
                                ap=stage[q % 2][:, (b % BPG) * TPB + k:(b % BPG) * TPB + k + 1], axis=0)
                        ).then_inc(gathered[b % BPG], 16)

                gather(0, 0)
                with p.Fori(0, NG // STEP) as i:
                    for b in range(1, BB + 1):
                        gather(i, b)

            @block.scalar
            def _(s):
                def put_stage(i, h):
                    s.activation(stage[h][:], t["src"][:, bass.ds((STEP * i + h) * BPG * TPB, BPG * TPB)],
                                 ACT.Copy).then_inc(staged, 1)

                def high(i, b):
                    q = b // BPG
                    s.wait_ge(sum_ready, BB * i + b + 1 + C_SUM)
                    if b % BPG == 0:
                        s.wait_ge(conv_ready, STEP * i + q + 1)
                    s.activation(block_of(agg[q % 2], 0, b % BPG), block_sums(sums[b % 2]), ACT.Copy).then_inc(hi_done, 1)

                s.sem_inc(kv_ready, C_RING)
                for h in range(STEP):
                    put_stage(0, h)
                high(0, 0)
                with s.Fori(0, NG // STEP) as i:
                    for g in range(STEP):
                        for b in range(g * BPG + 1, (g + 1) * BPG + 1):
                            high(i, b)
                            if b % BPG == BPG - 1:
                                put_stage(i + 1, g)
                        s.wait_ge(biased, STEP * i + g + 1 + C_RING)
                        s.activation(q_part(t, STEP * i + g, 0), qkv[g][:, 0:D], ACT.Relu).then_inc(q_high, 1)
                        s.wait_ge(kvo_free, STEP * i + g + 1)
                        s.activation(kvo[g][:], qkv[g][:, D:W3], ACT.Relu).then_inc(kv_ready, 1)

            @block.vector
            def _(v):
                def make_hot(i, b):
                    v.wait_ge(sum_ready, BB * i + b - 1 + C_SUM)
                    for k in range(TPB):
                        m = v.tensor_scalar(hot[b % 2][:, k, :], t["iota"][:, 0:NBIN],
                                            t["key"][:, bass.ds((BB * i + b) * TPB + k, 1)], None, ALU.is_equal)
                    m.then_inc(hot_ready, 1)

                def low(i, b):
                    q = b // BPG
                    v.wait_ge(hi_done, BB * i + b + 1)
                    v.tensor_tensor(block_of(agg[q % 2], 1, b % BPG), block_sums(sums[b % 2]),
                                    block_of(agg[q % 2], 0, b % BPG), ALU.subtract).then_inc(lo_done, 1)

                v.sem_inc(lo_done, C_RING)
                v.sem_inc(biased, C_RING)
                v.wait_ge(lb, 48)
                make_hot(0, 0)
                make_hot(0, 1)
                low(0, 0)
                with v.Fori(0, NG // STEP) as i:
                    for g in range(STEP):
                        for b in range(g * BPG + 1, (g + 1) * BPG + 1):
                            make_hot(i, b + 1)
                            low(i, b)
                        v.wait_ge(conv_ready, STEP * i + g + 1 + C_RING)
                        v.wait_ge(kv_ready, STEP * i + g + 1)
                        for h in range(2):
                            m = v.scalar_tensor_tensor(qkv[g][:, h * HC:(h + 1) * HC], cps[g][h][0:GN, 0:HC], DESC,
                                                       bias[:, h * HC:(h + 1) * HC], ALU.mult, ALU.add)
                        m.then_inc(biased, 1)
                        v.wait_ge(q_high, STEP * i + g + 1)
                        v.wait_ge(biased, STEP * i + g + 1 + C_RING)
                        m = v.scalar_tensor_tensor(q_part(t, STEP * i + g, 1), qkv[g][:, 0:D], 0.0,
                                                   q_part(t, STEP * i + g, 0), ALU.max, ALU.subtract)

            @block.tensor
            def _(e):
                def sum_block(i, b):
                    q = b // BPG
                    e.wait_ge(gathered[b % BPG], 16 * TPB * (STEP * i + q + 1))
                    e.wait_ge(hot_ready, BB * i + b + 1)
                    e.wait_ge(lo_done, BB * i + b + 1)
                    for kc in range(KC):
                        for k in range(TPB):
                            for part in range(2):
                                m = e.matmul(sums[b % 2][:, kc * NBIN:(kc + 1) * NBIN],
                                             rows[b % BPG][:, k, part * D + kc * 128:part * D + (kc + 1) * 128],
                                             hot[b % 2][:, k, :], start=(k == 0 and part == 0),
                                             stop=(k == TPB - 1 and part == 1))
                    m.then_inc(sum_ready, 1)

                e.sem_inc(sum_ready, C_SUM)
                e.sem_inc(conv_ready, C_RING)
                sum_block(0, 0)
                with e.Fori(0, NG // STEP) as i:
                    for g in range(STEP):
                        for b in range(g * BPG + 1, (g + 1) * BPG + 1):
                            sum_block(i, b)
                        e.wait_ge(lo_done, BB * i + (g + 1) * BPG + C_RING)
                        e.wait_ge(biased, STEP * i + g + 1)
                        conv_product(e, agg[g], w, cps[g], HC).then_inc(conv_ready, 1)


def q_part(t, graph, part):
    return t["q"][:, bass.ds(graph, 1), part, :].rearrange("p o d -> p (o d)")


def block_sums(bank):
    return bank[:, 0:KC * NBIN].rearrange("p (c n r) -> p c r n", c=KC, r=R)


def block_of(agg, part, b):
    return agg[:, part, :, :, b * BN:(b + 1) * BN]


def conv_product(e, agg, w, banks, hc):
    for h in range(2):
        n = 0
        for r in range(R):
            for kc in range(KC):
                for pa, pw in ((0, 0), (0, 1), (1, 0)):
                    m = e.matmul(banks[h][0:GN, 0:hc], agg[:, pa, kc, r, :], w[:, r, kc, pw, h * hc:(h + 1) * hc],
                                 start=(n == 0), stop=(n == R * KC * 3 - 1))
                    n += 1
    return m

def list_columns(nc, ps, a, t):
    TPG, GRP = 100, 7
    with ExitStack() as c:
        sb = lambda n, s, d: c.enter_context(nc.sbuf_tensor(n, s, d))
        sem = lambda n: c.enter_context(nc.semaphore(n))
        tl = sb("list_tiles", [TPG, GRP, 3, 128], I32)
        tf = sb("list_tiles_f", [TPG, GRP, 3, 128], F32)
        load, dve, pe = (sem(n) for n in ("list_tiles_loaded", "columns_done", "list_turned"))
        with nc.Block() as block:
            @block.sync
            def _(sp):
                for g in range(GRP):
                    sp.dma_start(tl[:, g], a["edges"][:, g * TPG * 128:(g + 1) * TPG * 128]
                                 .rearrange("a (p e) -> p a e", e=128)).then_inc(load, 16)

            @block.vector
            def _(v):
                v.wait_ge(load, 16 * GRP)
                v.tensor_copy(tf[:], tl[:]).then_inc(dve, 1)
                v.wait_ge(dve, 1)
                v.scalar_tensor_tensor(tf[:, :, TYP, :], tf[:, :, DST, :], float(R), tf[:, :, TYP, :],
                                       ALU.mult, ALU.add).then_inc(dve, 1)
                for g in range(GRP):
                    v.wait_ge(pe, 1 + g)
                    cols = slice(g * TPG, (g + 1) * TPG)
                    v.tensor_copy(t["loc"][:, cols], ps[g % 2][:, 0:TPG])
                    v.tensor_copy(t["src"][:, cols], ps[g % 2][:, 128:128 + TPG])
                    v.tensor_copy(t["key"][:, cols], ps[g % 2][:, 256:256 + TPG]).then_inc(dve, 1)

            @block.tensor
            def _(e):
                for g in range(GRP):
                    e.wait_ge(dve, max(2, g + 1))
                    for k in range(3):
                        m = e.transpose(ps[g % 2][:, 128 * k:128 * k + TPG], tf[:, g, k, :], t["ident"][0:TPG, 0:TPG])
                    m.then_inc(pe, 1)


def conv_general(nc, ps, a, t):
    W3 = 3 * D
    HC = W3 // 2
    C = NCH
    with ExitStack() as c:
        sb = lambda n, s, d: c.enter_context(nc.sbuf_tensor(n, s, d))
        sem = lambda n: c.enter_context(nc.semaphore(n))
        w = t["w"]
        bias = sb("g_qkv_bias", [GN, W3], F32)
        rows = sb("g_rows", [128, TPB, 2 * D], F16)
        stage = sb("g_stage", [128, TPB], I32)
        hot = sb("g_hot", [128, TPB, GBIN], F16)
        zero = sb("g_zero", [128, 512], F16)
        agg = sb("g_agg", [128, 2, KC, R, GN], F16)
        qkv = sb("g_qkv", [GN, W3], F32)
        kvo = sb("g_kvo", [GN, 2 * D], F32)
        ticks = sem("g_ticks")
        lb, zeroed, gathered, hot_ready, summed, opened, hi_done, lo_done, conv_ready, biased, act_ready, shifted, stored = (
            sem("g_" + n) for n in ("bias_loaded", "zeroed", "gathered", "hot_ready", "summed", "opened",
                                    "hi_done", "lo_done", "conv_ready", "biased", "act_ready", "shifted", "stored"))
        kvo_free = sem("g_kvo_free")
        with nc.Block() as block:
            @block.sync
            def _(sp):
                sp.sem_inc(kvo_free)
                for k, n in enumerate(("q", "k", "v")):
                    sp.dma_start(bias[:, k * D:(k + 1) * D], row(a[f"{n}_bias"], GN)).then_inc(lb, 16)
                with sp.Fori(0, NG) as g:
                    sp.wait_ge(act_ready, g + 1)
                    sp.dma_start(t["kv"][bass.ds(g * GN, GN), :], kvo[:]).then_inc(stored, 16)
                    sp.wait_ge(stored, 16 * (g + 1))
                    sp.sem_inc(kvo_free)

            @block.gpsimd
            def _(p):
                p.memset(zero[:], 0.0).then_inc(zeroed, 1)
                with p.Fori(0, NG) as g:
                    with p.Fori(0, C) as i:
                        p.wait_ge(hot_ready, g * C + i + 1)
                        p.sem_inc(ticks)
                        for k in range(TPB):
                            p.indirect_dma_start(out=rows[:, k, :], out_offset=None, in_=t["tab"],
                                                 in_offset=bass.IndirectOffsetOnAxis(ap=stage[:, k:k + 1], axis=0)
                                                 ).then_inc(gathered, 16)

            @block.vector
            def _(v):
                v.sem_inc(lo_done)
                v.sem_inc(biased)
                v.wait_ge(lb, 48)
                with v.Fori(0, NG) as g:
                    with v.Fori(0, C) as i:
                        v.wait_ge(summed, g * C + i + 1)
                        v.tensor_copy(stage[:], t["src"][:, bass.ds(i * TPB, TPB)])
                        for k in range(TPB):
                            m = v.tensor_scalar(hot[:, k, :], t["iota"][:], t["key"][:, bass.ds(i * TPB + k, 1)],
                                                None, ALU.is_equal)
                        m.then_inc(hot_ready, 1)
                    v.wait_ge(hot_ready, g * C + C)
                    v.tensor_scalar(t["key"][:, 0:NCH * TPB], t["key"][:, 0:NCH * TPB], float(-GBIN), None, ALU.add).then_inc(shifted, 1)
                    v.wait_ge(shifted, g + 1)
                    for b in range(BPG):
                        v.wait_ge(hi_done, BPG * g + b + 1)
                        v.tensor_tensor(block_of(agg, 1, b), block_sums(ps[b]), block_of(agg, 0, b), ALU.subtract).then_inc(lo_done, 1)
                    v.wait_ge(conv_ready, g + 2)
                    for h in range(2):
                        m = v.scalar_tensor_tensor(qkv[:, h * HC:(h + 1) * HC], ps[5 + h][0:GN, 0:HC], DESC,
                                                   bias[:, h * HC:(h + 1) * HC], ALU.mult, ALU.add)
                    m.then_inc(biased, 1)
                    v.wait_ge(act_ready, g + 1)
                    v.wait_ge(biased, 2 * g + 2)
                    v.scalar_tensor_tensor(q_part(t, g, 1), qkv[:, 0:D], 0.0, q_part(t, g, 0), ALU.max, ALU.subtract).then_inc(biased, 1)

            @block.scalar
            def _(s):
                with s.Fori(0, NG) as g:
                    s.wait_ge(summed, g * C + C + 1)
                    s.wait_ge(conv_ready, g + 1)
                    for b in range(BPG):
                        s.activation(block_of(agg, 0, b), block_sums(ps[b]), ACT.Copy).then_inc(hi_done, 1)
                    s.wait_ge(biased, 2 * g + 2)
                    s.wait_ge(kvo_free, g + 1)
                    s.activation(q_part(t, g, 0), qkv[:, 0:D], ACT.Relu)
                    s.activation(kvo[:], qkv[:, D:W3], ACT.Relu).then_inc(act_ready, 1)

            @block.tensor
            def _(e):
                e.sem_inc(summed)
                e.sem_inc(conv_ready)
                e.wait_ge(zeroed, 1)
                with e.Fori(0, NG) as g:
                    e.wait_ge(lo_done, BPG * g + 1)
                    for b in range(BPG):
                        e.matmul(ps[b][:, 0:KC * NBIN], zero[:, 0:128], zero[:, 0:KC * NBIN], start=True, stop=False,
                                 skip_group_check=True)
                    with e.Fori(0, C) as i:
                        e.wait_ge(gathered, (g * C + i + 1) * 16 * TPB)
                        e.wait_ge(hot_ready, g * C + i + 1)
                        for b in range(BPG):
                            for kc in range(KC):
                                for k in range(TPB):
                                    for part in range(2):
                                        m = e.matmul(ps[b][:, kc * NBIN:(kc + 1) * NBIN],
                                                     rows[:, k, part * D + kc * 128:part * D + (kc + 1) * 128],
                                                     hot[:, k, b * NBIN:(b + 1) * NBIN], start=False,
                                                     stop=(part == 1 and k == TPB - 1), skip_group_check=True)
                        m.then_inc(summed, 1)
                    e.wait_ge(lo_done, BPG * g + BPG + 1)
                    e.wait_ge(biased, 2 * g + 1)
                    conv_product(e, agg, w, (ps[5], ps[6]), HC).then_inc(conv_ready, 1)


def attend_edges_general(nc, ps, a, t):
    C = NCH
    with ExitStack() as c:
        sb = lambda n, s, d: c.enter_context(nc.sbuf_tensor(n, s, d))
        sem = lambda n: c.enter_context(nc.semaphore(n))
        kv = sb("ge_kv", [128, TPB, 2 * D], F32)
        stage = sb("ge_stage", [128, TPB], I32)
        hot = sb("ge_hot", [128, TPB, GN], F32)
        hotT = sb("ge_hotT", [GN, TPB, 128], F16)
        prod = sb("ge_prod", [128, TPB, D], F32)
        raw = sb("ge_raw", [128, TPB, H], F32)
        clip = sb("ge_clip", [128, TPB, H], F32)
        sv = sb("ge_sv", [128, TPB, D + H], F32)
        zero = sb("ge_zero", [128, D + H], F32)
        zinv = sb("ge_zinv", [GN, 2, H], F32)
        rows = sb("ge_rows", [GN, D], F32)
        ticks = sem("ge_ticks")
        gathered, hot_ready, turned, ht_ready, q_ready, dve, exp_ready, sv_ready, summed, norm, stored, zeroed = (
            sem("ge_" + n) for n in ("gathered", "hot_ready", "turned", "hotT_ready", "q_ready", "scores", "exp_ready",
                                     "weighted", "summed", "normalised", "stored", "zeroed"))
        rows_free = sem("ge_rows_free")
        with nc.Block() as block:
            @block.sync
            def _(sp):
                sp.sem_inc(rows_free)
                with sp.Fori(0, NG) as g:
                    sp.wait_ge(norm, 4 * g + 5)
                    sp.dma_start(t["attn"][bass.ds(g * GN, GN), :], rows[:]).then_inc(stored, 16)
                    sp.wait_ge(stored, 16 * (g + 1))
                    sp.sem_inc(rows_free)

            @block.gpsimd
            def _(p):
                p.memset(zero[:], 0.0).then_inc(zeroed, 1)
                with p.Fori(0, NG) as g:
                    with p.Fori(0, C) as i:
                        p.wait_ge(hot_ready, g * C + i + 1)
                        p.sem_inc(ticks)
                        for k in range(TPB):
                            p.indirect_dma_start(out=kv[:, k, :], out_offset=None, in_=t["kv"],
                                                 in_offset=bass.IndirectOffsetOnAxis(ap=stage[:, k:k + 1], axis=0)
                                                 ).then_inc(gathered, 16)

            @block.vector
            def _(v):
                v.sem_inc(norm)
                with v.Fori(0, NG) as g:
                    with v.Fori(0, C) as i:
                        n = g * C + i
                        v.wait_ge(summed, n + 1)
                        v.tensor_copy(stage[:], t["src"][:, bass.ds(i * TPB, TPB)])
                        for k in range(TPB):
                            m = v.tensor_scalar(hot[:, k, :], t["iota"][:, 0:GN], t["loc"][:, bass.ds(i * TPB + k, 1)],
                                                None, ALU.is_equal)
                        m.then_inc(hot_ready, 1)
                        v.wait_ge(q_ready, n + 1)
                        v.wait_ge(gathered, (n + 1) * 16 * TPB)
                        for k in range(2):
                            m = v.tensor_tensor(prod[:, 2 * k:2 * k + 2, :], ps[1 + k].rearrange("p (k d) -> p k d", k=2),
                                                kv[:, 2 * k:2 * k + 2, 0:D], ALU.mult)
                        m.then_inc(dve, 1)
                        v.wait_ge(dve, 3 * n + 1)
                        v.reduce_sum(raw[:].rearrange("p k h -> p (k h)"),
                                     prod[:].rearrange("p k (h d) -> p (k h) d", h=H), X).then_inc(dve, 1)
                        v.wait_ge(dve, 3 * n + 2)
                        v.tensor_scalar(clip[:], raw[:], -10.0 * SQRT_DH, 10.0 * SQRT_DH, ALU.max, ALU.min).then_inc(dve, 1)
                        v.wait_ge(exp_ready, n + 1)
                        v.tensor_tensor(sv[:, :, 0:D].rearrange("p k (h d) -> p k h d", h=H),
                                        kv[:, :, D:].rearrange("p k (h d) -> p k h d", h=H),
                                        sv[:, :, D:].unsqueeze(3).broadcast_to([128, TPB, H, DH]), ALU.mult).then_inc(sv_ready, 1)
                    v.wait_ge(hot_ready, g * C + C)
                    v.tensor_scalar(t["loc"][:, 0:NCH * TPB], t["loc"][:, 0:NCH * TPB], float(-GN), None, ALU.add).then_inc(norm, 1)
                    v.wait_ge(summed, g * C + C + 1)
                    v.tensor_scalar(zinv[:, 0, :], ps[3][0:GN, D:D + H], 1e-6, None, ALU.add).then_inc(norm, 1)
                    v.wait_ge(norm, 4 * g + 3)
                    v.reciprocal(zinv[:, 1, :], zinv[:, 0, :])
                    v.wait_ge(rows_free, g + 1)
                    v.tensor_copy(rows[:], ps[3][0:GN, 0:D]).then_inc(norm, 1)
                    v.wait_ge(norm, 4 * g + 4)
                    v.tensor_tensor(rows[:].rearrange("p (h d) -> p h d", h=H), rows[:].rearrange("p (h d) -> p h d", h=H),
                                    zinv[:, 1, :].unsqueeze(2).broadcast_to([GN, H, DH]), ALU.mult).then_inc(norm, 1)

            @block.scalar
            def _(s):
                with s.Fori(0, NG) as g:
                    with s.Fori(0, C) as i:
                        n = g * C + i
                        s.wait_ge(turned, n + 1)
                        s.activation(hotT[:], ps[0][0:GN, :].rearrange("p (k e) -> p k e", k=TPB), ACT.Copy).then_inc(ht_ready, 1)
                        s.wait_ge(dve, 3 * n + 3)
                        s.activation(sv[:, :, D:], clip[:], ACT.Exp, scale=1.0 / SQRT_DH).then_inc(exp_ready, 1)

            @block.tensor
            def _(e):
                e.sem_inc(summed)
                e.wait_ge(zeroed, 1)
                with e.Fori(0, NG) as g:
                    e.wait_ge(norm, 4 * g + 1)
                    e.matmul(ps[3][0:GN, 0:D + H], zero[:, 0:GN], zero[:], start=True, stop=False, skip_group_check=True)
                    with e.Fori(0, C) as i:
                        n = g * C + i
                        e.wait_ge(hot_ready, n + 1)
                        for k in range(TPB):
                            m = e.transpose(ps[0][0:GN, k * 128:(k + 1) * 128], hot[:, k, :], t["ident"][:])
                        m.then_inc(turned, 1)
                        e.wait_ge(ht_ready, n + 1)
                        for k in range(TPB):
                            for part in range(2):
                                m = e.matmul(ps[1 + k // 2][:, (k % 2) * D:(k % 2 + 1) * D], hotT[:, k, :],
                                             q_part(t, g, part), start=(part == 0), stop=(part == 1))
                        m.then_inc(q_ready, 1)
                        e.wait_ge(sv_ready, n + 1)
                        for k in range(TPB):
                            m = e.matmul(ps[3][0:GN, 0:D + H], hot[:, k, :], sv[:, k, :], start=False, stop=(k == TPB - 1),
                                         skip_group_check=True)
                        m.then_inc(summed, 1)


class Steps:

    def __init__(self, sem, names):
        self.sem, self.names = sem, names

    def at(self, s, name):
        return s * len(self.names) + self.names.index(name) + 2

    def before(self, s):
        return s * len(self.names) + 1


BS = TG * BPG
RK = 5
LEAD = 2
WHEN = {"attnT": 6, "o": 7, "up_0": 9, "up_1": 9, "down": 11, "rowsT": 13, "route": 14, "l1_0": 15,
        "l1_1": 16, "l2_0": 17, "l2_1": 18, "l3_0": 19, "l3_1": 20, "l1_2": 21, "l1_3": 22, "l2_2": 23,
        "l2_3": 24, "l3_2": 25, "l3_3": 26, "l1_4": 27, "l1_5": 28, "l2_4": 29, "l2_5": 30, "l3_4": 31,
        "l3_5": 32, "l1_6": 33, "l1_7": 34, "l2_6": 35, "l2_7": 36, "l3_6": 37, "l3_7": 38}
PRODUCTS = list(WHEN)
EXPERTS = [x for x in PRODUCTS if x[0] == "l"]
ACT_OF = {"attnT": ["attnT_hi"], "o": ["o_out", "gn_std", "gn_hi"], "up_0": ["up_0", "up_0_hi"],
          "up_1": ["up_1", "up_1_hi"], "down": ["ln_std"], "rowsT": ["rowsT_hi"], "route": ["mix_exp"]}
DVE_OF = {"attnT": ["attnT_lo"], "o": ["gn_st", "gn_mv", "gn_a", "gn_b", "gn_c", "gn_d", "gn_e", "gn_f", "gn_g", "gn_h", "gn_out"],
          "up_0": [], "up_1": [], "down": ["x_bias", "x1", "ln_st", "ln_mv", "ln_rstd", "ln_out"],
          "rowsT": ["rowsT_lo"], "route": ["logit", "lmax", "lsub", "lsum", "lrec", "mix", "mix_d"]}
for _x in EXPERTS:
    ACT_OF[_x] = [_x, _x + "_hi"] if _x[:2] != "l3" else []
    DVE_OF[_x] = [] if _x[:2] != "l3" else [_x + "_add"]
POOL_OF = {p: [] for p in PRODUCTS}
POOL_OF.update({"o": ["gn_lo"], "up_0": ["up_0_lo"], "up_1": ["up_1_lo"]})
POOL_OF.update({x: [x + "_lo"] for x in EXPERTS if x[:2] != "l3"})


def prepare_ffn(nc, ps, a, t, k, pre):
    BNS = ("v1", "g1", "be1", "b1", "m1", "v2", "g2", "be2", "b2", "m2")
    SHORT = (("O_b", KC), ("gn2_w", KC), ("gn2_b", KC), ("gn2_ms", KC), ("ffn1_b", FF // 128))
    EK = NX * KC
    NST = 6
    with ExitStack() as c:
        sb = lambda n, s, d: c.enter_context(nc.sbuf_tensor(pre + n, s, d))
        sem = t["shared_sem"]
        stg = sb("weight_stage", [128, NST, 3 * KC * D], F32)
        lines = sb("par_rows", [EK, 15, 128], F32)
        bost = sb("bo_stage", [NX, D], F32)
        bsd = sb("bn_std", [128, 2, EK], F32)
        btm = sb("bn_tmp", [128, 2, EK], F32)
        pieces = []
        for e in range(NX):
            pieces.append(([a[n][e].rearrange("(k p) o -> p k o", p=128) for n in ("W1", "W2", "Wo")], KC * D,
                           lambda part, e=e: k["we"][:, e, :, :, part, :].rearrange("p l k o -> p (l k) o"), 3 * KC, D))
        for n, w, m, o in (("O_w", "wo", KC, D), ("ffn1_w", "w1", KC, FF), ("ffn2_w", "w2", FF // 128, D), ("Wr", "wr", KC, NX)):
            pieces.append(([a[n].rearrange("(k p) o -> p k o", p=128)], m * o, lambda part, w=w: k[w][:, :, part, :], m, o))
        lw = [sem(f"piece_loaded{i}") for i in range(NST)]
        ll, lo_, pool, hi, low, pe, dve, act = (sem(n) for n in (
            "rows_loaded", "others_loaded", "pool_done", "high_done", "low_done", "turned", "dve_done", "act_done"))
        stage = lambda n, m, o: stg[:, n % NST, 0:m * o].rearrange("p (k o) -> p k o", o=o)
        with nc.Block() as block:
            @block.sync
            def _(sp):
                for n, (srcs, width, _, m, o) in enumerate(pieces):
                    if n >= NST:
                        sp.wait_ge(low, n - NST + 1)
                    for j, src in enumerate(srcs):
                        sp.dma_start(stg[:, n % NST, j * width:(j + 1) * width].rearrange("p (k o) -> p k o", o=o), src
                                     ).then_inc(lw[n % NST], 16)

            @block.gpsimd
            def _(p):
                p.memset(lines[:], 0.0).then_inc(pool, 1)
                p.memset(k["epsc"][:, 0:1], 1e-5).then_inc(pool, 1)
                p.memset(k["epsc"][:, 1:2], 1e-6).then_inc(pool, 1)
                p.memset(k["epsc"][:, 2:3], 1e-3).then_inc(pool, 1)

            @block.scalar
            def _(s):
                s.wait_ge(pool, 4)
                for j, n in enumerate(BNS):
                    s.dma_start(lines[:, j, :], a[n].rearrange("e (k p) -> (e k) p", p=128)).then_inc(ll, 16)
                for j, (n, r) in enumerate(SHORT):
                    s.dma_start(lines[0:r, len(BNS) + j, :], a[n].rearrange("(k p) -> k p", p=128)).then_inc(ll, 16)
                s.dma_start(k["rb"][:, 0:D], row(a["ffn2_b"], GN)).then_inc(lo_, 16)
                s.dma_start(k["rb"][:, D:], row(a["br"], GN)).then_inc(lo_, 16)
                s.dma_start(bost[:], a["bo"]).then_inc(lo_, 16)
                loads = [0] * NST
                for n, (srcs, width, place, m, o) in enumerate(pieces):
                    loads[n % NST] += 16 * len(srcs)
                    s.wait_ge(lw[n % NST], loads[n % NST])
                    s.activation(place(0), stage(n, m, o), ACT.Copy, scale=SW).then_inc(hi, 1)
                s.wait_ge(dve, 1)
                for l in range(2):
                    i = s.activation(bsd[:, l, :], k["par"][:, 5 * l, :], ACT.Sqrt, bias=k["epsc"][:, 2:3])
                i.then_inc(act, 1)
                s.wait_ge(lo_, 48)
                s.activation(k["bo"][:, 0, :], bost[:], ACT.Copy, scale=SW).then_inc(hi, 1)

            @block.vector
            def _(v):
                for n, (srcs, width, place, m, o) in enumerate(pieces):
                    v.wait_ge(hi, n + 1)
                    v.scalar_tensor_tensor(place(1), stage(n, m, o), SW, place(0), ALU.mult, ALU.subtract).then_inc(low, 1)
                v.wait_ge(pe, 1)
                v.tensor_copy(k["par"][:].rearrange("p j r -> p (j r)"), ps[0][:, 0:15 * EK]).then_inc(dve, 1)
                v.wait_ge(act, 1)
                v.reciprocal(btm[:], bsd[:]).then_inc(dve, 1)
                v.wait_ge(dve, 2)
                for l in range(2):
                    v.tensor_tensor(btm[:, l, :], btm[:, l, :], k["par"][:, 5 * l + 1, :], ALU.mult)
                    i = v.tensor_tensor(bsd[:, l, :], k["par"][:, 5 * l + 3, :], k["par"][:, 5 * l + 4, :], ALU.subtract)
                i.then_inc(dve, 1)
                v.wait_ge(dve, 3)
                v.tensor_tensor(bsd[:], bsd[:], btm[:], ALU.mult).then_inc(dve, 1)
                v.wait_ge(dve, 4)
                for l in range(2):
                    i = v.tensor_tensor(bsd[:, l, :], bsd[:, l, :], k["par"][:, 5 * l + 2, :], ALU.add)
                i.then_inc(dve, 1)
                v.wait_ge(dve, 5)
                v.tensor_scalar(k["bsc"][:], btm[:], 1.0 / SW, None, ALU.mult)
                v.tensor_scalar(k["bbi"][:], bsd[:], SA, None, ALU.mult)
                v.tensor_scalar(k["upb"][:], k["par"][:, 14, 0:FF // 128], SA, None, ALU.mult)
                for j, col in enumerate((13, 11, 12)):
                    for g in range(TG):
                        v.tensor_copy(k["gnp"][:, j, :, g], k["par"][:, col, 0:KC])
                v.wait_ge(hi, len(pieces) + 1)
                v.scalar_tensor_tensor(k["bo"][:, 1, :], bost[:], SW, k["bo"][:, 0, :], ALU.mult, ALU.subtract).then_inc(low, 1)
                v.tensor_scalar(k["pick"][:], t["ident"][0:NX, 0:NX].unsqueeze(2).broadcast_to([NX, NX, GN]), SA, None,
                                ALU.mult).then_inc(low, 1)
                v.wait_ge(low, len(pieces) + 2)

            @block.tensor
            def _(e):
                e.wait_ge(ll, 16 * 15)
                for j in range(15):
                    m = e.transpose(ps[0][:, j * EK:(j + 1) * EK], lines[:, j, :], t["ident"][0:EK, 0:EK])
                m.then_inc(pe, 1)


def attend(nc, ps, a, t, out, general=False):
    pre = "general_" if general else ""
    with ExitStack() as c:
        sb = lambda n, s, d: c.enter_context(nc.sbuf_tensor(pre + n, s, d))
        sem = t["shared_sem"]
        place = t["w"][:].rearrange("p r k l o -> p (r k l o)")
        WE, WO, W1 = NX * 3 * KC * 2 * D, KC * 2 * D, KC * 2 * FF
        we = place[:, 0:WE].rearrange("p (e n k l o) -> p e n k l o", e=NX, n=3, k=KC, l=2)
        wo = place[:, WE:WE + WO].rearrange("p (k l o) -> p k l o", k=KC, l=2)
        w1 = place[:, WE + WO:WE + WO + W1].rearrange("p (k l o) -> p k l o", k=KC, l=2)
        w2 = sb("down_w", [128, FF // 128, 2, D], F16)
        wr = sb("router_w", [128, KC, 2, NX], F16)
        bo = sb("bo_parts", [NX, 2, D], F16)
        pick = t["iota"][0:NX, GN:GBIN].rearrange("p (e n) -> p e n", e=NX)
        rb = sb("row_bias", [GN, D + NX], F32)
        par = sb("feature_par", [128, 15, 16], F32)
        bsc = sb("bn_scale", [128, 2, NX * KC], F32)
        bbi = sb("bn_bias", [128, 2, NX * KC], F32)
        gnp = sb("gn2_par", [128, 3, KC, TG], F32)
        upb = sb("up_bias", [128, FF // 128], F32)
        epsc = sb("eps2", [128, 3], F32)
        prepare_ffn(nc, ps, a, t, dict(we=we, wo=wo, w1=w1, w2=w2, wr=wr, bo=bo, pick=pick, rb=rb, par=par, bsc=bsc, bbi=bbi,
                                       gnp=gnp, upb=upb, epsc=epsc), pre)
        kv = [sb(f"kv_rows{k}", [128, TPB, 2 * D], F32) for k in range(RK)]
        stage = [sb(f"kv_stage{k}", [128, BS // 2 * TPB], I32) for k in range(2)]
        hot = [sb(f"hot_node{k}", [128, TPB, GN], F16) for k in range(RK)]
        hotT = [sb(f"hot_nodeT{k}", [GN, TPB, 128], F16) for k in range(2)]
        prod = sb("prod", [128, TPB, D], F32)
        raw = sb("score_raw", [128, TPB, H], F32)
        clip = sb("score_clip", [128, TPB, H], F32)
        ex = [sb(f"weights{k}", [128, TPB, H], F32) for k in range(2)]
        sv = [sb(f"weighted{k}", [128, 2, TPB, D + H], F16) for k in range(2)]
        zinv = sb("zinv", [GN, 2, H], F32)
        attn = sb("attn", [GN, TG, D], F32)
        xt = sb("x_tile", [GN, TG, D], F32)
        actT = sb("actT", [128, 2, KC, TT], F16)
        gnT = sb("gnT", [128, 2, KC, TT], F16)
        wide = sb("wide", [128, 4, TT], F32)
        rows = wide[0:GN].rearrange("p a b -> p (a b)")[:, 0:TG * D].rearrange("p (g d) -> p g d", g=TG)
        parts = sb("parts", [128, 2, 2, KC, TT], F16)
        st = sb("st", [128, 2 * TG, 6], F32)
        mv = sb("mv2", [128, 2 * TG, 2], F32)
        gs = sb("gs", [128, 8, 2 * TG], F32)
        lst = sb("lst", [GN, TG, 6], F32)
        lmv = sb("lmv", [GN, TG, 2], F32)
        lsd = sb("lsd", [GN, 2, TG], F32)
        lg = sb("lg", [GN, 4, TG, NX], F32)
        lred = sb("lred", [GN, 3, TG], F32)
        mixd = sb("mixd", [GN, TG, NX], F32)

        gathered = [sem(f"kv_gathered{k}") for k in range(RK)]
        names = ("staged", "hot_ready", "hotT_sum", "hotT_ready", "q_ready", "prod_ready", "raw_ready", "clip_ready",
                 "exp_ready", "q_copied", "weighted", "weighted_high", "weighted_low", "summed", "z_ready", "attn_ready")
        (staged, hot_ready, t_ready, ht_ready, q_ready, prod_ready, raw_ready, clip_ready, exp_ready, q_copied, weighted, sv_high, sv_ready,
         summed, z_ready, attn_ready) = (sem(n) for n in names)
        x_loaded, stored, ticks = sem("x_loaded"), sem("out_stored"), sem("ticks2")
        PE = Steps(sem("tensor_steps"), PRODUCTS)
        AC = Steps(sem("scalar_steps"), [x for p in PRODUCTS for x in ACT_OF[p]])
        DV = Steps(sem("vector_steps"), [x for p in PRODUCTS for x in DVE_OF[p]])
        PO = Steps(sem("pool_steps"), [x for p in PRODUCTS for x in POOL_OF[p]])
        pT, pQ, pW = ps[0], (ps[1], ps[2]), ps[3]
        bankT = pT[0:GN, :].rearrange("p (k e) -> p k e", k=TPB)
        pair = [t["psum"][:, 4:6, :], t["psum"][:, 6:8, :]]
        PAIR = {"attnT": 0, "o": 1, "up_0": 0, "up_1": 1, "down": 0, "rowsT": 1, "route": 1}
        for x in EXPERTS:
            PAIR[x] = int(x[3:]) % 2
        TAKEN = {"attnT": (DV, "attnT_lo"), "o": (AC, "o_out"), "up_0": (AC, "up_0"), "up_1": (AC, "up_1"),
                 "down": (DV, "x1"), "rowsT": (DV, "rowsT_lo"), "route": (DV, "logit")}
        for x in EXPERTS:
            TAKEN[x] = (DV, x + "_add") if x[:2] == "l3" else (AC, x)
        CW, CQ, CV, CE, CR = RK, 2, RK, 1, 1

        def schedule(eng, s, edges_step, product, late):
            for b in range(BS):
                for half in range(2):
                    if edges_step:
                        edges_step(b, half)
                    if product:
                        for p in PRODUCTS:
                            if WHEN[p] + late == 2 * b + half:
                                product(s, p)

        def stream(eng, edges_step, product, late):
            if general:
                with eng.Fori(0, NS) as i:
                    schedule(eng, i, None, product, late)
                return
            schedule(eng, None, lambda b, h: edges_step(0, b, h), None, late)
            with eng.Fori(0, NS - 1) as i:
                schedule(eng, i, lambda b, h: edges_step(i + 1, b, h), product, late)
            for b in range(3):
                for half in range(2):
                    edges_step(NS, b, half)
            schedule(eng, NS - 1, None, product, late)

        def ago(s, b, d):
            if isinstance(s, int) and (BS * s + b < d or BS * s + b - d >= BS * NS):
                return None
            return (s, b - d) if b >= d else (s - 1, b - d + BS)

        def ends(s, b):
            return isinstance(s, int) and s == 0 and b == 0, isinstance(s, int) and s == NS

        with nc.Block() as block:
            @block.sync
            def _(sp):
                with sp.Fori(0, NS) as s:
                    if general:
                        sp.wait_ge(PE.sem, PE.before(s))
                        sp.dma_start(attn[:], t["attn"][bass.ds(s * TT, TT), :].rearrange("(g p) d -> p g d", p=GN)
                                     ).then_inc(attn_ready, 16)
                    sp.dma_start(xt[:], a["x"][bass.ds(s * TT, TT), :].rearrange("(g p) d -> p g d", p=GN)).then_inc(x_loaded, 16)
                    sp.wait_ge(DV.sem, DV.at(s, f"l3_{NX - 1}_add"))
                    sp.dma_start(out[bass.ds(s * TT, TT), :].rearrange("(g p) d -> p g d", p=GN), xt[:]).then_inc(stored, 16)
                    sp.wait_ge(stored, 16 * (s + 1))
                    sp.sem_inc(ticks)

            @block.gpsimd
            def _(p):
                def gather(s, b, half):
                    h = b // (BS // 2)
                    if half == 0:
                        if b % (BS // 2) == 0:
                            p.wait_ge(staged, 2 * s + h + 1)
                        p.wait_ge(sv_ready, BS * s + b + 1)
                        p.sem_inc(ticks)
                    for k in range(TPB // 2 * half, TPB // 2 * (half + 1)):
                        col = (b - h * BS // 2) * TPB + k
                        p.indirect_dma_start(
                            out=kv[b % RK][:, k, :], out_offset=None, in_=t["kv"],
                            in_offset=bass.IndirectOffsetOnAxis(ap=stage[h][:, col:col + 1], axis=0)
                        ).then_inc(gathered[b % RK], 16)

                def edges_step(s, b, half):
                    first, last = ends(s, b)
                    if first and half == 0:
                        for n in range(2 * LEAD):
                            gather(s, n // 2, n % 2)
                    if not last:
                        gather(s if b + LEAD < BS else s + 1, (b + LEAD) % BS, half)

                def product(s, q):
                    if not POOL_OF[q]:
                        return
                    p.wait_ge(AC.sem, AC.at(s, q + "_hi" if q != "o" else "gn_hi"))
                    if q == "o":
                        low, x, high = gnT[:, 1], wide[:, 2:4, :], gnT[:, 0]
                    else:
                        e = int(q[3:]) % 2
                        low, x, high = parts[:, e, 1], wide[:, 2 * e:2 * e + 2, :], parts[:, e, 0]
                    p.tensor_tensor(low, x, high, ALU.subtract).then_inc(PO.sem, 1)

                p.sem_inc(PO.sem, 1)
                stream(p, edges_step, product, 1)

            @block.scalar
            def _(v):
                def put_stage(s, h):
                    n = BS // 2 * TPB
                    v.activation(stage[h][:], t["src"][:, bass.ds((2 * s + h) * n, n)], ACT.Copy).then_inc(staged, 1)

                def transposed(s, b):
                    v.wait_ge(t_ready, BS * s + b + 1)
                    v.wait_ge(q_ready, BS * s + b + 1)
                    v.activation(hotT[b % 2][:], bankT, ACT.Copy).then_inc(ht_ready, 1)

                def copy_q(s, b):
                    v.wait_ge(q_ready, BS * s + b + 1 + CQ)
                    v.wait_ge(raw_ready, BS * s + b + CR)
                    v.activation(prod[:], t["psum"][:, 1:3, :].rearrange("p b (k d) -> p (b k) d", d=D),
                                 ACT.Copy).then_inc(q_copied, 1)

                def high(s, b):
                    n = BS * s + b
                    v.wait_ge(weighted, n + 1)
                    v.wait_ge(summed, n - 1 + CW)
                    v.activation(sv[b % 2][:, 0, :, D:], ex[b % 2][:], ACT.Copy, scale=WS)
                    v.activation(sv[b % 2][:, 0, :, 0:D], kv[b % RK][:, :, D:], ACT.Copy, scale=WS).then_inc(sv_high, 1)

                def weights(s, b):
                    n = BS * s + b
                    v.wait_ge(clip_ready, n + 1)
                    v.wait_ge(sv_ready, n - 1 + CV)
                    v.activation(ex[b % 2][:], clip[:], ACT.Exp, scale=1.0 / SQRT_DH).then_inc(exp_ready, 1)

                def edges_step(s, b, half):
                    first, last = ends(s, b)
                    if half == 0:
                        if first:
                            transposed(s, 0)
                        if not last:
                            copy_q(s, b)
                        if ago(s, b, 1):
                            weights(*ago(s, b, 1))
                        if ago(s, b, 2):
                            high(*ago(s, b, 2))
                    elif not last:
                        transposed(s, b + 1)
                        if b in (BS // 2 - 1, BS - 1):
                            h = b // (BS // 2)
                            v.wait_ge(gathered[b % RK], 16 * TPB * ((BS // RK) * s + b // RK + 1))
                            put_stage(s + 1, h)

                def product(s, p):
                    bk = pair[PAIR[p]]
                    if p in ("attnT", "rowsT"):
                        v.wait_ge(PE.sem, PE.at(s, p))
                        v.activation(actT[:, 0], bk[:, :, 0:TT], ACT.Copy, scale=SA).then_inc(AC.sem, 1)
                    elif p == "o":
                        v.wait_ge(PE.sem, PE.at(s, p))
                        for m in range(KC):
                            i = v.activation(wide[:, m, :], bk[:, m, 0:TT], ACT.Identity, bias=par[:, 10, m:m + 1], scale=DESC)
                        i.then_inc(AC.sem, 1)
                        v.wait_ge(DV.sem, DV.at(s, "gn_d"))
                        v.activation(gs[:, 3, :], gs[:, 2, :], ACT.Sqrt, bias=epsc[:, 1:2]).then_inc(AC.sem, 1)
                        v.wait_ge(DV.sem, DV.at(s, "gn_out"))
                        v.activation(gnT[:, 0], wide[:, 2:4, :], ACT.Copy).then_inc(AC.sem, 1)
                    elif p[:2] == "up":
                        h = int(p[3])
                        v.wait_ge(PE.sem, PE.at(s, p))
                        if h == 1:
                            v.wait_ge(PO.sem, PO.at(s, "gn_lo"))
                        for m in range(KC):
                            i = v.activation(wide[:, 2 * h + m, :], bk[:, m, 0:TT], ACT.Relu, scale=DESC * SA,
                                             bias=upb[:, 2 * h + m:2 * h + m + 1])
                        i.then_inc(AC.sem, 1)
                        v.wait_ge(AC.sem, AC.at(s, p))
                        v.activation(parts[:, h, 0], wide[:, 2 * h:2 * h + 2, :], ACT.Copy).then_inc(AC.sem, 1)
                    elif p == "down":
                        v.wait_ge(DV.sem, DV.at(s, "ln_mv"))
                        v.activation(lsd[:, 0, :], lmv[:, :, 1], ACT.Sqrt, bias=epsc[0:GN, 0:1]).then_inc(AC.sem, 1)
                    elif p == "route":
                        v.wait_ge(DV.sem, DV.at(s, "lsub"))
                        v.activation(lg[:, 2], lg[:, 1], ACT.Exp).then_inc(AC.sem, 1)
                    elif p[:2] in ("l1", "l2"):
                        e, l = int(p[3:]), int(p[1]) - 1
                        v.wait_ge(PE.sem, PE.at(s, p))
                        for m in range(KC):
                            k = e * KC + m
                            i = v.activation(wide[:, 2 * (e % 2) + m, :], bk[:, m, 0:TT], ACT.Relu,
                                             scale=bsc[:, l, k:k + 1], bias=bbi[:, l, k:k + 1])
                        i.then_inc(AC.sem, 1)
                        v.wait_ge(AC.sem, AC.at(s, p))
                        v.activation(parts[:, e % 2, 0], wide[:, 2 * (e % 2):2 * (e % 2) + 2, :], ACT.Copy).then_inc(AC.sem, 1)

                v.sem_inc(AC.sem, 1)
                v.sem_inc(exp_ready, CE)
                if not general:
                    for h in range(2):
                        put_stage(0, h)
                stream(v, edges_step, product, 1)

            @block.vector
            def _(v):
                def make_hot(s, b):
                    v.wait_ge(summed, BS * s + b + 1)
                    v.tensor_tensor(hot[b % RK][:], t["iota"][:, 0:GN].unsqueeze(1).broadcast_to([128, TPB, GN]),
                                    t["loc"][:, bass.ds((BS * s + b) * TPB, TPB)].unsqueeze(2).broadcast_to([128, TPB, GN]),
                                    ALU.is_equal).then_inc(hot_ready, 1)

                def weigh(s, b):
                    v.wait_ge(exp_ready, BS * s + b + 1 + CE)
                    x = kv[b % RK][:, :, D:].rearrange("p k (h d) -> p k h d", h=H)
                    v.tensor_tensor(x, x, ex[b % 2][:].unsqueeze(3).broadcast_to([128, TPB, H, DH]), ALU.mult
                                    ).then_inc(weighted, 1)

                def low(s, b):
                    v.wait_ge(sv_high, BS * s + b + 1)
                    x = sv[b % 2]
                    v.scalar_tensor_tensor(x[:, 1, :, D:], ex[b % 2][:], WS, x[:, 0, :, D:], ALU.mult, ALU.subtract)
                    v.scalar_tensor_tensor(x[:, 1, :, 0:D], kv[b % RK][:, :, D:], WS, x[:, 0, :, 0:D],
                                           ALU.mult, ALU.subtract).then_inc(sv_ready, 1)

                def graph_out(g_abs, g):
                    v.wait_ge(summed, (g_abs + 1) * BPG + CW)
                    v.tensor_scalar(zinv[:, 0, :], pW[0:GN, D:D + H], 1e-6 * WS, None, ALU.add).then_inc(z_ready, 1)
                    v.wait_ge(z_ready, 2 * g_abs + 1)
                    v.reciprocal(zinv[:, 1, :], zinv[:, 0, :]).then_inc(z_ready, 1)
                    v.wait_ge(z_ready, 2 * g_abs + 2)
                    v.tensor_tensor(attn[:, g, :].rearrange("p (h d) -> p h d", h=H),
                                    pW[0:GN, 0:D].rearrange("p (h d) -> p h d", h=H),
                                    zinv[:, 1, :].unsqueeze(2).broadcast_to([GN, H, DH]), ALU.mult).then_inc(attn_ready, 1)

                def edges_step(s, b, half):
                    first, last = ends(s, b)
                    n = BS * s + b
                    if half == 0:
                        if first:
                            make_hot(s, 0)
                            make_hot(s, 1)
                        if not last:
                            v.wait_ge(gathered[b % RK], 16 * TPB * ((BS // RK) * s + b // RK + 1))
                            v.wait_ge(q_copied, n + 1)
                            v.tensor_tensor(prod[:], prod[:], kv[b % RK][:, :, 0:D], ALU.mult).then_inc(prod_ready, 1)
                    else:
                        if not last:
                            v.wait_ge(prod_ready, n + 1)
                            v.reduce_sum(raw[:].rearrange("p k h -> p (k h)"),
                                         prod[:].rearrange("p k (h d) -> p (k h) d", h=H), X).then_inc(raw_ready, 1)
                            v.wait_ge(raw_ready, n + 1 + CR)
                            v.wait_ge(exp_ready, n + CE)
                            v.tensor_scalar(clip[:], raw[:], -10.0 * SQRT_DH, 10.0 * SQRT_DH, ALU.max, ALU.min).then_inc(clip_ready, 1)
                        if ago(s, b, 1):
                            weigh(*ago(s, b, 1))
                        if ago(s, b, 2):
                            low(*ago(s, b, 2))
                        if not last:
                            make_hot(s, b + 2)
                        if b % BPG == 2 and (b > 2 or not isinstance(s, int) or s > 0):
                            g = TG * s + b // BPG - 1
                            if b == BPG + 2 and not isinstance(s, int):
                                v.wait_ge(PE.sem, PE.at(s - 1, "attnT"))
                            graph_out(g, (b // BPG - 1) % TG)

                def product(s, p):
                    bk = pair[PAIR[p]]
                    wait = lambda e, n: v.wait_ge(e.sem, e.at(s, n))
                    inc = lambda i: i.then_inc(DV.sem, 1)
                    if p in ("attnT", "rowsT"):
                        wait(AC, p + "_hi")
                        inc(v.scalar_tensor_tensor(actT[:, 1], bk[:, :, 0:TT], SA, actT[:, 0], ALU.mult, ALU.subtract))
                    elif p == "o":
                        wait(AC, "o_out")
                        for m in range(KC):
                            for g in range(TG):
                                i = v.bn_stats(st[:, TG * m + g, :], wide[:, m, g * GN:(g + 1) * GN])
                        inc(i)
                        wait(DV, "gn_st")
                        v.sem_inc(ticks)
                        for k in range(2 * TG):
                            i = v.bn_aggr(mv[:, k, :], st[:, k, :])
                        inc(i)
                        wait(DV, "gn_mv")
                        ms, gw, gb = (gnp[:, k].rearrange("p m g -> p (m g)") for k in range(3))
                        inc(v.tensor_tensor(gs[:, 0, :], mv[:, :, 0], ms, ALU.mult))
                        wait(DV, "gn_a")
                        inc(v.tensor_tensor(gs[:, 1, :], mv[:, :, 0], gs[:, 0, :], ALU.subtract))
                        wait(DV, "gn_b")
                        inc(v.tensor_tensor(gs[:, 4, :], gs[:, 1, :], gs[:, 1, :], ALU.mult))
                        wait(DV, "gn_c")
                        inc(v.tensor_tensor(gs[:, 2, :], gs[:, 4, :], mv[:, :, 1], ALU.add))
                        wait(AC, "gn_std")
                        inc(v.reciprocal(gs[:, 5, :], gs[:, 3, :]))
                        wait(DV, "gn_e")
                        inc(v.scalar_tensor_tensor(gs[:, 6, :], gs[:, 5, :], SA, gw, ALU.mult, ALU.mult))
                        wait(DV, "gn_f")
                        inc(v.tensor_tensor(gs[:, 7, :], gs[:, 0, :], gs[:, 6, :], ALU.mult))
                        wait(DV, "gn_g")
                        inc(v.scalar_tensor_tensor(gs[:, 5, :], gb, SA, gs[:, 7, :], ALU.mult, ALU.subtract))
                        wait(DV, "gn_h")
                        for m in range(KC):
                            for g in range(TG):
                                k = TG * m + g
                                i = v.tensor_scalar(wide[:, 2 + m, g * GN:(g + 1) * GN], wide[:, m, g * GN:(g + 1) * GN],
                                                    gs[:, 6, k:k + 1], gs[:, 5, k:k + 1], ALU.mult, ALU.add)
                        inc(i)
                    elif p == "down":
                        v.wait_ge(x_loaded, 16 * (s + 1))
                        inc(v.tensor_tensor(xt[:], xt[:], rb[:, 0:D].unsqueeze(1).broadcast_to([GN, TG, D]), ALU.add))
                        wait(PE, "down")
                        wait(DV, "x_bias")
                        inc(v.scalar_tensor_tensor(xt[:].rearrange("p (b g) d -> p b (g d)", b=2), bk[0:GN], DESC,
                                                   xt[:].rearrange("p (b g) d -> p b (g d)", b=2), ALU.mult, ALU.add))
                        wait(DV, "x1")
                        for g in range(TG):
                            i = v.bn_stats(lst[:, g, :], xt[:, g, :])
                        inc(i)
                        wait(DV, "ln_st")
                        v.sem_inc(ticks)
                        for g in range(TG):
                            i = v.bn_aggr(lmv[:, g, :], lst[:, g, :])
                        inc(i)
                        wait(AC, "ln_std")
                        inc(v.reciprocal(lsd[:, 1, :], lsd[:, 0, :]))
                        wait(DV, "ln_rstd")
                        for g in range(TG):
                            i = v.tensor_scalar(rows[:, g, :], xt[:, g, :], lmv[:, g, 0:1], lsd[:, 1, g:g + 1],
                                                ALU.subtract, ALU.mult)
                        inc(i)
                    elif p == "route":
                        wait(PE, "route")
                        inc(v.scalar_tensor_tensor(lg[:, 0], bk[0:GN, 0, 0:TG * NX].rearrange("p (g e) -> p g e", g=TG), DESC,
                                                   rb[:, D:].unsqueeze(1).broadcast_to([GN, TG, NX]), ALU.mult, ALU.add))
                        wait(DV, "logit")
                        inc(v.reduce_max(lred[:, 0, :], lg[:, 0], X))
                        wait(DV, "lmax")
                        inc(v.tensor_tensor(lg[:, 1], lg[:, 0], lred[:, 0, :].unsqueeze(2).broadcast_to([GN, TG, NX]), ALU.subtract))
                        wait(AC, "mix_exp")
                        inc(v.reduce_sum(lred[:, 1, :], lg[:, 2], X))
                        wait(DV, "lsum")
                        inc(v.reciprocal(lred[:, 2, :], lred[:, 1, :]))
                        wait(DV, "lrec")
                        inc(v.tensor_tensor(lg[:, 3], lg[:, 2], lred[:, 2, :].unsqueeze(2).broadcast_to([GN, TG, NX]), ALU.mult))
                        wait(DV, "mix")
                        inc(v.tensor_scalar(mixd[:], lg[:, 3], DESC, None, ALU.mult))
                    elif p[:2] == "l3":
                        e = int(p[3:])
                        wait(PE, p)
                        wait(DV, "mix_d" if e == 0 else f"l3_{e - 1}_add")
                        for g in range(TG):
                            i = v.scalar_tensor_tensor(xt[:, g, :], bk[0:GN, g // 2, (g % 2) * D:(g % 2 + 1) * D],
                                                       mixd[:, g, e:e + 1], xt[:, g, :], ALU.mult, ALU.add)
                        inc(i)

                v.sem_inc(sv_ready, CV)
                v.sem_inc(raw_ready, CR)
                v.sem_inc(DV.sem, 1)
                stream(v, edges_step, product, 1)

            @block.tensor
            def _(e):
                def turn(s, b):
                    e.wait_ge(hot_ready, BS * s + b + 1)
                    if not (isinstance(s, int) and s == 0 and b == 0):
                        e.wait_ge(ht_ready, BS * s + b)
                    for k in range(TPB):
                        m = e.matmul(bankT[:, k, :], hot[b % RK][:, k, :], t["ident16"][:], start=True, stop=True)
                    m.then_inc(t_ready, 1)

                def look_up(s, b):
                    n = BS * s + b
                    e.wait_ge(ht_ready, n + 1)
                    if not (isinstance(s, int) and s == 0 and b == 0):
                        e.wait_ge(q_copied, n)
                    for k in range(TPB):
                        for part in range(2):
                            m = e.matmul(pQ[k // 2][:, (k % 2) * D:(k % 2 + 1) * D], hotT[b % 2][:, k, :],
                                         t["q"][:, bass.ds(s * TG + b // BPG, 1), part, :].rearrange("p o d -> p (o d)"),
                                         start=(part == 0), stop=(part == 1))
                    m.then_inc(q_ready, 1)

                def add_up(s, b):
                    n = BS * s + b
                    e.wait_ge(sv_ready, n + 1 + CV)
                    if b % BPG == 0 and not (isinstance(s, int) and s == 0 and b == 0):
                        e.wait_ge(attn_ready, TG * s + b // BPG)
                    for k in range(TPB):
                        for part in range(2):
                            m = e.matmul(pW[0:GN, 0:D + H], hot[b % RK][:, k, :], sv[b % 2][:, part, k, :],
                                         start=(b % BPG == 0 and k == 0 and part == 0),
                                         stop=(b % BPG == BPG - 1 and k == TPB - 1 and part == 1))
                    m.then_inc(summed, 1)

                def edges_step(s, b, half):
                    first, last = ends(s, b)
                    if half == 0:
                        if first:
                            turn(s, 0)
                        if b == 0 and not last:
                            look_up(s, 0)
                        if ago(s, b, 3):
                            add_up(*ago(s, b, 3))
                        if not last:
                            turn(s, b + 1)
                    elif b + 1 < BS and not last:
                        look_up(s, b + 1)

                def parts3(dst, left, right, start, stop):
                    for n, (pl, pr) in enumerate(((0, 0), (0, 1), (1, 0))):
                        m = e.matmul(dst, left(pl), right(pr), start=(start and n == 0), stop=(stop and n == 2))
                    return m

                def product(s, p):
                    q = PAIR[p]
                    bk = pair[q]
                    before = [x for x in PRODUCTS[:PRODUCTS.index(p)] if PAIR[x] == q]
                    if before:
                        eng, name = TAKEN[before[-1]]
                        e.wait_ge(eng.sem, eng.at(s, name))
                    else:
                        e.wait_ge(DV.sem, DV.before(s))
                    wait = lambda eng, n: e.wait_ge(eng.sem, eng.at(s, n))
                    if p == "attnT" or p == "rowsT":
                        src = attn if p == "attnT" else rows
                        if p == "attnT":
                            e.wait_ge(attn_ready, (16 if general else TG) * (s + 1))
                        else:
                            wait(DV, "ln_out")
                        for kc in range(KC):
                            for g in range(TG):
                                m = e.transpose(bk[:, kc, g * GN:(g + 1) * GN], src[:, g, kc * 128:(kc + 1) * 128],
                                                t["ident"][0:GN, 0:GN])
                    elif p in ("o", "up_0", "up_1") or p[:2] in ("l1", "l2"):
                        if p == "o":
                            wait(DV, "attnT_lo")
                            x, m0 = lambda k, pa: actT[:, pa, k, :], 0
                            w = lambda k, pw, m: wo[:, k, pw, m * 128:(m + 1) * 128]
                        elif p[:2] == "up":
                            wait(PO, "gn_lo")
                            x, m0 = lambda k, pa: gnT[:, pa, k, :], 2 * int(p[3])
                            w = lambda k, pw, m: w1[:, k, pw, m * 128:(m + 1) * 128]
                        else:
                            ex, l, m0 = int(p[3:]), int(p[1]) - 1, 0
                            w = lambda k, pw, m: we[:, ex, l, k, pw, m * 128:(m + 1) * 128]
                            if l == 0:
                                wait(DV, "rowsT_lo")
                                x = lambda k, pa: actT[:, pa, k, :]
                            else:
                                wait(PO, f"l1_{ex}_lo")
                                x = lambda k, pa: parts[:, ex % 2, pa, k, :]
                        for mm in range(KC):
                            for k in range(KC):
                                m = parts3(bk[:, mm, 0:TT], lambda pw: w(k, pw, m0 + mm), lambda pa: x(k, pa),
                                           k == 0, k == KC - 1)
                    elif p == "down":
                        wait(PO, "up_1_lo")
                        for g in range(TG):
                            for k in range(FF // 128):
                                m = parts3(bk[0:GN, g // 2, (g % 2) * D:(g % 2 + 1) * D],
                                           lambda pa: parts[:, k // 2, pa, k % 2, g * GN:(g + 1) * GN],
                                           lambda pw: w2[:, k, pw, :], k == 0, k == FF // 128 - 1)
                    elif p == "route":
                        wait(DV, "rowsT_lo")
                        for g in range(TG):
                            for k in range(KC):
                                m = parts3(bk[0:GN, 0, g * NX:(g + 1) * NX], lambda pa: actT[:, pa, k, g * GN:(g + 1) * GN],
                                           lambda pw: wr[:, k, pw, :], k == 0, k == KC - 1)
                    else:
                        ex = int(p[3:])
                        wait(PO, f"l2_{ex}_lo")
                        for g in range(TG):
                            for k in range(KC):
                                m = parts3(bk[0:GN, g // 2, (g % 2) * D:(g % 2 + 1) * D],
                                           lambda pa: parts[:, ex % 2, pa, k, g * GN:(g + 1) * GN],
                                           lambda pw: we[:, ex, 2, k, pw, :], k == 0, False)
                            for part in range(2):
                                m = e.matmul(bk[0:GN, g // 2, (g % 2) * D:(g % 2 + 1) * D], pick[:, ex, :], bo[:, part, :],
                                             start=False, stop=(part == 1))
                    m.then_inc(PE.sem, 1)

                e.sem_inc(summed, CW)
                e.sem_inc(q_ready, CQ)
                e.sem_inc(PE.sem, 1)
                stream(e, edges_step, product, 0)


_GNN = [f"{n}_{m}" for n in ("q", "k", "v") for m in ("bases", "comb", "bias")] + [
    "gn1_w", "gn1_b", "gn1_ms", "gn2_w", "gn2_b", "gn2_ms", "O_w", "O_b", "ffn1_w", "ffn1_b", "ffn2_w", "ffn2_b"]
_FFN = ["Wr", "br", "W1", "b1", "g1", "be1", "m1", "v1", "W2", "b2", "g2", "be2", "m2", "v2", "Wo", "bo"]


def arrays(inputs):
    import numpy as np
    edges = np.zeros((3, EP), np.int32)
    edges[DST] = FAR
    for r, n in ((DST, "dst"), (SRC, "src"), (TYP, "edge_type_9")):
        edges[r, :ED] = np.asarray(inputs[n])
    arr = {"x": np.asarray(inputs["x"]), "edges": edges}
    arr.update({n: np.asarray(inputs[f"L0_gnn_{n}"]) for n in _GNN})
    arr.update({n: np.asarray(inputs[f"L0_ffn_{n}"]) for n in _FFN})
    return arr


def kernel(**inputs):
    import concourse.bacc as bacc
    from concourse.bass_utils import run_bass_kernel_spmd

    nc = bacc.Bacc("TRN2", target_bir_lowering=False, num_devices=1)
    arr = arrays(inputs)
    a = {n: nc.dram_tensor(f"in_{n}", list(v.shape), mybir.dt.from_np(v.dtype), kind="ExternalInput").ap()
         for n, v in arr.items()}
    out = nc.dram_tensor("out", [N, D], F32, kind="ExternalOutput").ap()
    build(nc, a, out)
    r = run_bass_kernel_spmd(nc, [{f"in_{n}": v for n, v in arr.items()}], core_ids=[0])
    return r.results[0]["out"]
```
